# Optimizing a Trainium2 kernel written in Bass

```python
import numpy as np
import jax
import jax.numpy as jnp

def _softmax(x, axis=-1):
    return jax.nn.softmax(x, axis=axis)

def _gelu(x):
    return jax.nn.gelu(x, approximate=True)

def _silu(x):
    return jax.nn.silu(x)

def _sigmoid(x):
    return jax.nn.sigmoid(x)

def _layernorm(x, axis=-1, eps=1e-05):
    m = jnp.mean(x, axis=axis, keepdims=True)
    v = jnp.var(x, axis=axis, keepdims=True)
    return (x - m) / jnp.sqrt(v + eps)

def _scatter_add(tgt, idx, src, axis=0):
    return tgt.at[idx].add(src)

def _segment_sum(src, seg, n):
    return jax.ops.segment_sum(src, seg, n)
kernel_name = 'mk_flamingo_gated_d2_seqx_r4_644b22'

def setup_inputs(seed: int=0):
    np.random.seed(seed)
    _w = jnp.asarray

    def _rec_inputs():
        import jax
        import jax.numpy as jnp
        _rk = jax.random.key(seed)
        x = -0.0002928 + 1 * jax.random.normal(jax.random.fold_in(_rk, 1), (8, 256, 256), jnp.float32)
        _lenS = 256 - jax.random.randint(jax.random.fold_in(_rk, 7), (8,), 0, max(1, 256 // 4) + 1, jnp.int32)
        _lenS2 = 77 - jax.random.randint(jax.random.fold_in(_rk, 8), (8,), 0, max(1, 77 // 4) + 1, jnp.int32)
        _ctx_1024P = jax.random.normal(jax.random.fold_in(_rk, 11), (8, 16, 256), jnp.float32)
        _ctx_1024c = jax.random.dirichlet(jax.random.fold_in(_rk, 511), 0.3 * jnp.ones((16,), jnp.float32), (8, 77))
        _ctx_1024t = jnp.einsum('bsk,bkd->bsd', _ctx_1024c, _ctx_1024P)
        _ctx_1024t = _ctx_1024t * jax.lax.rsqrt(jnp.mean(jnp.square(_ctx_1024t)) + 1e-12) * 0.953939
        ctx_1024 = 4.13588e-05 + 0.999923 * (_ctx_1024t + 0.3 * jax.random.normal(jax.random.fold_in(_rk, 611), (8, 77, 256), jnp.float32))
        _g = jax.random.normal(jax.random.fold_in(_rk, 9001), (2, 2), jnp.float32)
        _g = jnp.sign(_g) * jnp.maximum(jnp.abs(_g), 1.0) + (_g == 0) * 1.0
        g_xattn = _g[0]
        g_ffn = _g[1]
        return (x, ctx_1024, g_xattn, g_ffn)
    x, ctx_1024, g_xattn, g_ffn = _rec_inputs()

    def _L0_xattn_setup():
        import jax, jax.numpy as jnp
        import numpy as np
        HIDDEN = 256
        NUM_HEADS = 16
        HEAD_DIM = HIDDEN // NUM_HEADS
        key = jax.random.key(seed)
        k1, k2, k3, k4, k5, k6 = jax.random.split(key, 6)
        B, SQ, SKV = (4, 256, 512)
        s = HIDDEN ** (-0.5)
        return {'xq': jax.random.normal(k1, (B, SQ, HIDDEN), jnp.float32), 'xkv': jax.random.normal(k2, (B, SKV, HIDDEN), jnp.float32), 'Wq': jax.random.normal(k3, (HIDDEN, HIDDEN), jnp.float32) * s, 'Wkv': jax.random.normal(k4, (2 * HIDDEN, HIDDEN), jnp.float32) * s, 'Wout': jax.random.normal(k5, (HIDDEN, HIDDEN), jnp.float32) * s, 'bout': jax.random.normal(k6, (HIDDEN,), jnp.float32) * 0.01}
    _L0_xattn_all = _L0_xattn_setup()
    _L0_xattn_in = {k: v for k, v in _L0_xattn_all.items() if k in ('Wq', 'Wkv', 'Wout', 'bout')}
    del _L0_xattn_all

    def _L0_ffn_setup():
        import jax, jax.numpy as jnp
        import numpy as np
        D_MODEL = 256
        D_FF = 704
        N_EXPERTS = 8
        key = jax.random.key(seed)
        k_in, k1, k2, k3 = jax.random.split(key, 4)
        scale = 0.02
        inputs = jax.random.normal(k_in, (4, N_EXPERTS * 512, D_MODEL), dtype=jnp.float32)
        w1 = jax.random.normal(k1, (N_EXPERTS, D_MODEL, D_FF), dtype=jnp.float32) * scale
        w3 = jax.random.normal(k3, (N_EXPERTS, D_MODEL, D_FF), dtype=jnp.float32) * scale
        w2 = jax.random.normal(k2, (N_EXPERTS, D_FF, D_MODEL), dtype=jnp.float32) * scale
        return {'inputs': inputs, 'w1': w1, 'w3': w3, 'w2': w2}
    _L0_ffn_all = _L0_ffn_setup()
    _L0_ffn_in = {k: v for k, v in _L0_ffn_all.items() if k in ('w1', 'w3', 'w2')}
    del _L0_ffn_all

    def _L1_xattn_setup():
        import jax, jax.numpy as jnp
        import numpy as np
        import math
        D_MODEL = 256
        NUM_HEADS = 16
        D_K = D_MODEL // NUM_HEADS

        def _split_heads(x):
            B, S, D = x.shape
            return x.reshape(B, S, NUM_HEADS, D_K).transpose(0, 2, 1, 3)
        key = jax.random.key(seed)
        ks = jax.random.split(key, 11)
        B, S, D = (2, 512, D_MODEL)
        scale = 1.0 / math.sqrt(D)
        inp = {'Q': jax.random.normal(ks[0], (B, S, D), jnp.float32), 'K': jax.random.normal(ks[1], (B, S, D), jnp.float32), 'V': jax.random.normal(ks[2], (B, S, D), jnp.float32), 'W_q': jax.random.normal(ks[3], (D, D), jnp.float32) * scale, 'b_q': jax.random.normal(ks[4], (D,), jnp.float32) * scale, 'W_k': jax.random.normal(ks[5], (D, D), jnp.float32) * scale, 'b_k': jax.random.normal(ks[6], (D,), jnp.float32) * scale, 'W_v': jax.random.normal(ks[7], (D, D), jnp.float32) * scale, 'b_v': jax.random.normal(ks[8], (D,), jnp.float32) * scale, 'W_o': jax.random.normal(ks[9], (D, D), jnp.float32) * scale, 'b_o': jax.random.normal(ks[10], (D,), jnp.float32) * scale}
        return inp
    _L1_xattn_all = _L1_xattn_setup()
    _L1_xattn_in = {k: v for k, v in _L1_xattn_all.items() if k in ('W_q', 'b_q', 'W_k', 'b_k', 'W_v', 'b_v', 'W_o', 'b_o')}
    del _L1_xattn_all

    def _L1_ffn_setup():
        import jax, jax.numpy as jnp
        import numpy as np
        import math
        D_MODEL = 256
        D_FF = 1024
        NUM_EXPERTS = 8
        NUM_SHARED = 1
        E_ROUTED = NUM_EXPERTS - NUM_SHARED
        TOP_K = 2
        CAP_FACTOR = 1.25
        B, S = (4, 512)
        T = B * S
        CAPACITY = math.ceil(CAP_FACTOR * T * TOP_K / E_ROUTED)
        SHARED_SCALE = 1.0

        def _layernorm(x, g, b, eps=1e-05):
            mu = jnp.mean(x, axis=-1, keepdims=True)
            var = jnp.mean((x - mu) ** 2, axis=-1, keepdims=True)
            return (x - mu) * jax.lax.rsqrt(var + eps) * g + b
        key = jax.random.key(seed)
        ks = jax.random.split(key, 10)
        s = 0.02
        return {'x': jax.random.normal(ks[0], (B, S, D_MODEL), dtype=jnp.float32), 'ln_g': jnp.ones((D_MODEL,), jnp.float32), 'ln_b': jnp.zeros((D_MODEL,), jnp.float32), 'Wr': jax.random.normal(ks[1], (D_MODEL, E_ROUTED), jnp.float32) * s, 'W1': jax.random.normal(ks[2], (E_ROUTED, D_MODEL, D_FF), jnp.float32) * s, 'W3': jax.random.normal(ks[3], (E_ROUTED, D_MODEL, D_FF), jnp.float32) * s, 'W2': jax.random.normal(ks[4], (E_ROUTED, D_FF, D_MODEL), jnp.float32) * s, 'W1s': jax.random.normal(ks[5], (D_MODEL, D_FF), jnp.float32) * s, 'W3s': jax.random.normal(ks[6], (D_MODEL, D_FF), jnp.float32) * s, 'W2s': jax.random.normal(ks[7], (D_FF, D_MODEL), jnp.float32) * s}
    _L1_ffn_all = _L1_ffn_setup()
    _L1_ffn_in = {k: v for k, v in _L1_ffn_all.items() if k in ('ln_g', 'ln_b', 'Wr', 'W1', 'W3', 'W2', 'W1s', 'W3s', 'W2s')}
    del _L1_ffn_all
    return {'x': x, 'ctx_1024': ctx_1024, 'g_xattn': g_xattn, 'g_ffn': g_ffn, 'L0_xattn_Wq': _L0_xattn_in['Wq'], 'L0_xattn_Wkv': _L0_xattn_in['Wkv'], 'L0_xattn_Wout': _L0_xattn_in['Wout'], 'L0_xattn_bout': _L0_xattn_in['bout'], 'L0_ffn_w1': _L0_ffn_in['w1'], 'L0_ffn_w3': _L0_ffn_in['w3'], 'L0_ffn_w2': _L0_ffn_in['w2'], 'L1_xattn_W_q': _L1_xattn_in['W_q'], 'L1_xattn_b_q': _L1_xattn_in['b_q'], 'L1_xattn_W_k': _L1_xattn_in['W_k'], 'L1_xattn_b_k': _L1_xattn_in['b_k'], 'L1_xattn_W_v': _L1_xattn_in['W_v'], 'L1_xattn_b_v': _L1_xattn_in['b_v'], 'L1_xattn_W_o': _L1_xattn_in['W_o'], 'L1_xattn_b_o': _L1_xattn_in['b_o'], 'L1_ffn_ln_g': _L1_ffn_in['ln_g'], 'L1_ffn_ln_b': _L1_ffn_in['ln_b'], 'L1_ffn_Wr': _L1_ffn_in['Wr'], 'L1_ffn_W1': _L1_ffn_in['W1'], 'L1_ffn_W3': _L1_ffn_in['W3'], 'L1_ffn_W2': _L1_ffn_in['W2'], 'L1_ffn_W1s': _L1_ffn_in['W1s'], 'L1_ffn_W3s': _L1_ffn_in['W3s'], 'L1_ffn_W2s': _L1_ffn_in['W2s']}

def reference(x, ctx_1024, g_xattn, g_ffn, L0_xattn_Wq, L0_xattn_Wkv, L0_xattn_Wout, L0_xattn_bout, L0_ffn_w1, L0_ffn_w3, L0_ffn_w2, L1_xattn_W_q, L1_xattn_b_q, L1_xattn_W_k, L1_xattn_b_k, L1_xattn_W_v, L1_xattn_b_v, L1_xattn_W_o, L1_xattn_b_o, L1_ffn_ln_g, L1_ffn_ln_b, L1_ffn_Wr, L1_ffn_W1, L1_ffn_W3, L1_ffn_W2, L1_ffn_W1s, L1_ffn_W3s, L1_ffn_W2s):
    import jax
    import jax.numpy as jnp

    def _L0_xattn_ref(xq, xkv, Wq, Wkv, Wout, bout):
        import jax, jax.numpy as jnp
        import numpy as np
        HIDDEN = 256
        NUM_HEADS = 16
        HEAD_DIM = HIDDEN // NUM_HEADS
        B, SQ, H = xq.shape
        SKV = xkv.shape[1]
        scale = HEAD_DIM ** (-0.5)
        q = (xq @ Wq.T).reshape(B, SQ, NUM_HEADS, HEAD_DIM)
        kv = (xkv @ Wkv.T).reshape(B, SKV, 2, NUM_HEADS, HEAD_DIM)
        k, v = (kv[:, :, 0], kv[:, :, 1])
        att = jax.nn.softmax(jnp.einsum('bxhd,byhd->bhxy', q, k) * scale, axis=-1)
        x = jnp.einsum('bhxy,byhd->bxhd', att, v).reshape(B, SQ, H)
        return x @ Wout.T + bout

    def _L0_ffn_ref(inputs, w1, w3, w2):
        import jax, jax.numpy as jnp
        import numpy as np
        D_MODEL = 256
        D_FF = 704
        N_EXPERTS = 8
        B, T, D = inputs.shape
        E = w1.shape[0]
        C = T // E
        x = inputs.reshape(B, E, C, D)
        gate = jnp.einsum('becd,edf->becf', x, w1)
        up = jnp.einsum('becd,edf->becf', x, w3)
        h = jax.nn.silu(gate) * up
        out = jnp.einsum('becf,efd->becd', h, w2)
        return out.reshape(B, T, D)

    def _L1_xattn_ref(Q, K, V, W_q, b_q, W_k, b_k, W_v, b_v, W_o, b_o):
        import jax, jax.numpy as jnp
        import numpy as np
        import math
        D_MODEL = 256
        NUM_HEADS = 16
        D_K = D_MODEL // NUM_HEADS

        def _split_heads(x):
            B, S, D = x.shape
            return x.reshape(B, S, NUM_HEADS, D_K).transpose(0, 2, 1, 3)
        q = _split_heads(Q @ W_q.T + b_q)
        k = _split_heads(K @ W_k.T + b_k)
        v = _split_heads(V @ W_v.T + b_v)
        scores = jnp.einsum('bhqd,bhkd->bhqk', q, k) / jnp.sqrt(jnp.float32(D_K))
        probs = jax.nn.softmax(scores, axis=-1)
        out = jnp.einsum('bhqk,bhkd->bhqd', probs, v)
        B, H, S, dk = out.shape
        out = out.transpose(0, 2, 1, 3).reshape(B, S, H * dk)
        return out @ W_o.T + b_o

    def _L1_ffn_ref(x, ln_g, ln_b, Wr, W1, W3, W2, W1s, W3s, W2s):
        import jax, jax.numpy as jnp
        import numpy as np
        import math
        D_MODEL = 256
        D_FF = 1024
        NUM_EXPERTS = 8
        NUM_SHARED = 1
        E_ROUTED = NUM_EXPERTS - NUM_SHARED
        TOP_K = 2
        CAP_FACTOR = 1.25
        B, S = (4, 512)
        T = B * S
        CAPACITY = math.ceil(CAP_FACTOR * T * TOP_K / E_ROUTED)
        SHARED_SCALE = 1.0

        def _layernorm(x, g, b, eps=1e-05):
            mu = jnp.mean(x, axis=-1, keepdims=True)
            var = jnp.mean((x - mu) ** 2, axis=-1, keepdims=True)
            return (x - mu) * jax.lax.rsqrt(var + eps) * g + b
        Bx, Sx, D = x.shape
        Tn = Bx * Sx
        h = _layernorm(x, ln_g, ln_b).reshape(Tn, D)
        logits = h @ Wr
        top_vals, top_idx = jax.lax.top_k(logits, TOP_K)
        gates = jax.nn.softmax(top_vals, axis=-1)
        idx = top_idx.T.reshape(-1)
        gat = gates.T.reshape(-1)
        tok = jnp.tile(jnp.arange(Tn), TOP_K)
        onehot = jax.nn.one_hot(idx, E_ROUTED, dtype=jnp.int32)
        pos = jnp.sum(jnp.cumsum(onehot, axis=0) * onehot, axis=-1) - 1
        keep = pos < CAPACITY
        pos_c = jnp.where(keep, pos, CAPACITY)
        xe = jnp.zeros((E_ROUTED, CAPACITY, D), h.dtype).at[idx, pos_c].set(h[tok], mode='drop')
        a = jnp.einsum('ecd,edf->ecf', xe, W1)
        b = jnp.einsum('ecd,edf->ecf', xe, W3)
        ye = jnp.einsum('ecf,efd->ecd', jax.nn.silu(a) * b, W2)
        out_slots = ye[jnp.clip(idx, 0, E_ROUTED - 1), jnp.clip(pos_c, 0, CAPACITY - 1)]
        out_slots = out_slots * (gat * keep.astype(gat.dtype))[:, None]
        routed = jnp.zeros((Tn, D), h.dtype).at[tok].add(out_slots)
        shared = jax.nn.silu(h @ W1s) * (h @ W3s) @ W2s
        out = routed + SHARED_SCALE * shared
        return out.reshape(Bx, Sx, D)
    x = x + jnp.tanh(g_xattn[0]) * _L0_xattn_ref(_layernorm(x, axis=-1), ctx_1024, L0_xattn_Wq, L0_xattn_Wkv, L0_xattn_Wout, L0_xattn_bout)
    x = x + jnp.tanh(g_ffn[0]) * _L0_ffn_ref(_layernorm(x, axis=-1), L0_ffn_w1, L0_ffn_w3, L0_ffn_w2)
    x = x + jnp.tanh(g_xattn[1]) * _L1_xattn_ref(_layernorm(x, axis=-1), ctx_1024, ctx_1024, L1_xattn_W_q, L1_xattn_b_q, L1_xattn_W_k, L1_xattn_b_k, L1_xattn_W_v, L1_xattn_b_v, L1_xattn_W_o, L1_xattn_b_o)
    x = x + jnp.tanh(g_ffn[1]) * _L1_ffn_ref(_layernorm(x, axis=-1), L1_ffn_ln_g, L1_ffn_ln_b, L1_ffn_Wr, L1_ffn_W1, L1_ffn_W3, L1_ffn_W2, L1_ffn_W1s, L1_ffn_W3s, L1_ffn_W2s)
    return x

_drawn_inputs = setup_inputs


def setup_inputs(seed=0):
    import zlib

    import numpy as np

    out = dict(_drawn_inputs(seed))
    spreads = {'g_ffn': (-1.0, 0.6), 'L1_ffn_ln_g': (1.0, 0.6), 'L1_ffn_ln_b': (0.0, 0.8)}
    factors = {'L0_xattn_bout': 8.0,
     'L0_ffn_w1': 3.151,
     'L0_ffn_w3': 3.123,
     'L0_ffn_w2': 3.11,
     'L1_xattn_b_q': 4.65,
     'L1_xattn_b_k': 8.0,
     'L1_ffn_Wr': 3.819,
     'L1_ffn_W1': 3.352,
     'L1_ffn_W3': 3.322,
     'L1_ffn_W2': 3.318}
    for name, (base, spread) in spreads.items():
        noise = np.random.default_rng([zlib.crc32(name.encode()), seed]).standard_normal(out[name].shape)
        drawn = base * np.exp(spread * noise) if base else spread * noise
        out[name] = jnp.asarray(drawn.astype(out[name].dtype))
    for name, factor in factors.items():
        out[name] = (out[name] * factor).astype(out[name].dtype)
    return out
```

```python
from contextlib import ExitStack

import numpy as np

import concourse.bass as bass
from concourse import mybir

ALU = mybir.AluOpType
ACT = mybir.ActivationFunctionType
F32 = mybir.dt.float32
F32R = mybir.dt.float32r
I32 = mybir.dt.int32
AX_X = mybir.AxisListType.X

P = 128
B, S, D = 8, 256, 256
KT = D // P
HALVES = S // P
T = B * HALVES
KV, H, HD = 77, 16, 16
HT = H // KT
SW = HT // 2 * KV
E0, F0 = 8, 704
C0 = S // E0
M0 = 6
E1, F1, CAP = 7, 1024, 732
FT = F1 // P
SLOTS = E1 * CAP
TT, TR = 6, CAP // 6
HC = CAP // 2
EPS = 1e-5
PIECE = 512
Q, K, V, O = range(4)


def flamingo_program(nc, x, ctx_t, attn_w, rows, cols, gates, router_w, w_first, w_second, xe, ye, out):
    with ExitStack() as scope:
        def sem(name):
            return scope.enter_context(nc.semaphore(name))

        def psum(name, shape):
            return scope.enter_context(nc.psum_tensor(name, shape, F32))

        place = [nc.sbuf_base + (-nc.sbuf_base) % 64]

        def sb(name, shape, dt=F32):
            size = int(np.prod(shape[1:])) * 4
            t = nc.alloc_sbuf_tensor_at(name, shape, dt, offset=place[0])
            place[0] += size + (-size) % 64
            return t

        xs = sb("residual", [P, T, D])
        act_hi = sb("act_hi", [P, KT, B * S], F32R)
        act_lo = sb("act_lo", [P, KT, B * S], F32R)
        raw = sb("raw", [P, 8, PIECE])
        w_hi = sb("w_hi", [P, 12, PIECE], F32R)
        w_lo = sb("w_lo", [P, 12, PIECE], F32R)
        yh = sb("yh", [P, B, HALVES * D])
        ident = sb("ident", [P, P])
        before = sb("before", [P, P])
        ones = sb("ones", [P, P])
        head_mask = sb("head_mask", [P, HT])
        neg_half = sb("neg_half", [P, HALVES])
        eps_tile = sb("eps", [P, HALVES])
        row = sb("row", [P, 5, D])
        bias_cols = sb("bias_cols", [P, 2, 2, KT])
        gate = sb("gate", [P, 4])
        tanh_gate = sb("tanh_gate", [P, 4])
        rw = sb("rw", [P, KT, 8])
        logits = sb("logits", [P, T, 8])
        phase = place[0]

        xn = sb("xn", [P, HALVES, D])
        xn_t = sb("xn_t", [P, KT, S])
        xn2 = sb("xn2", [P, HALVES, D])
        stage = sb("stage", [P, KT, S])
        y_stage = sb("y_stage", [P, KT, S])
        k_t = sb("k_t", [P, KT, B * KV])
        kb = sb("kb", [P, 2, KT, HT * KV])
        ctx_b = sb("ctx_b", [P, KT, KV])
        v_blk = sb("v_blk", [P, H * P + P])
        prob = [sb(f"prob{u}", [P, 2, HT // 2, KV]) for u in range(4)]
        prob_t = sb("prob_t", [P, H, S])
        ctx_all = prob_t[:].rearrange("p a b -> p (a b)")[:, 0:KT * B * KV].rearrange("p (k n) -> p k n", k=KT)
        q_t = sb("q_t", [P, KT, S])
        o_t = sb("o_t", [P, KT, S])
        wa = sb("wa", [P, KT, 4, D])
        mx = sb("mx", [P, 4, 2, HT // 2])
        total = sb("total", [P, 4, 2, HT // 2])
        recip = sb("recip", [P, 4, 2, HT // 2])
        waited = sb("waited", [P, 1])
        stats = sb("stats", [P, HALVES, 6])
        mv = sb("mv", [P, HALVES, 2])
        rstd = sb("rstd", [P, HALVES])
        stats2 = sb("stats2", [P, HALVES, 6])
        mv2 = sb("mv2", [P, HALVES, 2])
        rstd2 = sb("rstd2", [P, HALVES])
        stats3 = sb("stats3", [P, HALVES, 6])
        mv3 = sb("mv3", [P, HALVES, 2])
        rstd3 = sb("rstd3", [P, HALVES])
        end_attention = place[0]

        place[0] = phase
        hid_hi = sb("hid_hi", [P, FT, CAP], F32R)
        hid_lo = sb("hid_lo", [P, FT, CAP], F32R)
        xe_hi = sb("xe_hi", [P, KT, CAP], F32R)
        xe_lo = sb("xe_lo", [P, KT, CAP], F32R)
        silu = sb("silu", [P, 2, PIECE])
        prod = sb("prod", [P, PIECE])
        eq = sb("eq", [P, T, E1])
        cand = sb("cand", [P, T, E1])
        pick = sb("pick", [P, 2, T, E1])
        cum = [sb(f"cum{i}", [P, 2 * T, E1]) for i in range(2)]
        order_w = sb("order_w", [P, E1])
        base_e = sb("base_e", [P, E1])
        top = sb("top", [P, 2, T])
        best = sb("best", [P, T])
        e_dif = sb("e_dif", [P, T])
        den = sb("den", [P, T])
        gates12 = sb("gates12", [P, 2, T])
        pos = sb("pos", [P, 2 * T])
        first = sb("first", [P, 2 * T])
        keep = sb("keep", [P, 2 * T])
        slot = sb("slot", [P, 2 * T])
        slot_put = sb("slot_put", [P, 2 * T], I32)
        slot_get = sb("slot_get", [P, 2 * T], I32)
        weight = sb("weight", [P, 2 * T])
        end_ffn = place[0]
        yh_rows = yh[:].rearrange("p b n -> p (b n)")
        xe_in = yh_rows[0:TR, 0:TT * D].rearrange("p (j n) -> p j n", j=TT)
        y_out = yh_rows[0:TR, TT * D:2 * TT * D].rearrange("p (j n) -> p j n", j=TT)
        place[0] = phase
        yg = sb("yg", [P, 2 * T, D])
        assert max(end_attention, end_ffn, place[0]) <= nc.sbuf_usable_end, (end_attention, end_ffn)

        bank = [psum(f"bank{i}", [P, 512]) for i in range(2)]
        score = [psum(f"score{i}", [P, 2, 512]) for i in range(2)]
        bank_p = [psum(f"bank_p{i}", [P, 512]) for i in range(2)]
        banks = [bank[0][:], bank[1][:], score[0][:, 0, :], score[0][:, 1, :], score[1][:, 0, :], score[1][:, 1, :],
                 bank_p[0][:], bank_p[1][:]]

        x_in, small_in, zero_out = sem("x_in"), sem("small_in"), sem("zero_out")
        wa_in, ctx_in, ctx_all_in = sem("wa_in"), sem("ctx_in"), sem("ctx_all_in")
        raw_in = [sem(f"raw_in{i}") for i in range(8)]
        consts, masked, zeros, v_zero, tanh_done = sem("consts"), sem("masked"), sem("zeros"), sem("v_zero"), sem("tanh_done")
        bias_done = sem("bias_done")
        stats_done, mv_done, eps_done, rstd_done, xn_ready, xnt_psum, xnt_ready = (
            sem(n) for n in ("stats_done", "mv_done", "eps_done", "rstd_done", "xn_ready", "xnt_psum", "xnt_ready"))
        stats2_done, mv2_done, eps2_done, rstd2_done, xn2_ready, xn2t_psum, stage_ready, hi_ready, lo_ready = (
            sem(n) for n in ("stats2_done", "mv2_done", "eps2_done", "rstd2_done", "xn2_ready", "xn2t_psum",
                             "stage_ready", "hi_ready", "lo_ready"))
        y_ready, stats3_done, mv3_done, eps3_done, rstd3_done, h_step = (
            sem(n) for n in ("y_ready", "stats3_done", "mv3_done", "eps3_done", "rstd3_done", "h_step"))
        h_normed = sem("h_normed")
        logit_psum, logit_done = sem("logit_psum"), sem("logit_done")
        k_psum, kt_ready, kb_ready, q_psum, qt_ready = (sem(n) for n in ("k_psum", "kt_ready", "kb_ready", "q_psum", "qt_ready"))
        s_psum, max_done, sub_done, exp_done, sum_done, recip_done, norm_done = (
            sem(n) for n in ("s_psum", "max_done", "sub_done", "exp_done", "sum_done", "recip_done", "norm_done"))
        pt_psum, pt_ready, v_psum, v_ready, pv_psum, ot_ready, o_psum, x_new = (
            sem(n) for n in ("pt_psum", "pt_ready", "v_psum", "v_ready", "pv_psum", "ot_ready", "o_psum", "x_new"))
        y_staged, yt_psum, x_ffn, xb_done = sem("y_staged"), sem("yt_psum"), sem("x_ffn"), sem("xb_done")
        hi13, lo13, hi2, lo2 = sem("hi13"), sem("lo13"), sem("hi2"), sem("lo2")
        gu_psum, silu_done, gu_free, hid_hi_done, hid_ready, tail_zero = (
            sem(n) for n in ("gu_psum", "silu_done", "gu_free", "hid_hi_done", "hid_ready", "tail_zero"))
        y0_psum, y0_done = sem("y0_psum"), sem("y0_done")
        ys_psum, ys_done = sem("ys_psum"), sem("ys_done")
        xe_load, xet_psum, xe_hi_done, xe_ready = sem("xe_load"), sem("xet_psum"), sem("xe_hi_done"), sem("xe_ready")
        yr_psum, yr_copied, y_stored = sem("yr_psum"), sem("yr_copied"), sem("y_stored")
        route, e_done, pos_psum, slots_ready = sem("route"), sem("e_done"), sem("pos_psum"), sem("slots_ready")
        scattered, rows_kept = sem("scattered"), sem("rows_kept")
        gathered = [sem(f"gathered{i}") for i in range(4)]
        added, final, stored = sem("added"), sem("final"), sem("stored")

        PIECES0 = M0 * E0
        SHARED_CHUNKS = B * S // PIECE
        GU_SHARED = M0 * E0
        GU_ROUTED = GU_SHARED + FT * SHARED_CHUNKS
        SLOT_LOADS0 = [E0] * 6 + [2 * E0, E0]

        def mm3(o, a_hi, a_lo, b_hi, b_lo, start, stop):
            nc.tensor.matmul(o, a_hi, b_hi, start=start, stop=False)
            nc.tensor.matmul(o, a_hi, b_lo, start=False, stop=False)
            return nc.tensor.matmul(o, a_lo, b_hi, start=False, stop=stop)

        def piece13_slot_load(x1, f):
            return SLOT_LOADS0[f] + (2 * x1 if f < 4 else x1) + 1

        def piece2_slot_load(x1, j):
            return SLOT_LOADS0[j] + 2 * x1 + 2

        def settle(eng):
            eng.wait_ge(consts, 1)

        block = scope.enter_context(nc.Block())

        @block.sync
        def _(sp):
            def load_wa(layer):
                for kt in range(KT):
                    sp.dma_start(wa[:, kt], attn_w[layer, kt]).then_inc(wa_in, 16)
                for kt in range(KT):
                    sp.dma_start(ctx_all[:, kt, :], ctx_t[kt].rearrange("p b n -> p (b n)")).then_inc(ctx_all_in, 16)

            def load_ctx(b, g):
                if not isinstance(g, int) or g > 0:
                    sp.wait_ge(v_psum, g)
                sp.dma_start(ctx_b[:], ctx_t[:, :, b, :].rearrange("k p n -> p k n")).then_inc(ctx_in, 16)

            def attention_loads(layer):
                load_ctx(0, B * layer)
                with sp.Fori(1, B) as b:
                    load_ctx(b, b + B * layer)

            sp.dma_start(gate[:], gates).then_inc(small_in, 16)
            sp.dma_start(row[:], rows).then_inc(small_in, 16)
            sp.dma_start(bias_cols[:], cols).then_inc(small_in, 16)
            sp.dma_start(rw[:], router_w).then_inc(small_in, 16)
            for b in range(2):
                sp.dma_start(xs[:, b * T // 2:(b + 1) * T // 2, :], x[:, b * T // 2:(b + 1) * T // 2, :]).then_inc(x_in, 16)
            load_wa(0)
            for m in range(M0):
                sp.dma_start(raw[:, m, :], w_first[0, m]).then_inc(raw_in[m], 16)
            sp.wait_ge(zeros, 1)
            flat = xe.rearrange("s d -> (s d)").rearrange("(p n) -> p n", p=P)
            wide, at = B * HALVES * D, 0
            while at < SLOTS * D // P:
                n = min(wide, SLOTS * D // P - at)
                sp.dma_start(flat[:, at:at + n], yh_rows[:, 0:n]).then_inc(zero_out, 16)
                at += n
            attention_loads(0)

            def first_layer_loads(e, last):
                for j in range(3):
                    slot_j = 6 + j % 2
                    if j == 2:
                        sp.wait_ge(hi2, 3 * e + 1)
                        sp.wait_ge(lo2, 3 * e + 1)
                    elif not isinstance(e, int) or e > 0:
                        sp.wait_ge(hi2, 3 * e - (0 if j == 0 else 1))
                        sp.wait_ge(lo2, 3 * e - (0 if j == 0 else 1))
                    sp.dma_start(raw[:, slot_j, :], w_first[e, M0 + j]).then_inc(raw_in[slot_j], 16)
                if last:
                    return
                for m in range(M0):
                    sp.wait_ge(hi13, M0 * e + m + 1)
                    sp.wait_ge(lo13, M0 * e + m + 1)
                    sp.dma_start(raw[:, m, :], w_first[e + 1, m]).then_inc(raw_in[m], 16)

            first_layer_loads(0, False)
            with sp.Fori(1, E0 - 1) as e:
                first_layer_loads(e, False)
            first_layer_loads(E0 - 1, True)
            sp.wait_ge(x_new, B)
            load_wa(1)
            sp.wait_ge(hi13, PIECES0)
            sp.wait_ge(lo13, PIECES0)
            sp.wait_ge(hi2, 3 * E0)
            sp.wait_ge(lo2, 3 * E0)
            for f in range(FT):
                sp.dma_start(raw[:, f, :], w_second[0, f]).then_inc(raw_in[f], 16)
            attention_loads(1)

            def pieces2(x1):
                for j in range(4):
                    sp.wait_ge(hi13, PIECES0 + FT * x1 + j + 1)
                    sp.wait_ge(lo13, PIECES0 + FT * x1 + j + 1)
                    sp.dma_start(raw[:, j, :], w_second[x1, FT + j]).then_inc(raw_in[j], 16)

            def pieces13(x1):
                for f in range(FT):
                    if f < 4:
                        sp.wait_ge(hi2, 3 * E0 + 4 * (x1 - 1) + f + 1)
                        sp.wait_ge(lo2, 3 * E0 + 4 * (x1 - 1) + f + 1)
                    else:
                        sp.wait_ge(hi13, PIECES0 + FT * (x1 - 1) + f + 1)
                        sp.wait_ge(lo13, PIECES0 + FT * (x1 - 1) + f + 1)
                    sp.dma_start(raw[:, f, :], w_second[x1, f]).then_inc(raw_in[f], 16)

            def load_slots(e):
                rows_e = xe[bass.ds(e * CAP, CAP), :] if not isinstance(e, int) else xe[e * CAP:(e + 1) * CAP, :]
                sp.dma_start(xe_in, rows_e.rearrange("(j p) d -> p j d", p=TR)).then_inc(xe_load, 16)

            def store_outputs(e):
                sp.wait_ge(yr_copied, TT * e + TT)
                rows_e = ye[bass.ds(e * CAP, CAP), :] if not isinstance(e, int) else ye[e * CAP:(e + 1) * CAP, :]
                sp.dma_start(rows_e.rearrange("(j p) d -> p j d", p=TR), y_out).then_inc(y_stored, 16)

            pieces2(0)
            pieces13(1)
            sp.wait_ge(scattered, 16 * 2 * T)
            load_slots(0)

            def expert_loads(e, last):
                if not last:
                    sp.wait_ge(xet_psum, 4 * e + 4)
                    load_slots(e + 1)
                pieces2(e + 1)
                if not last:
                    pieces13(e + 2)
                store_outputs(e)

            with sp.Fori(0, E1 - 1) as e:
                expert_loads(e, False)
            expert_loads(E1 - 1, True)
            for c in range(4):
                sp.wait_ge(final, 4 * c + 4)
                sp.dma_start(out[:, 4 * c:4 * c + 4, :], xs[:, 4 * c:4 * c + 4, :]).then_inc(stored, 16)
            sp.wait_ge(stored, 64)

        @block.tensor
        def _(pe):
            def transpose4(o, src):
                for kt in range(KT):
                    for h in range(HALVES):
                        last = nc.tensor.transpose(o[:, kt * S + h * P:kt * S + (h + 1) * P],
                                                   src[:, h, kt * P:(kt + 1) * P], ident[:])
                return last

            def keys(layer):
                pe.wait_ge(wa_in, 16 * KT * (layer + 1))
                pe.wait_ge(ctx_all_in, 16 * KT * (layer + 1))
                if layer == 1:
                    pe.wait_ge(gu_free, GU_SHARED + 3)
                for dt in range(KT):
                    for hf in range(2):
                        w = B * KV // 2
                        for kt in range(KT):
                            last = nc.tensor.matmul(score[dt][:, hf, 0:w], wa[:, kt, K, dt * P:(dt + 1) * P],
                                                    ctx_all[:, kt, hf * w:(hf + 1) * w], start=kt == 0, stop=kt == KT - 1)
                last.then_inc(k_psum, 1)

            def untranspose(layer, b):
                pe.wait_ge(y_staged, b + 1)
                for h in range(HALVES):
                    for m in range(KT):
                        last = nc.tensor.transpose(bank_p[1][:, h * D + m * P:h * D + (m + 1) * P],
                                                   y_stage[:, m, h * P:(h + 1) * P], ident[:])
                last.then_inc(yt_psum, 1)

            def norm_t(g):
                pe.wait_ge(xn_ready, g + 1)
                transpose4(bank[0], xn).then_inc(xnt_psum, 1)

            def norm2_t(g):
                pe.wait_ge(xn2_ready, g + 1)
                transpose4(bank[0], xn2).then_inc(xn2t_psum, 1)

            def route_logits(g, b):
                pe.wait_ge(stage_ready, g + 1)
                for h in range(HALVES):
                    for kt in range(KT):
                        last = nc.tensor.matmul(bank[0][:, h * 8:h * 8 + 8], stage[:, kt, h * P:(h + 1) * P], rw[:, kt, :],
                                                start=kt == 0, stop=kt == KT - 1)
                last.then_inc(logit_psum, 1)

            def scores(g, b, u, first):
                dt, qt = divmod(u, 2)
                if not (first and u < 2):
                    pe.wait_ge(sub_done, 4 * g + u - 1)
                for hf in range(2):
                    last = nc.tensor.matmul(score[u % 2][:, hf, 0:SW], q_t[:, dt, qt * P:(qt + 1) * P],
                                            kb[:, b % 2, dt, hf * SW:(hf + 1) * SW], start=True, stop=True)
                last.then_inc(s_psum, 1)

            def prob_transposes(g, u):
                pe.wait_ge(norm_done, 4 * g + u + 1)
                if u > 0:
                    pe.wait_ge(pt_ready, 8 * g + 2 * u)
                for grp in range(2):
                    for j in range(4):
                        last = nc.tensor.transpose(bank_p[grp][0:KV, j * P:(j + 1) * P], prob[u][:, grp, j, :], ident[:])
                    last.then_inc(pt_psum, 1)

            def weighted_values(g):
                pe.wait_ge(pt_ready, 8 * g + 8)
                pe.wait_ge(v_ready, g + 1)
                for dt in range(KT):
                    for j in range(HT):
                        h = dt * HT + j
                        last = nc.tensor.matmul(bank[1][:, dt * S:(dt + 1) * S], v_blk[0:KV, h * P:(h + 1) * P],
                                                prob_t[0:KV, h, :], start=j == 0, stop=j == HT - 1)
                last.then_inc(pv_psum, 1)

            def project_out(g):
                pe.wait_ge(ot_ready, g + 1)
                for qt in range(HALVES):
                    for dt in range(KT):
                        last = nc.tensor.matmul(bank[1][:, qt * D:(qt + 1) * D], o_t[:, dt, qt * P:(qt + 1) * P],
                                                wa[:, dt, O, :], start=dt == 0, stop=dt == KT - 1)
                last.then_inc(o_psum, 1)

            def attention_step(layer, b, n):
                g = b + B * layer
                start = layer == 0 and n == 0
                pe.wait_ge(xnt_ready, g + 1)
                if n is None or g >= 2:
                    pe.wait_ge(x_new, g - 1)
                for dt in range(KT):
                    for kt in range(KT):
                        last = nc.tensor.matmul(bank[1][:, dt * S:(dt + 1) * S], wa[:, kt, Q, dt * P:(dt + 1) * P],
                                                xn_t[:, kt, :], start=kt == 0, stop=kt == KT - 1)
                last.then_inc(q_psum, 1)
                pe.wait_ge(qt_ready, g + 1)
                pe.wait_ge(kb_ready, g + 1)
                scores(g, b, 0, start)
                scores(g, b, 1, start)
                if n is None or n >= 2:
                    norm2_t(g - 2)
                if n != 0:
                    weighted_values(g - 1)
                pe.wait_ge(ctx_in, 16 * (g + 1))
                for kt in range(KT):
                    last = nc.tensor.matmul(bank_p[0][0:KV, 0:D], ctx_b[:, kt, :], wa[:, kt, V, :],
                                            start=kt == 0, stop=kt == KT - 1)
                last.then_inc(v_psum, 1)
                if layer == 1 and n != B - 1:
                    untranspose(layer, b + 1)
                if layer == 1 and (n is None or n >= 2):
                    route_logits(g - 2, b - 2)
                if n != 0:
                    project_out(g - 1)
                pe.wait_ge(v_ready, g + 1)
                if layer == 1 and n != B - 1:
                    pe.wait_ge(x_ffn, b + 2)
                prob_transposes(g, 0)
                scores(g, b, 2, start)
                prob_transposes(g, 1)
                scores(g, b, 3, start)
                if n != B - 1:
                    if n is None or n >= 2:
                        pe.wait_ge(stage_ready, g - 1)
                        if layer == 1:
                            pe.wait_ge(logit_done, b - 1)
                    norm_t(g + 1)
                prob_transposes(g, 2)
                prob_transposes(g, 3)

            def attention(layer):
                keys(layer)
                if layer == 1:
                    untranspose(layer, 0)
                norm_t(B * layer)
                attention_step(layer, 0, 0)
                attention_step(layer, 1, 1)
                with pe.Fori(2, B - 1) as b:
                    attention_step(layer, b, None)
                attention_step(layer, B - 1, B - 1)
                g = B * layer + B - 1
                pe.wait_ge(stage_ready, g - 1)
                if layer == 1:
                    pe.wait_ge(logit_done, B - 2)
                norm2_t(g - 1)
                weighted_values(g)
                if layer == 1:
                    route_logits(g - 1, B - 2)
                project_out(g)
                pe.wait_ge(stage_ready, g)
                if layer == 1:
                    pe.wait_ge(logit_done, B - 1)
                norm2_t(g)
                if layer == 1:
                    route_logits(g, B - 1)

            def first_layer(e):
                for m in range(M0):
                    pe.wait_ge(hi13, M0 * e + m + 1)
                    pe.wait_ge(lo13, M0 * e + m + 1)
                    pe.wait_ge(gu_free, M0 * e + m + 1)
                    for gu in range(2 if m < M0 - 1 else 1):
                        for kt in range(KT):
                            c = kt * (2 * P if m < M0 - 1 else P) + gu * P
                            rhs = [a[:, kt, :].rearrange("p (b s) -> p b s", s=S)[:, :, bass.ds(e * C0, C0)] for a in (act_hi, act_lo)]
                            last = mm3(banks[2 + m % 3][:, gu * S:(gu + 1) * S], w_hi[:, m, c:c + P], w_lo[:, m, c:c + P],
                                       rhs[0], rhs[1], kt == 0, kt == KT - 1)
                    last.then_inc(gu_psum, 1)
                pe.wait_ge(y0_done, e + 1)
                for k in range(M0):
                    pe.wait_ge(hid_ready, M0 * e + k + 1)
                    if k % 2 == 0:
                        pe.wait_ge(hi2, 3 * e + k // 2 + 1)
                        pe.wait_ge(lo2, 3 * e + k // 2 + 1)
                    for m in range(KT):
                        c = k % 2 * D + m * P
                        last = mm3(bank_p[m][:, 0:S], w_hi[:, M0 + k // 2, c:c + P], w_lo[:, M0 + k // 2, c:c + P],
                                   hid_hi[:, k, 0:S], hid_lo[:, k, 0:S], k == 0, k == M0 - 1)
                last.then_inc(y0_psum, 1)

            def gate_up(n, f, width, rhs_hi, rhs_lo):
                for gu in range(2):
                    for kt in range(KT):
                        c = kt * 2 * P + gu * P
                        last = mm3(banks[2 * (f % 2) + gu][:, 0:width], w_hi[:, f, c:c + P], w_lo[:, f, c:c + P],
                                   rhs_hi[kt], rhs_lo[kt], kt == 0, kt == KT - 1)
                last.then_inc(gu_psum, 1)

            def down(o, at, width):
                for f in range(FT):
                    j, c = FT + f // 2, f % 2 * D
                    last = mm3(o, hid_hi[:, f, at:at + width], hid_lo[:, f, at:at + width], w_hi[:, j, c:c + D], w_lo[:, j, c:c + D],
                               f == 0, f == FT - 1)
                return last

            def shared(c):
                for f in range(FT):
                    n = GU_SHARED + FT * c + f
                    pe.wait_ge(gu_free, n + 2)
                    gate_up(n, f, PIECE, *([a[:, kt, bass.ds(c * PIECE, PIECE)] for kt in range(KT)] for a in (act_hi, act_lo)))
                pe.wait_ge(hid_ready, GU_SHARED + FT * c + FT)
                for j in range(4):
                    if not (isinstance(c, int) and c == 0 and j < 2):
                        pe.wait_ge(ys_done, 4 * c + j - 1)
                    down(bank_p[j % 2][:, 0:D], j * P, P).then_inc(ys_psum, 1)

            def slots_t(e):
                pe.wait_ge(xe_load, 16 * (e + 1))
                for kt in range(KT):
                    for hf in range(2):
                        if kt == 1:
                            pe.wait_ge(xe_ready, 4 * e + hf + 1)
                        elif not isinstance(e, int) or e > 0:
                            pe.wait_ge(xe_ready, 4 * e + hf - 1)
                        for j in range(3):
                            last = nc.tensor.transpose(banks[4 + hf][:, j * TR:(j + 1) * TR],
                                                       xe_in[:, 3 * hf + j, kt * P:(kt + 1) * P], ident[0:TR, 0:TR])
                        last.then_inc(xet_psum, 1)

            def expert(e, last_one):
                pe.wait_ge(xe_ready, 4 * e + 4)
                for hf in range(2):
                    for f in range(FT):
                        n = GU_ROUTED + 2 * FT * e + FT * hf + f
                        if hf == 0:
                            pe.wait_ge(hi13, PIECES0 + FT * (e + 1) + f + 1)
                            pe.wait_ge(lo13, PIECES0 + FT * (e + 1) + f + 1)
                        pe.wait_ge(gu_free, n + 2)
                        gate_up(n, f, HC, *([a[:, kt, hf * HC:(hf + 1) * HC] for kt in range(KT)] for a in (xe_hi, xe_lo)))
                if not last_one:
                    slots_t(e + 1)
                pe.wait_ge(hi2, 3 * E0 + 4 * (e + 1) + 4)
                pe.wait_ge(lo2, 3 * E0 + 4 * (e + 1) + 4)
                for j in range(TT):
                    pe.wait_ge(hid_ready, GU_ROUTED + 2 * FT * e + FT * (j // 3) + FT)
                    if not (isinstance(e, int) and e == 0 and j < 2):
                        pe.wait_ge(yr_copied, TT * e + j - 1)
                    down(bank_p[j % 2][0:TR, 0:D], j * TR, TR).then_inc(yr_psum, 1)

            pe.wait_ge(masked, 2)
            attention(0)
            pe.wait_ge(lo_ready, B)
            pe.wait_ge(hi_ready, B)
            with pe.Fori(0, E0) as e:
                first_layer(e)
            attention(1)
            pe.wait_ge(lo_ready, 2 * B)
            pe.wait_ge(hi_ready, 2 * B)
            pe.wait_ge(hi13, PIECES0 + FT)
            pe.wait_ge(lo13, PIECES0 + FT)
            pe.wait_ge(hi2, 3 * E0 + 4)
            pe.wait_ge(lo2, 3 * E0 + 4)
            pe.wait_ge(logit_done, B)
            pe.wait_ge(x_new, 2 * B)
            shared(0)
            pe.wait_ge(route, 1)
            pick_v = pick[:].rearrange("p c t e -> p (c t e)")
            nc.tensor.matmul(banks[4][:, 0:2 * T * E1], before[:], pick_v, start=True, stop=False)
            nc.tensor.matmul(banks[4][:, 0:2 * T * E1], ones[:], cum[1][:].rearrange("p g e -> p (g e)"),
                             start=False, stop=True).then_inc(pos_psum, 1)
            with pe.Fori(1, SHARED_CHUNKS) as c:
                shared(c)
            slots_t(0)
            pe.wait_ge(ys_done, 4 * SHARED_CHUNKS)
            expert(0, False)
            with pe.Fori(1, E1 - 1) as e:
                expert(e, False)
            expert(E1 - 1, True)

        @block.scalar
        def _(act):
            def split13(slot_f, n_load, at, width=PIECE):
                act.wait_ge(raw_in[slot_f], 16 * n_load)
                nc.scalar.activation(w_hi[:, at, 0:width], raw[:, slot_f, 0:width], ACT.Copy).then_inc(hi13, 1)

            def split2(slot_j, n_load, at):
                act.wait_ge(raw_in[slot_j], 16 * n_load)
                nc.scalar.activation(w_hi[:, at, :], raw[:, slot_j, :], ACT.Copy).then_inc(hi2, 1)

            def keys(layer):
                act.wait_ge(k_psum, layer + 1)
                w = B * KV // 2
                for dt in range(KT):
                    last = nc.scalar.activation(k_t[:, dt, :].rearrange("p (h n) -> p h n", h=2), score[dt][:, :, 0:w], ACT.Identity,
                                                bias=bias_cols[:, layer, 1, dt:dt + 1])
                last.then_inc(kt_ready, 1)

            def norm_t(g):
                act.wait_ge(xnt_psum, g + 1)
                nc.scalar.activation(xn_t[:].rearrange("p k s -> p (k s)"), bank[0][:], ACT.Copy).then_inc(xnt_ready, 1)

            def norm2_t(g, b, first):
                act.wait_ge(xn2t_psum, g + 1)
                if not first:
                    act.wait_ge(lo_ready, g)
                    act.wait_ge(hi_ready, g)
                nc.scalar.activation(stage[:].rearrange("p k s -> p (k s)"), bank[0][:], ACT.Copy).then_inc(stage_ready, 1)
                act.wait_ge(stage_ready, g + 1)
                nc.scalar.activation(act_hi[:, :, bass.ds(b * S, S)], stage[:], ACT.Copy).then_inc(hi_ready, 1)

            def exps(g, u):
                act.wait_ge(sub_done, 4 * g + u + 1)
                pv = prob[u][:].rearrange("p a b n -> p (a b n)")
                nc.scalar.activation(pv, pv, ACT.Exp).then_inc(exp_done, 1)

            def probs_t(g, u):
                dt, qt = divmod(u, 2)
                for grp in range(2):
                    act.wait_ge(pt_psum, 8 * g + 2 * u + grp + 1)
                    h = dt * HT + grp * 4
                    nc.scalar.activation(prob_t[0:KV, h:h + 4, qt * P:(qt + 1) * P],
                                         bank_p[grp][0:KV, :].rearrange("p (h n) -> p h n", h=4), ACT.Copy).then_inc(pt_ready, 1)

            def out_t(g):
                act.wait_ge(pv_psum, g + 1)
                nc.scalar.activation(o_t[:].rearrange("p k s -> p (k s)"), bank[1][:], ACT.Copy).then_inc(ot_ready, 1)

            def attention_step(layer, b, n):
                g = b + B * layer
                act.wait_ge(q_psum, g + 1)
                for dt in range(KT):
                    last = nc.scalar.activation(q_t[:, dt, :], bank[1][:, dt * S:(dt + 1) * S], ACT.Identity,
                                                bias=bias_cols[:, layer, 0, dt:dt + 1])
                last.then_inc(qt_ready, 1)
                exps(g, 0)
                exps(g, 1)
                if n is None or n >= 2:
                    norm2_t(g - 2, b - 2, layer == 0 and n == 2)
                if n != 0:
                    out_t(g - 1)
                if layer == 1:
                    nc.scalar.activation(w_hi[:, b, :], raw[:, b, :], ACT.Copy).then_inc(hi13, 1)
                probs_t(g, 0)
                exps(g, 2)
                probs_t(g, 1)
                exps(g, 3)
                if n != B - 1:
                    norm_t(g + 1)
                probs_t(g, 2)
                probs_t(g, 3)

            def attention(layer):
                keys(layer)
                norm_t(B * layer)
                if layer == 1:
                    for f in range(FT):
                        act.wait_ge(raw_in[f], 16 * piece13_slot_load(0, f))
                    act.wait_ge(y0_psum, E0)
                attention_step(layer, 0, 0)
                attention_step(layer, 1, 1)
                if layer == 0:
                    attention_step(layer, 2, 2)
                with act.Fori(3 if layer == 0 else 2, B - 1) as b:
                    attention_step(layer, b, None)
                attention_step(layer, B - 1, B - 1)
                g = B * layer + B - 1
                norm2_t(g - 1, B - 2, False)
                out_t(g)
                norm2_t(g, B - 1, False)

            def silu_of(n, buf, src, rows_n, width):
                act.wait_ge(gu_psum, n + 1)
                act.wait_ge(gu_free, n + 2)
                nc.scalar.activation(silu[0:rows_n, buf, 0:width], src, ACT.Silu).then_inc(silu_done, 1)

            def first_layer(e, last_one):
                for m in range(M0):
                    src = banks[2 + m % 3]
                    silu_of(M0 * e + m, m % 2, src[:, 0:S] if m < M0 - 1 else src[0:64, 0:S], P if m < M0 - 1 else 64, S)
                    if m < 3:
                        split2(6 + m % 2, (2 * e + m // 2 if m % 2 == 0 else e) + 1, M0 + m)
                    if not last_one:
                        split13(m, e + 2, m)

            def shared(c, last_one):
                for f in range(FT):
                    silu_of(GU_SHARED + FT * c + f, f % 2, banks[2 * (f % 2)], P, PIECE)
                    if last_one:
                        split13(f, piece13_slot_load(1, f), f)

            def expert(e, last_one):
                for hf in range(2):
                    for f in range(FT):
                        silu_of(GU_ROUTED + 2 * FT * e + FT * hf + f, f % 2, banks[2 * (f % 2)][:, 0:HC], P, HC)
                        if hf == 0 and f < 4:
                            split2(f, piece2_slot_load(e + 1, f), FT + f)
                        if hf == 1 and not last_one:
                            split13(f, piece13_slot_load(e + 2, f), f)
                if not last_one:
                    slots_hi(e + 1)

            def slots_hi(e):
                for kt in range(KT):
                    for hf in range(2):
                        act.wait_ge(xet_psum, 4 * e + 2 * kt + hf + 1)
                        nc.scalar.activation(xe_hi[:, kt, hf * HC:(hf + 1) * HC], banks[4 + hf][:, 0:HC], ACT.Copy).then_inc(xe_hi_done, 1)

            act.wait_ge(small_in, 64)
            nc.scalar.activation(tanh_gate[:], gate[:], ACT.Tanh).then_inc(tanh_done, 1)
            for m in range(M0):
                split13(m, 1, m)
            attention(0)
            with act.Fori(0, E0 - 1) as e:
                first_layer(e, False)
            first_layer(E0 - 1, True)
            attention(1)
            for j in range(4):
                split2(j, piece2_slot_load(0, j), FT + j)
            shared(0, False)
            act.wait_ge(e_done, 1)
            nc.scalar.activation(e_dif[:], e_dif[:], ACT.Exp).then_inc(e_done, 1)
            with act.Fori(1, SHARED_CHUNKS - 1) as c:
                shared(c, False)
            shared(SHARED_CHUNKS - 1, True)
            slots_hi(0)
            with act.Fori(0, E1 - 1) as e:
                expert(e, False)
            expert(E1 - 1, True)

        @block.vector
        def _(dve):
            def carry(n):
                if not isinstance(n, int):
                    nc.vector.memset(waited[:], 0.0)

            def row_stats(src, st, st_sem, m, m_sem, g):
                for h in range(HALVES):
                    last = nc.vector.bn_stats(st[:, h, :], src(h))
                last.then_inc(st_sem, 1)
                dve.wait_ge(st_sem, g + 1)
                carry(g)
                for h in range(HALVES):
                    last = nc.vector.bn_aggr(m[:, h, :], st[:, h, :])
                last.then_inc(m_sem, 1)

            def xs_row(b, h):
                return xs[:, bass.ds(b * HALVES + h, 1), :].rearrange("p a d -> p (a d)")

            def norm_stats(layer, b, first):
                g = b + B * layer
                if layer == 0 and isinstance(b, int) and b == 0:
                    dve.wait_ge(x_in, 32)
                if layer == 1:
                    dve.wait_ge(x_ffn, b + 1)
                if not first:
                    dve.wait_ge(xn_ready, g)
                carry(g)
                row_stats(lambda h: xs_row(b, h), stats, stats_done, mv, mv_done, g)

            def normalise(src, dst, m, r, r_sem, done, g):
                dve.wait_ge(r_sem, g + 1)
                for h in range(HALVES):
                    last = nc.vector.tensor_scalar(dst[:, h, :], src(h), m[:, h, 0:1], r[:, h:h + 1], ALU.subtract, ALU.mult)
                last.then_inc(done, 1)

            def norm(layer, b, first):
                g = b + B * layer
                if not first:
                    dve.wait_ge(xnt_psum, g)
                normalise(lambda h: xs_row(b, h), xn, mv, rstd, rstd_done, xn_ready, g)

            def norm2(layer, b, g, first):
                if not first:
                    dve.wait_ge(xn2t_psum, g)
                if layer == 1 and not (isinstance(b, int) and b == 0):
                    dve.wait_ge(rows_kept, b)
                normalise(lambda h: xs_row(b, h), xn2, mv2, rstd2, rstd2_done, xn2_ready if layer == 0 else y_ready, g)

            def norm3(b):
                normalise(lambda h: xn2[:, h, :], xn2, mv3, rstd3, rstd3_done, h_normed, b)

            def add_first_layer(b):
                dve.wait_ge(yt_psum, b + 1)
                two = xs[:, bass.ds(b * HALVES, HALVES), :].rearrange("p a d -> p (a d)")
                nc.vector.scalar_tensor_tensor(out=two, in0=bank_p[1][:], scalar=tanh_gate[:, 2:3], in1=two,
                                               op0=ALU.mult, op1=ALU.add).then_inc(x_ffn, 1)

            def max_sub(g, u, start):
                dve.wait_ge(s_psum, 4 * g + u + 1)
                sv = score[u % 2][:, :, 0:SW].rearrange("p a (h n) -> p a h n", n=KV)
                nc.vector.tensor_reduce(mx[:, u], sv, AX_X, ALU.max).then_inc(max_done, 1)
                dve.wait_ge(max_done, 4 * g + u + 1)
                if not start:
                    dve.wait_ge(pt_psum, 8 * g - 8 + 2 * u + 2)
                nc.vector.tensor_tensor(prob[u][:], sv, mx[:, u].unsqueeze(3).to_broadcast([P, 2, HT // 2, KV]),
                                        ALU.subtract).then_inc(sub_done, 1)

            def sums(g, u):
                dve.wait_ge(exp_done, 4 * g + u + 1)
                nc.vector.tensor_reduce(total[:, u], prob[u][:], AX_X, ALU.add).then_inc(sum_done, 1)
                dve.wait_ge(sum_done, 4 * g + u + 1)
                nc.vector.reciprocal(recip[:, u], total[:, u]).then_inc(recip_done, 1)

            def values(layer, g):
                dve.wait_ge(v_psum, g + 1)
                for dt in range(KT):
                    o = v_blk[0:KV, dt * HT * P:dt * HT * P + HT * (P + HD)].rearrange("p (h x) -> p h x", x=P + HD)[:, :, 0:HD]
                    v, bias = (a.rearrange("p (h d) -> p h d", d=HD) for a in (bank_p[0][0:KV, dt * P:(dt + 1) * P],
                                                                               row[0:KV, 2, dt * P:(dt + 1) * P]))
                    last = nc.vector.tensor_tensor(o, v, bias, ALU.add) if layer == 1 else nc.vector.tensor_copy(o, v)
                last.then_inc(v_ready, 1)

            def add_attention(layer, b, g):
                dve.wait_ge(o_psum, g + 1)
                dve.wait_ge(xb_done, g + 1)
                two = xs[:, bass.ds(b * HALVES, HALVES), :].rearrange("p a d -> p (a d)")
                nc.vector.scalar_tensor_tensor(out=two, in0=bank[1][:], scalar=tanh_gate[:, layer:layer + 1], in1=two,
                                               op0=ALU.mult, op1=ALU.add).then_inc(x_new, 1)

            def norm2_stats(b, g, first):
                dve.wait_ge(x_new, g + 1)
                if not first:
                    dve.wait_ge(xn2_ready, g)
                carry(g)
                row_stats(lambda h: xs_row(b, h), stats2, stats2_done, mv2, mv2_done, g)

            def norm3_stats(b):
                dve.wait_ge(y_ready, b + 1)
                carry(b)
                row_stats(lambda h: xn2[:, h, :], stats3, stats3_done, mv3, mv3_done, b)

            def keep_logits(b):
                dve.wait_ge(logit_psum, b + 1)
                nc.vector.tensor_copy(logits[:, bass.ds(b * HALVES, HALVES), :],
                                      bank[0][:, 0:HALVES * 8].rearrange("p (h e) -> p h e", h=HALVES)).then_inc(logit_done, 1)

            def attention_step(layer, b, n):
                g = b + B * layer
                start = layer == 0 and n == 0
                max_sub(g, 0, start)
                max_sub(g, 1, start)
                sums(g, 0)
                sums(g, 1)
                values(layer, g)
                if n != B - 1:
                    if layer == 1:
                        add_first_layer(b + 1)
                    norm_stats(layer, b + 1, False)
                if layer == 1 and (n is None or n >= 2):
                    keep_logits(b - 2)
                if n != 0:
                    add_attention(layer, b - 1, g - 1)
                    norm2_stats(b - 1, g - 1, layer == 0 and n == 1)
                if n != B - 1:
                    norm(layer, b + 1, False)
                max_sub(g, 2, start)
                if n != 0:
                    norm2(layer, b - 1, g - 1, layer == 0 and n == 1)
                max_sub(g, 3, start)
                sums(g, 2)
                if layer == 1 and n != 0:
                    norm3_stats(b - 1)
                sums(g, 3)
                if layer == 1 and n != 0:
                    norm3(b - 1)

            def attention(layer):
                if layer == 1:
                    nc.vector.memset(v_blk[:], 0.0).then_inc(v_zero, 1)
                    dve.wait_ge(v_zero, 2)
                    add_first_layer(0)
                norm_stats(layer, 0, layer == 0)
                norm(layer, 0, layer == 0)
                attention_step(layer, 0, 0)
                attention_step(layer, 1, 1)
                with dve.Fori(2, B - 1) as b:
                    attention_step(layer, b, None)
                attention_step(layer, B - 1, B - 1)
                g = B * layer + B - 1
                if layer == 1:
                    keep_logits(B - 2)
                add_attention(layer, B - 1, g)
                norm2_stats(B - 1, g, False)
                norm2(layer, B - 1, g, False)
                if layer == 1:
                    norm3_stats(B - 1)
                    norm3(B - 1)
                    keep_logits(B - 1)

            def hidden(n, buf, up, rows_n, at, f, width):
                dve.wait_ge(silu_done, n + 1)
                dve.wait_ge(hid_ready, n) if not isinstance(n, int) or n > 0 else None
                nc.vector.tensor_tensor(prod[0:rows_n, 0:width], silu[0:rows_n, buf, 0:width], up, ALU.mult).then_inc(gu_free, 1)
                dve.wait_ge(gu_free, n + 4)
                nc.vector.tensor_copy(hid_hi[0:rows_n, f, at:at + width], prod[0:rows_n, 0:width]).then_inc(hid_hi_done, 1)
                dve.wait_ge(hid_hi_done, n + 1)
                nc.vector.tensor_tensor(hid_lo[0:rows_n, f, at:at + width], prod[0:rows_n, 0:width],
                                        hid_hi[0:rows_n, f, at:at + width].bitcast(F32), ALU.subtract).then_inc(hid_ready, 1)

            def first_layer(e):
                for m in range(M0):
                    src = banks[2 + m % 3]
                    up = src[:, S:2 * S] if m < M0 - 1 else src[64:P, 0:S]
                    hidden(M0 * e + m, m % 2, up, P if m < M0 - 1 else 64, 0, m, S)
                dve.wait_ge(y0_psum, e + 1)
                for m in range(KT):
                    o = yh[:, :, m * S:(m + 1) * S][:, :, bass.ds(e * C0, C0)]
                    last = nc.vector.tensor_copy(o, bank_p[m][:, 0:S].rearrange("p (b c) -> p b c", c=C0))
                last.then_inc(y0_done, 1)

            def shared(c):
                for f in range(FT):
                    hidden(GU_SHARED + FT * c + f, f % 2, banks[2 * (f % 2) + 1], P, 0, f, PIECE)
                for j in range(4):
                    dve.wait_ge(ys_psum, 4 * c + j + 1)
                    two = xs[:, bass.ds(4 * c + j, 1), :].rearrange("p a d -> p (a d)")
                    nc.vector.scalar_tensor_tensor(out=two, in0=bank_p[j % 2][:, 0:D], scalar=tanh_gate[:, 3:4], in1=two,
                                                   op0=ALU.mult, op1=ALU.add).then_inc(ys_done, 1)

            def slots_lo(e):
                for kt in range(KT):
                    for hf in range(2):
                        dve.wait_ge(xe_hi_done, 4 * e + 2 * kt + hf + 1)
                        nc.vector.tensor_tensor(xe_lo[:, kt, hf * HC:(hf + 1) * HC], banks[4 + hf][:, 0:HC],
                                                xe_hi[:, kt, hf * HC:(hf + 1) * HC].bitcast(F32), ALU.subtract).then_inc(xe_ready, 1)

            def expert(e, last_one):
                for hf in range(2):
                    for f in range(FT):
                        hidden(GU_ROUTED + 2 * FT * e + FT * hf + f, f % 2, banks[2 * (f % 2) + 1][:, 0:HC], P, hf * HC, f, HC)
                if not last_one:
                    slots_lo(e + 1)
                for j in range(TT):
                    dve.wait_ge(yr_psum, TT * e + j + 1)
                    if j == 0 and not (isinstance(e, int) and e == 0):
                        dve.wait_ge(y_stored, 16 * e)
                    nc.vector.tensor_copy(y_out[:, j, :], bank_p[j % 2][0:TR, 0:D]).then_inc(yr_copied, 1)

            def routing_choices():
                steps = [0]

                def step(ins):
                    steps[0] += 1
                    ins.then_inc(added, 1)
                    dve.wait_ge(added, steps[0])

                for e in range(E1):
                    nc.vector.memset(order_w[:, e:e + 1], float(E1 - e))
                    last = nc.vector.memset(base_e[:, e:e + 1], float(CAP * e))
                step(last)
                dve.wait_ge(logit_done, B)
                lv = logits[:, :, 0:E1]
                wide = [P, T, E1]
                w_bc = order_w[:].unsqueeze(1).to_broadcast(wide)
                for c in range(2):
                    src = lv if c == 0 else cand[:]
                    step(nc.vector.tensor_reduce(top[:, c, :], src, AX_X, ALU.max))
                    step(nc.vector.tensor_tensor(eq[:], src, top[:, c, :].unsqueeze(2).to_broadcast(wide), ALU.is_equal))
                    step(nc.vector.tensor_tensor(eq[:], eq[:], w_bc, ALU.mult))
                    step(nc.vector.tensor_reduce(best[:], eq[:], AX_X, ALU.max))
                    step(nc.vector.tensor_tensor(pick[:, c], w_bc, best[:].unsqueeze(2).to_broadcast(wide), ALU.is_equal))
                    if c == 0:
                        step(nc.vector.scalar_tensor_tensor(out=cand[:], in0=pick[:, 0], scalar=-3.0e38, in1=lv, op0=ALU.mult, op1=ALU.add))
                nc.vector.tensor_tensor(e_dif[:], top[:, 1, :], top[:, 0, :], ALU.subtract).then_inc(e_done, 1)
                flat = pick[:].rearrange("p c t e -> p (c t) e")
                step(nc.vector.memset(cum[0][:, 0, :], 0.0))
                step(nc.vector.tensor_copy(cum[0][:, 1:, :], flat[:, 0:2 * T - 1, :]))
                d, at = 1, 0
                while d < 2 * T:
                    a, o = cum[at], cum[1 - at]
                    step(nc.vector.tensor_copy(o[:, 0:d, :], a[:, 0:d, :]))
                    ins = nc.vector.tensor_tensor(o[:, d:, :], a[:, d:, :], a[:, 0:2 * T - d, :], ALU.add)
                    d, at = 2 * d, 1 - at
                    if d >= 2 * T:
                        ins.then_inc(route, 1)
                    else:
                        step(ins)
                assert at == 1
                return steps

            def routing_slots(steps):
                def step(ins):
                    steps[0] += 1
                    ins.then_inc(added, 1)
                    dve.wait_ge(added, steps[0])

                flat = pick[:].rearrange("p c t e -> p (c t) e")
                dve.wait_ge(pos_psum, 1)
                step(nc.vector.tensor_tensor(cum[0][:], banks[4][:, 0:2 * T * E1].rearrange("p (g e) -> p g e", e=E1), flat, ALU.mult))
                step(nc.vector.tensor_reduce(pos[:], cum[0][:], AX_X, ALU.add))
                step(nc.vector.tensor_tensor(cum[0][:], flat, base_e[:].unsqueeze(1).to_broadcast([P, 2 * T, E1]), ALU.mult))
                step(nc.vector.tensor_reduce(first[:], cum[0][:], AX_X, ALU.add))
                step(nc.vector.tensor_scalar(keep[:], pos[:], float(CAP), None, ALU.is_lt))
                step(nc.vector.tensor_tensor(slot[:], pos[:], first[:], ALU.add))
                step(nc.vector.scalar_tensor_tensor(out=pos[:], in0=slot[:], scalar=-float(2 * SLOTS), in1=keep[:], op0=ALU.add, op1=ALU.mult))
                step(nc.vector.tensor_scalar(slot_put[:], pos[:], float(2 * SLOTS), None, ALU.add))
                step(nc.vector.tensor_tensor(slot_get[:], slot[:], keep[:], ALU.mult))
                dve.wait_ge(e_done, 2)
                step(nc.vector.tensor_scalar(den[:], e_dif[:], 1.0, None, ALU.add))
                step(nc.vector.reciprocal(gates12[:, 0, :], den[:]))
                step(nc.vector.tensor_tensor(gates12[:, 1, :], gates12[:, 0, :], e_dif[:], ALU.mult))
                nc.vector.scalar_tensor_tensor(out=weight[:], in0=gates12[:].rearrange("p c t -> p (c t)"), scalar=tanh_gate[:, 3:4],
                                               in1=keep[:], op0=ALU.mult, op1=ALU.mult).then_inc(slots_ready, 1)

            nc.vector.memset(v_blk[:], 0.0).then_inc(v_zero, 1)
            dve.wait_ge(v_zero, 1)
            dve.wait_ge(tanh_done, 1)
            for layer in range(2):
                last = nc.vector.tensor_scalar(row[:, layer, :], row[:, layer, :], tanh_gate[:, layer:layer + 1], None, ALU.mult)
            last.then_inc(bias_done, 1)
            attention(0)
            for t in (hid_hi, hid_lo):
                last = nc.vector.memset(t[64:P, M0 - 1, 0:S].bitcast(F32), 0.0)
            last.then_inc(tail_zero, 1)
            dve.wait_ge(tail_zero, 1)
            dve.wait_ge(zero_out, 48)
            dve.sem_inc(gu_free, 3)
            dve.sem_inc(y0_done, 1)
            with dve.Fori(0, E0) as e:
                first_layer(e)
            attention(1)
            steps = routing_choices()
            shared(0)
            routing_slots(steps)
            with dve.Fori(1, SHARED_CHUNKS) as c:
                shared(c)
            slots_lo(0)
            expert(0, False)
            with dve.Fori(1, E1 - 1) as e:
                expert(e, False)
            expert(E1 - 1, True)
            dve.wait_ge(slots_ready, 1)
            dve.wait_ge(ys_done, 4 * SHARED_CHUNKS)
            for c in range(4):
                dve.wait_ge(gathered[c], 16 * 8)
                for t in range(4 * c, 4 * c + 4):
                    for k in range(2):
                        if k == 1:
                            dve.wait_ge(added, steps[0] + t + 1)
                        ins = nc.vector.scalar_tensor_tensor(out=xs[:, t, :], in0=yg[:, k * T + t, :], scalar=weight[:, k * T + t:k * T + t + 1],
                                                             in1=xs[:, t, :], op0=ALU.mult, op1=ALU.add)
                        ins.then_inc(added if k == 0 else final, 1)

        @block.gpsimd
        def _(pool):
            def rstd_of(m, r, eps_sem, r_sem, g, m_sem):
                pool.wait_ge(m_sem, g + 1)
                nc.gpsimd.tensor_tensor(r[:], m[:, :, 1], eps_tile[:], ALU.add).then_inc(eps_sem, 1)
                pool.wait_ge(eps_sem, g + 1)
                nc.gpsimd.tensor_tensor(r[:], r[:], neg_half[:], ALU.pow).then_inc(r_sem, 1)

            def add_out_bias(layer, b):
                pool.wait_ge(xn_ready, b + B * layer + 1)
                settle(pool)
                two = xs[:, bass.ds(b * HALVES, HALVES), :]
                nc.gpsimd.tensor_tensor(two, two, row[:, layer, :].unsqueeze(1).to_broadcast([P, HALVES, D]), ALU.add).then_inc(xb_done, 1)

            def gain_and_bias(b, g):
                wide = [P, HALVES, D]
                pool.wait_ge(h_normed, b + 1)
                nc.gpsimd.tensor_tensor(xn2[:], xn2[:], row[:, 3, :].unsqueeze(1).to_broadcast(wide), ALU.mult).then_inc(h_step, 1)
                pool.wait_ge(h_step, b + 1)
                nc.gpsimd.tensor_tensor(xn2[:], xn2[:], row[:, 4, :].unsqueeze(1).to_broadcast(wide), ALU.add).then_inc(xn2_ready, 1)
                pool.wait_ge(xn2_ready, g + 1)
                settle(pool)
                nc.gpsimd.tensor_copy(yh[:, bass.ds(b, 1), :].rearrange("p a n -> p (a n)"),
                                      xn2[:].rearrange("p h d -> p (h d)")).then_inc(rows_kept, 1)

            def keys_blocked(b, g):
                if not isinstance(g, int) or g >= 2:
                    pool.wait_ge(s_psum, 4 * g - 4)
                    settle(pool)
                for dt in range(KT):
                    last = nc.gpsimd.tensor_tensor(
                        kb[:, b % 2, dt, :].rearrange("p (h n) -> p h n", n=KV),
                        k_t[:, dt, bass.ds(b * KV, KV)].unsqueeze(1).to_broadcast([P, HT, KV]),
                        head_mask[:].unsqueeze(2).to_broadcast([P, HT, KV]), ALU.mult)
                last.then_inc(kb_ready, 1)

            def normalise_probs(g, u):
                pool.wait_ge(recip_done, 4 * g + u + 1)
                nc.gpsimd.tensor_tensor(prob[u][:], prob[u][:], recip[:, u].unsqueeze(3).to_broadcast([P, 2, HT // 2, KV]),
                                        ALU.mult).then_inc(norm_done, 1)

            def act_low(b, g):
                pool.wait_ge(hi_ready, g + 1)
                settle(pool)
                nc.gpsimd.tensor_tensor(act_lo[:, :, bass.ds(b * S, S)], stage[:], act_hi[:, :, bass.ds(b * S, S)].bitcast(F32),
                                        ALU.subtract).then_inc(lo_ready, 1)

            def stage_first_layer(b):
                if not (isinstance(b, int) and b == 0):
                    pool.wait_ge(yt_psum, b)
                    settle(pool)
                nc.gpsimd.tensor_copy(y_stage[:].rearrange("p k s -> p (k s)"),
                                      yh[:, bass.ds(b, 1), :].rearrange("p a n -> p (a n)")).then_inc(y_staged, 1)

            def low(slot_f, at):
                return nc.gpsimd.tensor_tensor(w_lo[:, at, :], raw[:, slot_f, :], w_hi[:, at, :].bitcast(F32), ALU.subtract)

            def attention_step(layer, b, n):
                g = b + B * layer
                if layer == 1 and n != B - 1:
                    stage_first_layer(b + 1)
                normalise_probs(g, 0)
                normalise_probs(g, 1)
                if n != B - 1:
                    rstd_of(mv, rstd, eps_done, rstd_done, g + 1, mv_done)
                    keys_blocked(b + 1, g + 1)
                if n is None or n >= 2:
                    act_low(b - 2, g - 2)
                if n != 0:
                    rstd_of(mv2, rstd2, eps2_done, rstd2_done, g - 1, mv2_done)
                if n != B - 1:
                    add_out_bias(layer, b + 1)
                normalise_probs(g, 2)
                if layer == 1 and n != 0:
                    rstd_of(mv3, rstd3, eps3_done, rstd3_done, b - 1, mv3_done)
                normalise_probs(g, 3)
                if layer == 1:
                    pool.wait_ge(hi13, PIECES0 + b + 1)
                    settle(pool)
                    nc.gpsimd.tensor_tensor(w_lo[:, bass.ds(b, 1), :].rearrange("p a n -> p (a n)"),
                                            raw[:, bass.ds(b, 1), :].rearrange("p a n -> p (a n)"),
                                            w_hi[:, bass.ds(b, 1), :].rearrange("p a n -> p (a n)").bitcast(F32),
                                            ALU.subtract).then_inc(lo13, 1)
                    if n != 0:
                        gain_and_bias(b - 1, g - 1)

            def attention(layer):
                if layer == 1:
                    pool.wait_ge(y0_done, E0 + 1)
                    stage_first_layer(0)
                rstd_of(mv, rstd, eps_done, rstd_done, B * layer, mv_done)
                add_out_bias(layer, 0)
                pool.wait_ge(kt_ready, layer + 1)
                keys_blocked(0, B * layer)
                attention_step(layer, 0, 0)
                attention_step(layer, 1, 1)
                with pool.Fori(2, B - 1) as b:
                    attention_step(layer, b, None)
                attention_step(layer, B - 1, B - 1)
                g = B * layer + B - 1
                act_low(B - 2, g - 1)
                rstd_of(mv2, rstd2, eps2_done, rstd2_done, g, mv2_done)
                if layer == 1:
                    rstd_of(mv3, rstd3, eps3_done, rstd3_done, B - 1, mv3_done)
                    gain_and_bias(B - 1, g)
                act_low(B - 1, g)

            def low13(n, slot_f, at):
                pool.wait_ge(hi13, n + 1)
                low(slot_f, at).then_inc(lo13, 1)

            def low2(n, slot_j, at):
                pool.wait_ge(hi2, n + 1)
                low(slot_j, at).then_inc(lo2, 1)

            def first_layer(e, last_one):
                for m in range(M0):
                    if m < 3:
                        low2(3 * e + m, 6 + m % 2, M0 + m)
                    if not last_one:
                        low13(M0 * (e + 1) + m, m, m)

            def expert(e, last_one):
                for f in range(4):
                    low2(3 * E0 + 4 * (e + 1) + f, f, FT + f)
                if not last_one:
                    for f in range(FT):
                        low13(PIECES0 + FT * (e + 2) + f, f, f)

            for t in (ident, before, ones):
                nc.gpsimd.memset(t[:], 1.0)
            nc.gpsimd.memset(head_mask[:], float(HD) ** -0.5)
            nc.gpsimd.memset(eps_tile[:], EPS)
            nc.gpsimd.memset(neg_half[:], -0.5).then_inc(consts, 1)
            pool.wait_ge(consts, 1)
            nc.gpsimd.affine_select(out=ident[:], in_=ident[:], pattern=[[-1, P]], compare_op=ALU.is_equal, fill=0.0,
                                    base=0, channel_multiplier=1).then_inc(masked, 1)
            nc.gpsimd.affine_select(out=before[:], in_=before[:], pattern=[[1, P]], compare_op=ALU.is_gt, fill=0.0,
                                    base=0, channel_multiplier=-1).then_inc(masked, 1)
            nc.gpsimd.affine_select(out=head_mask[:], in_=head_mask[:], pattern=[[-HD, HT]], compare_op=ALU.is_ge, fill=0.0,
                                    base=0, channel_multiplier=1).then_inc(masked, 1)
            pool.wait_ge(masked, 3)
            nc.gpsimd.affine_select(out=head_mask[:], in_=head_mask[:], pattern=[[HD, HT]], compare_op=ALU.is_ge, fill=0.0,
                                    base=HD - 1, channel_multiplier=-1).then_inc(masked, 1)
            nc.gpsimd.memset(yh[:], 0.0).then_inc(zeros, 1)
            pool.wait_ge(masked, 4)
            for m in range(M0):
                low13(m, m, m)
            pool.wait_ge(bias_done, 1)
            attention(0)
            with pool.Fori(0, E0 - 1) as e:
                first_layer(e, False)
            first_layer(E0 - 1, True)
            attention(1)
            for j in range(4):
                low2(3 * E0 + j, j, FT + j)
            pool.wait_ge(slots_ready, 1)
            pool.wait_ge(rows_kept, B)
            pool.wait_ge(zero_out, 48)
            for k in range(2 * T):
                t = k % T
                nc.gpsimd.indirect_dma_start(
                    out=xe, out_offset=bass.IndirectOffsetOnAxis(ap=slot_put[:, k:k + 1], axis=0),
                    in_=yh[:, t // HALVES, t % HALVES * D:(t % HALVES + 1) * D], in_offset=None,
                    bounds_check=SLOTS - 1, oob_is_err=False).then_inc(scattered, 16)
            for f in range(FT):
                low13(PIECES0 + FT + f, f, f)
            with pool.Fori(0, E1 - 1) as e:
                expert(e, False)
            expert(E1 - 1, True)
            pool.wait_ge(y_stored, 16 * E1)
            for c in range(4):
                for t in range(4 * c, 4 * c + 4):
                    for k in (t, T + t):
                        nc.gpsimd.indirect_dma_start(
                            out=yg[:, k, :], out_offset=None, in_=ye,
                            in_offset=bass.IndirectOffsetOnAxis(ap=slot_get[:, k:k + 1], axis=0),
                            bounds_check=SLOTS - 1, oob_is_err=False).then_inc(gathered[c], 16)


def kernel(**inputs):
    import concourse.bacc as bacc
    from concourse.bass_utils import run_bass_kernel_spmd

    a = {k: np.asarray(v) for k, v in inputs.items()}
    f32 = np.float32

    def pad(t, rows):
        return np.concatenate([t, np.zeros((rows - t.shape[0],) + t.shape[1:], f32)]) if t.shape[0] < rows else t

    def attention_weights(*w):
        return np.stack([m.T for m in w], 1).reshape(KT, P, 4, D)

    def gate_up_pieces(w1, w3, n):
        g, u = (w[:, :n * P].reshape(KT, P, n, P) for w in (w1, w3))
        return [np.stack([g[:, :, f], u[:, :, f]], 2).transpose(1, 0, 2, 3).reshape(P, PIECE) for f in range(n)]

    def down_pieces(w2, n):
        w = pad(w2, n * 2 * P).reshape(n, 2, P, D)
        return [w[j].transpose(1, 0, 2).reshape(P, PIECE) for j in range(n)]

    first = []
    for w1, w3, w2 in zip(a["L0_ffn_w1"], a["L0_ffn_w3"], a["L0_ffn_w2"]):
        tail = np.concatenate([w1[:, 5 * P:], w3[:, 5 * P:]], 1).reshape(KT, P, P).transpose(1, 0, 2).reshape(P, KT * P)
        tail = np.concatenate([tail, np.zeros_like(tail)], 1)
        first.append(np.stack(gate_up_pieces(w1, w3, 5) + [tail] + down_pieces(w2, 3)))
    second = [np.stack(gate_up_pieces(w1, w3, FT) + down_pieces(w2, FT // 2))
              for w1, w3, w2 in [(a["L1_ffn_W1s"], a["L1_ffn_W3s"], a["L1_ffn_W2s"])]
              + list(zip(a["L1_ffn_W1"], a["L1_ffn_W3"], a["L1_ffn_W2"]))]
    zero = np.zeros(D, f32)
    wkv = a["L0_xattn_Wkv"]

    def on_rows(*v):
        return np.broadcast_to(np.stack(v), (P, len(v), v[0].shape[0]))

    def columns(v):
        return v.reshape(KT, P).T

    arrays = {
        "x_d": a["x"].reshape(T, P, D).transpose(1, 0, 2),
        "ctx_d": a["ctx_1024"].reshape(B * KV, D).T.reshape(KT, P, B, KV),
        "attn_w_d": np.stack([attention_weights(a["L0_xattn_Wq"], wkv[:D], wkv[D:], a["L0_xattn_Wout"]),
                              attention_weights(a["L1_xattn_W_q"], a["L1_xattn_W_k"], a["L1_xattn_W_v"], a["L1_xattn_W_o"])]),
        "rows_d": on_rows(a["L0_xattn_bout"], a["L1_xattn_b_o"], a["L1_xattn_b_v"], a["L1_ffn_ln_g"], a["L1_ffn_ln_b"]),
        "cols_d": np.stack([np.stack([columns(zero), columns(zero)], 1),
                            np.stack([columns(a["L1_xattn_b_q"]), columns(a["L1_xattn_b_k"])], 1)], 1),
        "gates_d": np.broadcast_to(np.concatenate([a["g_xattn"], a["g_ffn"]]), (P, 4)),
        "router_d": np.concatenate([a["L1_ffn_Wr"], np.zeros((D, 1), f32)], 1).reshape(KT, P, 8).transpose(1, 0, 2),
        "w_first_d": np.stack(first),
        "w_second_d": np.stack(second),
    }
    arrays = {k: np.ascontiguousarray(v) for k, v in arrays.items()}
    nc = bacc.Bacc("TRN2", target_bir_lowering=False, num_devices=1)
    ins = [nc.dram_tensor(k, v.shape, F32, kind="ExternalInput").ap() for k, v in arrays.items()]
    xe = nc.dram_tensor("slots_in", [SLOTS, D], F32, kind="Internal").ap()
    ye = nc.dram_tensor("slots_out", [SLOTS, D], F32, kind="Internal").ap()
    out = nc.dram_tensor("out_d", [P, T, D], F32, kind="ExternalOutput").ap()
    flamingo_program(nc, *ins, xe, ye, out)
    r = run_bass_kernel_spmd(nc, [arrays], core_ids=[0])
    return np.asarray(r.results[0]["out_d"]).transpose(1, 0, 2).reshape(B, S, D)
```

```python
from contextlib import ExitStack

import numpy as np

import concourse.bass as bass
from concourse import mybir

ALU = mybir.AluOpType
ACT = mybir.ActivationFunctionType
F32 = mybir.dt.float32
F32R = mybir.dt.float32r
I32 = mybir.dt.int32
AX_X = mybir.AxisListType.X

P = 128
B, S, D = 8, 256, 256
KT = D // P
HALVES = S // P
T = B * HALVES
KV, H, HD = 77, 16, 16
HT = H // KT
SW = HT // 2 * KV
PT = -(-HT * KV // P)
PR = -(-HT * KV // PT)
E0, F0 = 8, 704
C0 = S // E0
M0 = 6
E1, F1, CAP = 7, 1024, 732
FT = F1 // P
SLOTS = E1 * CAP
TT, TR = 6, CAP // 6
HC = CAP // 2
EPS = 1e-5
PIECE = 512
Q, K, V, O = range(4)


def flamingo_program(nc, x, ctx_t, attn_w, rows, cols, gates, router_w, w_first, w_second, xe, ye, out):
    with ExitStack() as scope:
        def sem(name):
            return scope.enter_context(nc.semaphore(name))

        def psum(name, shape):
            return scope.enter_context(nc.psum_tensor(name, shape, F32))

        place = [nc.sbuf_base + (-nc.sbuf_base) % 64]

        def sb(name, shape, dt=F32):
            size = int(np.prod(shape[1:])) * 4
            t = nc.alloc_sbuf_tensor_at(name, shape, dt, offset=place[0])
            place[0] += size + (-size) % 64
            return t

        xs = sb("residual", [P, T, D])
        act_hi = sb("act_hi", [P, KT, B * S], F32R)
        act_lo = sb("act_lo", [P, KT, B * S], F32R)
        raw = sb("raw", [P, 9, PIECE])
        w_hi = sb("w_hi", [P, 12, PIECE], F32R)
        w_lo = sb("w_lo", [P, 12, PIECE], F32R)
        yh = sb("yh", [P, B, HALVES * D])
        ident = sb("ident", [P, P])
        before = sb("before", [P, P])
        ones = sb("ones", [P, P])
        head_mask = sb("head_mask", [P, HT])
        neg_half = sb("neg_half", [P, HALVES])
        eps_tile = sb("eps", [P, HALVES])
        row = sb("row", [P, 5, D])
        bias_cols = sb("bias_cols", [P, 2, 2, KT])
        gate = sb("gate", [P, 4])
        tanh_gate = sb("tanh_gate", [P, 4])
        rw = sb("rw", [P, KT, 8])
        logits = sb("logits", [P, T, 8])
        phase = place[0]

        xn = sb("xn", [P, HALVES, D])
        xn_t = sb("xn_t", [P, KT, S])
        k_t = sb("k_t", [P, KT, B * KV])
        kb = sb("kb", [P, 2, KT, HT * KV])
        v_rows = sb("v_rows", [P, 2, D])
        v_blk = sb("v_blk", [P, KT * PT, P])
        prob = [sb(f"prob{u}", [P, PT * PR]) for u in range(4)]
        prob_t = sb("prob_t", [P, KT * PT, S])
        waited = sb("waited", [P, 1])
        stats = sb("stats", [P, HALVES, 6])
        mv = sb("mv", [P, HALVES, 2])
        rstd = sb("rstd", [P, HALVES])
        mx = sb("mx", [P, 4, 2, HT // 2])
        total = sb("total", [P, 4, 2, HT // 2])
        recip = sb("recip", [P, 4, 2, HT // 2])
        first_hidden_end = phase + 3 * PIECE * 4 + (FT + M0) * CAP * 4
        assert place[0] <= first_hidden_end
        place[0] = first_hidden_end
        ctx_all = sb("ctx_all", [P, KT, B * KV])
        end_attention = place[0]

        place[0] = phase
        silu = sb("silu", [P, 2, PIECE])
        prod = sb("prod", [P, PIECE])
        hid_hi = sb("hid_hi", [P, FT, CAP], F32R)
        hid_lo = sb("hid_lo", [P, FT, CAP], F32R)
        place[0] = late = max(place[0], end_attention)
        xn2 = sb("xn2", [P, HALVES, D])
        stage = sb("stage", [P, KT, S])
        o_t = sb("o_t", [P, KT, S])
        ctx_b = sb("ctx_b", [P, KT, KV])
        stats2 = sb("stats2", [P, HALVES, 6])
        mv2 = sb("mv2", [P, HALVES, 2])
        rstd2 = sb("rstd2", [P, HALVES])
        stats3 = sb("stats3", [P, HALVES, 6])
        mv3 = sb("mv3", [P, HALVES, 2])
        rstd3 = sb("rstd3", [P, HALVES])
        q_t = sb("q_t", [P, KT, S])
        wa = sb("wa", [P, KT, 4, D])
        end_late = place[0]

        place[0] = late
        xe_hi = sb("xe_hi", [P, KT, CAP], F32R)
        xe_lo = sb("xe_lo", [P, KT, CAP], F32R)
        eq = sb("eq", [P, T, E1])
        cand = sb("cand", [P, T, E1])
        pick = sb("pick", [P, 2, T, E1])
        cum = [sb(f"cum{i}", [P, 2 * T, E1]) for i in range(2)]
        order_w = sb("order_w", [P, E1])
        base_e = sb("base_e", [P, E1])
        top = sb("top", [P, 2, T])
        best = sb("best", [P, T])
        e_dif = sb("e_dif", [P, T])
        den = sb("den", [P, T])
        gates12 = sb("gates12", [P, 2, T])
        pos = sb("pos", [P, 2 * T])
        first = sb("first", [P, 2 * T])
        keep = sb("keep", [P, 2 * T])
        slot = sb("slot", [P, 2 * T])
        slot_put = sb("slot_put", [P, 2 * T], I32)
        slot_get = sb("slot_get", [P, 2 * T], I32)
        weight = sb("weight", [P, 2 * T])
        end_ffn = place[0]
        yh_rows = yh[:].rearrange("p b n -> p (b n)")
        xe_in = yh_rows[0:TR, 0:TT * D].rearrange("p (j n) -> p j n", j=TT)
        y_out = yh_rows[0:TR, TT * D:2 * TT * D].rearrange("p (j n) -> p j n", j=TT)
        assert max(end_late, end_ffn) <= nc.sbuf_usable_end, (end_late, end_ffn, nc.sbuf_usable_end)

        def yg(k, t):
            if k == 1:
                return yh_rows[:, t * D:(t + 1) * D]
            n = B * S // 2 // D
            half = (act_hi, act_lo)[t // (KT * n)]
            return half[:, t // n % KT, t % n * D:(t % n + 1) * D].bitcast(F32)

        bank = [psum(f"bank{i}", [P, 512]) for i in range(2)]
        score = [psum(f"score{i}", [P, 2, 512]) for i in range(2)]
        bank_p = [psum(f"bank_p{i}", [P, 512]) for i in range(2)]
        banks = [bank[0][:], bank[1][:], score[0][:, 0, :], score[0][:, 1, :], score[1][:, 0, :], score[1][:, 1, :],
                 bank_p[0][:], bank_p[1][:]]

        x_first, x_rest, small_in, zero_out = sem("x_first"), sem("x_rest"), sem("small_in"), sem("zero_out")
        wk_in, wa_in, ctx_in, ctx_all_in = sem("wk_in"), sem("wa_in"), sem("ctx_in"), sem("ctx_all_in")
        v_in = [sem(f"v_in{i}") for i in range(KT)]
        raw_in = [sem(f"raw_in{i}") for i in range(9)]
        consts, masked, zeros, v_zero, tanh_done = sem("consts"), sem("masked"), sem("zeros"), sem("v_zero"), sem("tanh_done")
        bias_done = sem("bias_done")
        stats_done, mv_done, eps_done, rstd_done, xn_ready, xnt_psum, xnt_ready = (
            sem(n) for n in ("stats_done", "mv_done", "eps_done", "rstd_done", "xn_ready", "xnt_psum", "xnt_ready"))
        stats2_done, mv2_done, eps2_done, rstd2_done, xn2_ready, xn2t_psum, stage_ready, hi_ready, lo_ready = (
            sem(n) for n in ("stats2_done", "mv2_done", "eps2_done", "rstd2_done", "xn2_ready", "xn2t_psum",
                             "stage_ready", "hi_ready", "lo_ready"))
        y_ready, stats3_done, mv3_done, eps3_done, rstd3_done, h_step = (
            sem(n) for n in ("y_ready", "stats3_done", "mv3_done", "eps3_done", "rstd3_done", "h_step"))
        h_normed = sem("h_normed")
        logit_psum, logit_done = sem("logit_psum"), sem("logit_done")
        k_psum, kt_ready, kb_ready, q_psum, qt_ready = (sem(n) for n in ("k_psum", "kt_ready", "kb_ready", "q_psum", "qt_ready"))
        s_psum, max_done, sub_done, exp_done, sum_done, recip_done, norm_done = (
            sem(n) for n in ("s_psum", "max_done", "sub_done", "exp_done", "sum_done", "recip_done", "norm_done"))
        pt_psum, pt_ready, v_psum, v_ready, pv_psum, ot_ready, o_psum, x_new = (
            sem(n) for n in ("pt_psum", "pt_ready", "v_psum", "v_ready", "pv_psum", "ot_ready", "o_psum", "x_new"))
        x_ffn, xb_done = sem("x_ffn"), sem("xb_done")
        hi13, lo13, hi2, lo2, lo2_first = sem("hi13"), sem("lo13"), sem("hi2"), sem("lo2"), sem("lo2_first")
        gu_psum, silu_done, gu_free, hid_hi_done, hid_ready, tail_zero = (
            sem(n) for n in ("gu_psum", "silu_done", "gu_free", "hid_hi_done", "hid_ready", "tail_zero"))
        y0_psum, y0_done = sem("y0_psum"), sem("y0_done")
        ys_psum, ys_done = sem("ys_psum"), sem("ys_done")
        xe_load, xet_psum, xe_hi_done, xe_ready = sem("xe_load"), sem("xet_psum"), sem("xe_hi_done"), sem("xe_ready")
        yr_psum, yr_copied, y_stored = sem("yr_psum"), sem("yr_copied"), sem("y_stored")
        route, e_done, pos_psum, slots_ready = sem("route"), sem("e_done"), sem("pos_psum"), sem("slots_ready")
        scattered, rows_kept = sem("scattered"), sem("rows_kept")
        gathered = [sem(f"gathered{i}") for i in range(4)]
        added, final, stored = sem("added"), sem("final"), sem("stored")

        PIECES0 = M0 * E0
        SHARED_CHUNKS = B * S // PIECE
        EARLY = SHARED_CHUNKS // 2
        GU_SHARED = M0 * E0
        GU_ROUTED = GU_SHARED + FT * EARLY
        GU_LATE = GU_ROUTED + 2 * FT * E1
        STREAM = E1 + 2

        def place_values_pieces():
            runs = []
            for h in range(HT):
                r = 0
                while r < KV:
                    tile, p = divmod(h * KV + r, PR)
                    n = min(KV - r, PR - p)
                    runs.append((tile, p, h, r, n))
                    r += n
            return runs

        RUNS = place_values_pieces()
        assert SLOTS * D % (P * B) == 0 and SLOTS * D // P // B <= B * HALVES * D

        def mm3(o, a_hi, a_lo, b_hi, b_lo, start, stop):
            nc.tensor.matmul(o, a_hi, b_hi, start=start, stop=False)
            nc.tensor.matmul(o, a_hi, b_lo, start=False, stop=False)
            return nc.tensor.matmul(o, a_lo, b_hi, start=False, stop=stop)

        def piece13_slot_load(x1, f):
            return E0 + (2 * x1 if f < 4 else x1) + 1

        def piece2_slot_load(x1, j):
            return E0 + 2 * x1 + 2

        def settle(eng):
            eng.wait_ge(consts, 1)

        block = scope.enter_context(nc.Block())

        @block.sync
        def _(sp):
            def load_wa(layer):
                def matrix(w):
                    return sp.dma_start(wa[:, :, w, :], attn_w[layer, :, :, w, :].rearrange("k p n -> p k n"))
                matrix(K).then_inc(wk_in, 16)
                sp.dma_start(ctx_all[:], ctx_t.rearrange("k p b n -> p k (b n)")).then_inc(ctx_all_in, 16)
                for w in (Q, V, O):
                    matrix(w).then_inc(wa_in, 16)

            def place_values(b, g):
                sp.wait_ge(v_ready, g + 1)
                for dt in range(KT):
                    if not isinstance(g, int) or g > 0:
                        sp.wait_ge(pv_psum, KT * g - KT + 1 + dt)
                    for tile, p, h, r, n in RUNS:
                        at = (dt * HT + h) * HD
                        sp.dma_start(v_blk[p:p + n, dt * PT + tile, h * HD:(h + 1) * HD],
                                     v_rows[r:r + n, bass.ds(b % 2, 1), at:at + HD].rearrange("p a d -> p (a d)")).then_inc(v_in[dt], 16)

            def load_ctx(b):
                sp.dma_start(ctx_b[:], ctx_t[:, :, b, :].rearrange("k p n -> p k n")).then_inc(ctx_in, 16)

            zero_at = xe.rearrange("s d -> (s d)").rearrange("(p n) -> p n", p=P)
            zero_w = SLOTS * D // P // B

            def zero_slots(b):
                sp.dma_start(zero_at[:, bass.ds(b * zero_w, zero_w)], yh_rows[:, 0:zero_w]).then_inc(zero_out, 16)

            def first_pieces(layer, b):
                if layer == 0:
                    zero_slots(b)
                    if isinstance(b, int) and b == 0:
                        for m in range(M0 + 3):
                            sp.dma_start(raw[:, m, :], w_first[0, m]).then_inc(raw_in[m], 16)

            def attention_loads(layer):
                if layer == 1:
                    load_ctx(0)
                else:
                    sp.wait_ge(zeros, 1)
                sp.wait_ge(v_zero, layer + 1)
                sp.wait_ge(v_psum, B * layer + 1)
                load_ctx(1)
                place_values(0, B * layer)
                first_pieces(layer, 0)
                with sp.Fori(1, B - 1) as b:
                    sp.wait_ge(v_psum, b + B * layer + 1)
                    load_ctx(b + 1)
                    place_values(b, b + B * layer)
                    first_pieces(layer, b)
                place_values(B - 1, B * layer + B - 1)
                first_pieces(layer, B - 1)

            sp.dma_start(xs[:, 0:HALVES, :], x[:, 0:HALVES, :]).then_inc(x_first, 16)
            sp.dma_start(gate[:], gates).then_inc(small_in, 16)
            sp.dma_start(bias_cols[:], cols).then_inc(small_in, 16)
            load_wa(0)
            load_ctx(0)
            sp.dma_start(row[:], rows).then_inc(small_in, 16)
            sp.dma_start(rw[:], router_w).then_inc(small_in, 16)
            sp.dma_start(xs[:, HALVES:, :], x[:, HALVES:, :]).then_inc(x_rest, 16)
            attention_loads(0)

            def gate_up_load(e, m):
                sp.wait_ge(lo13, M0 * (e - 1) + m + 1)
                sp.dma_start(raw[:, m, :], w_first[e, m]).then_inc(raw_in[m], 16)

            def down_load(e, j):
                if j == 0:
                    sp.wait_ge(lo2, e)
                else:
                    sp.wait_ge(lo2_first, 2 * (e - 1) + j)
                sp.dma_start(raw[:, M0 + j, :], w_first[e, M0 + j]).then_inc(raw_in[M0 + j], 16)

            for m in range(M0):
                gate_up_load(1, m)
            with sp.Fori(0, E0 - 2) as e:
                for m in range(M0):
                    if m < 3:
                        down_load(e + 1, m)
                    gate_up_load(e + 2, m)
            for j in range(3):
                down_load(E0 - 1, j)
            for m in range(M0):
                sp.wait_ge(lo13, M0 * (E0 - 1) + m + 1)
                sp.dma_start(raw[:, m, :], w_second[0, m]).then_inc(raw_in[m], 16)
            sp.wait_ge(x_new, B)
            load_wa(1)
            sp.wait_ge(lo2, E0)
            sp.wait_ge(lo2_first, 2 * E0)
            for f in range(M0, FT):
                sp.dma_start(raw[:, f, :], w_second[0, f]).then_inc(raw_in[f], 16)
            attention_loads(1)

            def weights(x1):
                return x1 % (STREAM - 1) if isinstance(x1, int) else x1

            def pieces2(x1):
                for j in range(4):
                    sp.wait_ge(lo13, PIECES0 + FT * x1 + j + 1)
                    sp.dma_start(raw[:, j, :], w_second[weights(x1), FT + j]).then_inc(raw_in[j], 16)

            def pieces13(x1):
                for f in range(FT):
                    if f < 4:
                        sp.wait_ge(lo2, E0 + 4 * (x1 - 1) + f + 1)
                    else:
                        sp.wait_ge(lo13, PIECES0 + FT * (x1 - 1) + f + 1)
                    sp.dma_start(raw[:, f, :], w_second[weights(x1), f]).then_inc(raw_in[f], 16)

            def load_slots(e):
                rows_e = xe[bass.ds(e * CAP, CAP), :] if not isinstance(e, int) else xe[e * CAP:(e + 1) * CAP, :]
                sp.dma_start(xe_in, rows_e.rearrange("(j p) d -> p j d", p=TR)).then_inc(xe_load, 16)

            def store_outputs(e):
                sp.wait_ge(yr_copied, TT * e + TT)
                rows_e = ye[bass.ds(e * CAP, CAP), :] if not isinstance(e, int) else ye[e * CAP:(e + 1) * CAP, :]
                sp.dma_start(rows_e.rearrange("(j p) d -> p j d", p=TR), y_out).then_inc(y_stored, 16)

            pieces2(0)
            pieces13(1)
            sp.wait_ge(scattered, 16 * 2 * T)
            load_slots(0)
            pieces2(1)
            sp.wait_ge(xet_psum, 4)
            load_slots(1)

            def expert_loads(e, slots):
                pieces13(e + 2)
                pieces2(e + 2)
                if slots:
                    sp.wait_ge(xet_psum, 4 * e + 8)
                    load_slots(e + 2)
                store_outputs(e)

            with sp.Fori(0, E1 - 2) as e:
                expert_loads(e, True)
            expert_loads(E1 - 2, False)
            expert_loads(E1 - 1, False)
            for c in range(4):
                sp.wait_ge(final, 4 * c + 4)
                sp.dma_start(out[:, 4 * c:4 * c + 4, :], xs[:, 4 * c:4 * c + 4, :]).then_inc(stored, 16)
            sp.wait_ge(stored, 64)

        @block.tensor
        def _(pe):
            def transpose4(o, src):
                for kt in range(KT):
                    for h in range(HALVES):
                        last = nc.tensor.transpose(o[:, kt * S + h * P:kt * S + (h + 1) * P],
                                                   src[:, h, kt * P:(kt + 1) * P], ident[:])
                return last

            def keys(layer):
                pe.wait_ge(wk_in, 16 * (layer + 1))
                pe.wait_ge(ctx_all_in, 16 * (layer + 1))
                if layer == 1:
                    pe.wait_ge(gu_free, GU_SHARED + 3)
                for dt in range(KT):
                    for hf in range(2):
                        w = B * KV // 2
                        for kt in range(KT):
                            last = nc.tensor.matmul(score[dt][:, hf, 0:w], wa[:, kt, K, dt * P:(dt + 1) * P],
                                                    ctx_all[:, kt, hf * w:(hf + 1) * w], start=kt == 0, stop=kt == KT - 1)
                last.then_inc(k_psum, 1)

            def norm_t(g):
                pe.wait_ge(xn_ready, g + 1)
                transpose4(bank[0], xn).then_inc(xnt_psum, 1)

            def norm2_t(g):
                pe.wait_ge(xn2_ready, g + 1)
                transpose4(bank[0], xn2).then_inc(xn2t_psum, 1)

            def route_logits(g, b):
                pe.wait_ge(stage_ready, g + 1)
                for h in range(HALVES):
                    for kt in range(KT):
                        last = nc.tensor.matmul(bank[0][:, h * 8:h * 8 + 8], stage[:, kt, h * P:(h + 1) * P], rw[:, kt, :],
                                                start=kt == 0, stop=kt == KT - 1)
                last.then_inc(logit_psum, 1)

            def scores(g, b, u, first):
                dt, qt = divmod(u, 2)
                if not (first and u < 2):
                    pe.wait_ge(sub_done, 4 * g + u - 1)
                for hf in range(2):
                    last = nc.tensor.matmul(score[u % 2][:, hf, 0:SW], q_t[:, dt, qt * P:(qt + 1) * P],
                                            kb[:, b % 2, dt, hf * SW:(hf + 1) * SW], start=True, stop=True)
                last.then_inc(s_psum, 1)

            def prob_transposes(g, u):
                pe.wait_ge(norm_done, 4 * g + u + 1)
                if not (isinstance(g, int) and g == 0 and u == 0):
                    pe.wait_ge(pt_ready, 8 * g + 2 * u)
                for grp, tiles in enumerate(((0, 1, 2), (3, 4))):
                    for i, j in enumerate(tiles):
                        last = nc.tensor.transpose(bank_p[grp][0:PR, i * P:(i + 1) * P], prob[u][:, j * PR:(j + 1) * PR], ident[:])
                    last.then_inc(pt_psum, 1)

            def weighted_values(g, dt):
                pe.wait_ge(pt_ready, 8 * g + 4 * dt + 4)
                pe.wait_ge(v_in[dt], 16 * len(RUNS) * (g + 1))
                for j in range(PT):
                    last = nc.tensor.matmul(bank[1][:, dt * S:(dt + 1) * S], v_blk[0:PR, dt * PT + j, :],
                                            prob_t[0:PR, dt * PT + j, :], start=j == 0, stop=j == PT - 1)
                last.then_inc(pv_psum, 1)

            def project_out(g):
                pe.wait_ge(ot_ready, g + 1)
                for qt in range(HALVES):
                    for dt in range(KT):
                        last = nc.tensor.matmul(bank[1][:, qt * D:(qt + 1) * D], o_t[:, dt, qt * P:(qt + 1) * P],
                                                wa[:, dt, O, :], start=dt == 0, stop=dt == KT - 1)
                last.then_inc(o_psum, 1)

            def queries(g):
                pe.wait_ge(xnt_ready, g + 1)
                for dt in range(KT):
                    for kt in range(KT):
                        last = nc.tensor.matmul(bank[1][:, dt * S:(dt + 1) * S], wa[:, kt, Q, dt * P:(dt + 1) * P],
                                                xn_t[:, kt, :], start=kt == 0, stop=kt == KT - 1)
                last.then_inc(q_psum, 1)

            def values(g):
                pe.wait_ge(ctx_in, 16 * (g + 1))
                for kt in range(KT):
                    last = nc.tensor.matmul(bank[0][0:KV, 0:D], ctx_b[:, kt, :], wa[:, kt, V, :], start=kt == 0, stop=kt == KT - 1)
                last.then_inc(v_psum, 1)

            def attention_step(layer, b, n):
                g = b + B * layer
                start = layer == 0 and n == 0
                settled = n is None or n >= 2
                pe.wait_ge(qt_ready, g + 1)
                pe.wait_ge(kb_ready, g + 1)
                scores(g, b, 0, start)
                if n != 0:
                    weighted_values(g - 1, 0)
                    prob_transposes(g - 1, 2)
                scores(g, b, 1, start)
                if n != 0:
                    prob_transposes(g - 1, 3)
                if settled:
                    pe.wait_ge(v_ready, g + 1)
                    norm2_t(g - 2)
                scores(g, b, 2, start)
                if n != 0:
                    weighted_values(g - 1, 1)
                prob_transposes(g, 0)
                if layer == 1 and settled:
                    route_logits(g - 2, b - 2)
                scores(g, b, 3, start)
                if n != B - 1:
                    if not settled:
                        pe.wait_ge(v_ready, g + 1)
                    else:
                        pe.wait_ge(stage_ready, g - 1)
                        if layer == 1:
                            pe.wait_ge(logit_done, b - 1)
                    norm_t(g + 1)
                if n != 0:
                    project_out(g - 1)
                prob_transposes(g, 1)
                if n != B - 1:
                    if n != 0:
                        pe.wait_ge(x_new, g)
                    queries(g + 1)
                    values(g + 1)

            def attention(layer):
                keys(layer)
                norm_t(B * layer)
                pe.wait_ge(wa_in, 16 * 3 * (layer + 1))
                queries(B * layer)
                values(B * layer)
                attention_step(layer, 0, 0)
                attention_step(layer, 1, 1)
                with pe.Fori(2, B - 1) as b:
                    attention_step(layer, b, None)
                attention_step(layer, B - 1, B - 1)
                g = B * layer + B - 1
                pe.wait_ge(x_new, g)
                weighted_values(g, 0)
                prob_transposes(g, 2)
                pe.wait_ge(stage_ready, g - 1)
                if layer == 1:
                    pe.wait_ge(logit_done, B - 2)
                norm2_t(g - 1)
                prob_transposes(g, 3)
                if layer == 1:
                    route_logits(g - 1, B - 2)
                weighted_values(g, 1)
                project_out(g)
                pe.wait_ge(stage_ready, g)
                if layer == 1:
                    pe.wait_ge(logit_done, B - 1)
                norm2_t(g)
                if layer == 1:
                    route_logits(g, B - 1)

            def first_layer(e):
                for m in range(M0):
                    pe.wait_ge(hi13, M0 * e + m + 1)
                    pe.wait_ge(lo13, M0 * e + m + 1)
                    pe.wait_ge(gu_free, M0 * e + m + 1)
                    for gu in range(2 if m < M0 - 1 else 1):
                        for kt in range(KT):
                            c = kt * (2 * P if m < M0 - 1 else P) + gu * P
                            rhs = [a[:, kt, :].rearrange("p (b s) -> p b s", s=S)[:, :, bass.ds(e * C0, C0)] for a in (act_hi, act_lo)]
                            last = mm3(banks[2 + m % 3][:, gu * S:(gu + 1) * S], w_hi[:, m, c:c + P], w_lo[:, m, c:c + P],
                                       rhs[0], rhs[1], kt == 0, kt == KT - 1)
                    last.then_inc(gu_psum, 1)
                pe.wait_ge(y0_done, e + 1)
                for k in range(M0):
                    j, c = k // 2, k % 2 * D
                    pe.wait_ge(hid_ready, M0 * e + k + 1)
                    if k % 2 == 0:
                        pe.wait_ge(hi2, 3 * e + j + 1)
                        if j == 0:
                            pe.wait_ge(lo2, e + 1)
                        else:
                            pe.wait_ge(lo2_first, 2 * e + j)
                    for h in range(HALVES):
                        last = mm3(bank_p[h][:, 0:D], hid_hi[:, k, h * P:(h + 1) * P], hid_lo[:, k, h * P:(h + 1) * P],
                                   w_hi[:, M0 + j, c:c + D], w_lo[:, M0 + j, c:c + D], k == 0, k == M0 - 1)
                last.then_inc(y0_psum, 1)

            def gate_up(n, f, width, rhs_hi, rhs_lo):
                for gu in range(2):
                    for kt in range(KT):
                        c = kt * 2 * P + gu * P
                        last = mm3(banks[2 + 2 * (f % 2) + gu][:, 0:width], w_hi[:, f, c:c + P], w_lo[:, f, c:c + P],
                                   rhs_hi[kt], rhs_lo[kt], kt == 0, kt == KT - 1)
                last.then_inc(gu_psum, 1)

            def down(o, at, width, n=None):
                for f in range(FT):
                    j, c = FT + f // 2, f % 2 * D
                    if n is not None:
                        pe.wait_ge(hid_ready, n + f + 1)
                    last = mm3(o, hid_hi[:, f, at:at + width], hid_lo[:, f, at:at + width], w_hi[:, j, c:c + D], w_lo[:, j, c:c + D],
                               f == 0, f == FT - 1)
                return last

            def shared_base(c):
                return GU_SHARED + FT * c if c < EARLY else GU_LATE + FT * (c - EARLY)

            def shared_gate_up(c, f):
                n = shared_base(c) + f
                pe.wait_ge(gu_free, n + 2)
                gate_up(n, f, PIECE, *([a[:, kt, c * PIECE:(c + 1) * PIECE] for kt in range(KT)] for a in (act_hi, act_lo)))

            def shared_down(c, j):
                if 4 * c + j >= 2:
                    pe.wait_ge(ys_done, 4 * c + j - 1)
                down(bank_p[j % 2][:, 0:D], j * P, P, shared_base(c) if j == 0 else None).then_inc(ys_psum, 1)

            def shared_weights(entry):
                pe.wait_ge(hi13, PIECES0 + FT * (entry + 1))
                pe.wait_ge(lo13, PIECES0 + FT * (entry + 1))

            def shared_down_weights(entry):
                pe.wait_ge(hi2, 3 * E0 + 4 * (entry + 1))
                pe.wait_ge(lo2, E0 + 4 * (entry + 1))

            def shared(c):
                for f in range(FT):
                    shared_gate_up(c, f)
                shared_down_weights(0 if c < EARLY else STREAM - 1)
                for j in range(4):
                    shared_down(c, j)

            def slots_t(e, hf):
                pe.wait_ge(xe_load, 16 * (e + 1))
                for kt in range(KT):
                    n = 4 * e + KT * hf + kt
                    if not isinstance(e, int) or n >= KT:
                        pe.wait_ge(xe_ready, n - KT + 1)
                    for j in range(3):
                        last = nc.tensor.transpose(bank[kt][:, j * TR:(j + 1) * TR],
                                                   xe_in[:, 3 * hf + j, kt * P:(kt + 1) * P], ident[0:TR, 0:TR])
                    last.then_inc(xet_psum, 1)

            def expert(e, last_one):
                for hf in range(2):
                    pe.wait_ge(xe_ready, 4 * e + KT * hf + KT)
                    for f in range(FT):
                        n = GU_ROUTED + 2 * FT * e + FT * hf + f
                        if hf == 0:
                            pe.wait_ge(hi13, PIECES0 + FT * (e + 1) + f + 1)
                            pe.wait_ge(lo13, PIECES0 + FT * (e + 1) + f + 1)
                        pe.wait_ge(gu_free, n + 2)
                        gate_up(n, f, HC, *([a[:, kt, hf * HC:(hf + 1) * HC] for kt in range(KT)] for a in (xe_hi, xe_lo)))
                        if hf == 1 and f == FT // 2 and not last_one:
                            slots_t(e + 1, 0)
                if not last_one:
                    slots_t(e + 1, 1)
                pe.wait_ge(hi2, 3 * E0 + 4 * (e + 1) + 4)
                pe.wait_ge(lo2, E0 + 4 * (e + 1) + 4)
                for j in range(TT):
                    pe.wait_ge(hid_ready, GU_ROUTED + 2 * FT * e + FT * (j // 3) + FT)
                    if not (isinstance(e, int) and e == 0 and j < 2):
                        pe.wait_ge(yr_copied, TT * e + j - 1)
                    down(bank_p[j % 2][0:TR, 0:D], j * TR, TR).then_inc(yr_psum, 1)

            pe.wait_ge(masked, 2)
            attention(0)
            pe.wait_ge(lo_ready, B)
            pe.wait_ge(hi_ready, B)
            with pe.Fori(0, E0) as e:
                first_layer(e)
            attention(1)
            pe.wait_ge(lo_ready, 2 * B)
            pe.wait_ge(hi_ready, 2 * B)
            shared_weights(0)
            pe.wait_ge(logit_done, B)
            pe.wait_ge(x_new, 2 * B)
            for f in range(FT):
                shared_gate_up(0, f)
                if f == 1:
                    pe.wait_ge(route, 1)
                    pick_v = pick[:].rearrange("p c t e -> p (c t e)")
                    nc.tensor.matmul(bank[0][:, 0:2 * T * E1], before[:], pick_v, start=True, stop=False)
                    nc.tensor.matmul(bank[0][:, 0:2 * T * E1], ones[:], cum[1][:].rearrange("p g e -> p (g e)"),
                                     start=False, stop=True).then_inc(pos_psum, 1)
            shared_down_weights(0)
            for j in range(4):
                shared_down(0, j)
            shared(1)
            slots_t(0, 0)
            slots_t(0, 1)
            pe.wait_ge(ys_done, 4 * EARLY)
            expert(0, False)
            with pe.Fori(1, E1 - 1) as e:
                expert(e, False)
            expert(E1 - 1, True)
            shared_weights(STREAM - 1)
            pe.wait_ge(yr_copied, TT * E1)
            shared(2)
            shared(3)

        @block.scalar
        def _(act):
            def split13(slot_f, n_load, at, width=PIECE):
                act.wait_ge(raw_in[slot_f], 16 * n_load)
                nc.scalar.activation(w_hi[:, at, 0:width], raw[:, slot_f, 0:width], ACT.Copy).then_inc(hi13, 1)

            def split2(slot_j, n_load, at):
                act.wait_ge(raw_in[slot_j], 16 * n_load)
                nc.scalar.activation(w_hi[:, at, :], raw[:, slot_j, :], ACT.Copy).then_inc(hi2, 1)

            def keys(layer):
                act.wait_ge(k_psum, layer + 1)
                w = B * KV // 2
                for dt in range(KT):
                    last = nc.scalar.activation(k_t[:, dt, :].rearrange("p (h n) -> p h n", h=2), score[dt][:, :, 0:w], ACT.Identity,
                                                bias=bias_cols[:, layer, 1, dt:dt + 1])
                last.then_inc(kt_ready, 1)

            def norm_t(g):
                act.wait_ge(xnt_psum, g + 1)
                nc.scalar.activation(xn_t[:].rearrange("p k s -> p (k s)"), bank[0][:], ACT.Copy).then_inc(xnt_ready, 1)

            def norm2_t(g, first):
                act.wait_ge(xn2t_psum, g + 1)
                if not first:
                    act.wait_ge(lo_ready, g)
                    act.wait_ge(hi_ready, g)
                nc.scalar.activation(stage[:].rearrange("p k s -> p (k s)"), bank[0][:], ACT.Copy).then_inc(stage_ready, 1)

            def high(g, b):
                act.wait_ge(stage_ready, g + 1)
                nc.scalar.activation(act_hi[:, :, bass.ds(b * S, S)], stage[:], ACT.Copy).then_inc(hi_ready, 1)

            def queries(layer, g):
                act.wait_ge(q_psum, g + 1)
                for dt in range(KT):
                    last = nc.scalar.activation(q_t[:, dt, :], bank[1][:, dt * S:(dt + 1) * S], ACT.Identity,
                                                bias=bias_cols[:, layer, 0, dt:dt + 1])
                last.then_inc(qt_ready, 1)

            def exps(g, u):
                act.wait_ge(sub_done, 4 * g + u + 1)
                pv = prob[u][:, 0:HT * KV]
                nc.scalar.activation(pv, pv, ACT.Exp).then_inc(exp_done, 1)

            def probs_t(g, u):
                dt, qt = divmod(u, 2)
                for grp, (j, n) in enumerate(((0, 3), (3, 2))):
                    act.wait_ge(pt_psum, 8 * g + 2 * u + grp + 1)
                    at = dt * PT + j
                    nc.scalar.activation(prob_t[0:PR, at:at + n, qt * P:(qt + 1) * P],
                                         bank_p[grp][0:PR, 0:n * P].rearrange("p (j n) -> p j n", j=n), ACT.Copy).then_inc(pt_ready, 1)

            def out_t(g):
                act.wait_ge(pv_psum, KT * g + KT)
                nc.scalar.activation(o_t[:].rearrange("p k s -> p (k s)"), bank[1][:], ACT.Copy).then_inc(ot_ready, 1)

            def attention_step(layer, b, n):
                g = b + B * layer
                settled = n is None or n >= 2
                exps(g, 0)
                if n != 0:
                    probs_t(g - 1, 2)
                    probs_t(g - 1, 3)
                if settled:
                    norm2_t(g - 2, layer == 0 and n == 2)
                exps(g, 1)
                if settled:
                    high(g - 2, b - 2)
                exps(g, 2)
                if n != 0:
                    out_t(g - 1)
                probs_t(g, 0)
                if layer == 1 and n in (0, 1):
                    split13(M0 + n, piece13_slot_load(0, M0 + n), M0 + n)
                if layer == 0 and settled:
                    p = bass.ds(b - 2, 1)
                    nc.scalar.activation(w_hi[:, p, :], raw[:, p, :], ACT.Copy).then_inc(hi13, 1)
                if n != B - 1:
                    norm_t(g + 1)
                exps(g, 3)
                probs_t(g, 1)
                if n != B - 1:
                    queries(layer, g + 1)

            def attention(layer):
                keys(layer)
                norm_t(B * layer)
                queries(layer, B * layer)
                if layer == 1:
                    act.wait_ge(y0_psum, E0)
                attention_step(layer, 0, 0)
                attention_step(layer, 1, 1)
                if layer == 0:
                    for m in range(M0):
                        act.wait_ge(raw_in[m], 16)
                    attention_step(layer, 2, 2)
                with act.Fori(3 if layer == 0 else 2, B - 1) as b:
                    attention_step(layer, b, None)
                attention_step(layer, B - 1, B - 1)
                g = B * layer + B - 1
                probs_t(g, 2)
                norm2_t(g - 1, False)
                probs_t(g, 3)
                high(g - 1, B - 2)
                out_t(g)
                norm2_t(g, False)
                high(g, B - 1)

            def silu_of(n, buf, src, rows_n, width):
                act.wait_ge(gu_psum, n + 1)
                act.wait_ge(gu_free, n + 2)
                nc.scalar.activation(silu[0:rows_n, buf, 0:width], src, ACT.Silu).then_inc(silu_done, 1)

            def first_layer(e, i, part):
                for m in range(M0):
                    src = banks[2 + m % 3]
                    silu_of(M0 * e + m, m % 2, src[:, 0:S] if m < M0 - 1 else src[0:64, 0:S], P if m < M0 - 1 else 64, S)
                    if m < 3:
                        split2(M0 + m, e + 1, M0 + m)
                    split13(m, e + 2, m)
                act.wait_ge(y0_psum, e + 1)
                for h in range(HALVES):
                    for j in range(B // HALVES):
                        last = nc.scalar.activation(
                            yh[i * C0:(i + 1) * C0, h * (B // HALVES) + j, bass.ds(part * D, D)], bank_p[h][j * C0:(j + 1) * C0, 0:D], ACT.Copy)
                last.then_inc(y0_done, 1)

            def shared(c):
                base = GU_SHARED + FT * c if c < EARLY else GU_LATE + FT * (c - EARLY)
                for f in range(FT):
                    silu_of(base + f, f % 2, banks[2 + 2 * (f % 2)], P, PIECE)
                    if c == 0 and f == 1:
                        act.wait_ge(e_done, 1)
                        nc.scalar.activation(e_dif[:], e_dif[:], ACT.Exp).then_inc(e_done, 1)
                    if c == EARLY - 1:
                        split13(f, piece13_slot_load(1, f), f)
                    if c == EARLY and f < 4:
                        split2(f, piece2_slot_load(STREAM - 1, f), FT + f)

            def expert(e, last_one):
                for hf in range(2):
                    for f in range(FT):
                        silu_of(GU_ROUTED + 2 * FT * e + FT * hf + f, f % 2, banks[2 + 2 * (f % 2)][:, 0:HC], P, HC)
                        if hf == 0 and f < 4:
                            split2(f, piece2_slot_load(e + 1, f), FT + f)
                        if hf == 1:
                            split13(f, piece13_slot_load(e + 2, f), f)
                        if hf == 1 and f == FT // 2 and not last_one:
                            slots_hi(e + 1, 0)
                if not last_one:
                    slots_hi(e + 1, 1)

            def slots_hi(e, hf):
                for kt in range(KT):
                    act.wait_ge(xet_psum, 4 * e + KT * hf + kt + 1)
                    nc.scalar.activation(xe_hi[:, kt, hf * HC:(hf + 1) * HC], bank[kt][:, 0:HC], ACT.Copy).then_inc(xe_hi_done, 1)

            act.wait_ge(small_in, 64)
            nc.scalar.activation(tanh_gate[:], gate[:], ACT.Tanh).then_inc(tanh_done, 1)
            attention(0)
            act.wait_ge(zero_out, 16 * B)
            per = E0 // HALVES
            with act.Fori(0, HALVES) as part:
                for i in range(per):
                    first_layer(per * part + i, i, part)
            attention(1)
            for j in range(4):
                split2(j, piece2_slot_load(0, j), FT + j)
            shared(0)
            shared(1)
            slots_hi(0, 0)
            slots_hi(0, 1)
            with act.Fori(0, E1 - 1) as e:
                expert(e, False)
            expert(E1 - 1, True)
            shared(2)
            shared(3)

        @block.vector
        def _(dve):
            def carry(n):
                if not isinstance(n, int):
                    nc.vector.memset(waited[:], 0.0)

            def row_stats(src, st, st_sem, m, m_sem, g):
                for h in range(HALVES):
                    last = nc.vector.bn_stats(st[:, h, :], src(h))
                last.then_inc(st_sem, 1)
                dve.wait_ge(st_sem, g + 1)
                carry(g)
                for h in range(HALVES):
                    last = nc.vector.bn_aggr(m[:, h, :], st[:, h, :])
                last.then_inc(m_sem, 1)

            def xs_row(b, h):
                return xs[:, bass.ds(b * HALVES + h, 1), :].rearrange("p a d -> p (a d)")

            def norm_stats(layer, b, first):
                g = b + B * layer
                if layer == 0 and isinstance(b, int) and b < 2:
                    dve.wait_ge(x_rest if b else x_first, 16)
                if layer == 1:
                    dve.wait_ge(x_ffn, b + 1)
                if not first:
                    dve.wait_ge(xn_ready, g)
                carry(g)
                row_stats(lambda h: xs_row(b, h), stats, stats_done, mv, mv_done, g)

            def normalise(src, dst, m, r, r_sem, done, g):
                dve.wait_ge(r_sem, g + 1)
                for h in range(HALVES):
                    last = nc.vector.tensor_scalar(dst[:, h, :], src(h), m[:, h, 0:1], r[:, h:h + 1], ALU.subtract, ALU.mult)
                last.then_inc(done, 1)

            def norm(layer, b, first):
                g = b + B * layer
                if not first:
                    dve.wait_ge(xnt_psum, g)
                normalise(lambda h: xs_row(b, h), xn, mv, rstd, rstd_done, xn_ready, g)

            def norm2(layer, b, g, first):
                if not first:
                    dve.wait_ge(xn2t_psum, g)
                if layer == 1 and not (isinstance(b, int) and b == 0):
                    dve.wait_ge(rows_kept, b)
                normalise(lambda h: xs_row(b, h), xn2, mv2, rstd2, rstd2_done, xn2_ready if layer == 0 else y_ready, g)

            def norm3(b):
                normalise(lambda h: xn2[:, h, :], xn2, mv3, rstd3, rstd3_done, h_normed, b)

            def add_first_layer(b):
                two = xs[:, bass.ds(b * HALVES, HALVES), :].rearrange("p a d -> p (a d)")
                nc.vector.scalar_tensor_tensor(out=two, in0=yh[:, bass.ds(b, 1), :].rearrange("p a n -> p (a n)"), scalar=tanh_gate[:, 2:3], in1=two,
                                               op0=ALU.mult, op1=ALU.add).then_inc(x_ffn, 1)

            def by_head(p):
                return p[:, 0:HT * KV].rearrange("p (a h n) -> p a h n", a=2, n=KV)

            def max_sub(g, u, start):
                dve.wait_ge(s_psum, 4 * g + u + 1)
                sv = score[u % 2][:, :, 0:SW].rearrange("p a (h n) -> p a h n", n=KV)
                nc.vector.tensor_reduce(mx[:, u], sv, AX_X, ALU.max).then_inc(max_done, 1)
                dve.wait_ge(max_done, 4 * g + u + 1)
                if not start:
                    dve.wait_ge(pt_psum, 8 * g - 8 + 2 * u + 2)
                nc.vector.tensor_tensor(by_head(prob[u]), sv, mx[:, u].unsqueeze(3).to_broadcast([P, 2, HT // 2, KV]),
                                        ALU.subtract).then_inc(sub_done, 1)

            def sums(g, u):
                dve.wait_ge(exp_done, 4 * g + u + 1)
                nc.vector.tensor_reduce(total[:, u], by_head(prob[u]), AX_X, ALU.add).then_inc(sum_done, 1)
                dve.wait_ge(sum_done, 4 * g + u + 1)
                nc.vector.reciprocal(recip[:, u], total[:, u]).then_inc(recip_done, 1)

            def values(layer, b, n):
                g = b + B * layer
                dve.wait_ge(v_psum, g + 1)
                if n is None or n >= 2 or layer == 1:
                    for dt in range(KT):
                        dve.wait_ge(v_in[dt], 16 * len(RUNS) * (g - 1))
                o = v_rows[0:KV, bass.ds(b % 2, 1), :].rearrange("p a d -> p (a d)")
                ins = (nc.vector.tensor_tensor(o, bank[0][0:KV, 0:D], row[0:KV, 2, :], ALU.add) if layer == 1
                       else nc.vector.tensor_copy(o, bank[0][0:KV, 0:D]))
                ins.then_inc(v_ready, 1)

            def add_attention(layer, b, g):
                dve.wait_ge(o_psum, g + 1)
                dve.wait_ge(xb_done, g + 1)
                two = xs[:, bass.ds(b * HALVES, HALVES), :].rearrange("p a d -> p (a d)")
                nc.vector.scalar_tensor_tensor(out=two, in0=bank[1][:], scalar=tanh_gate[:, layer:layer + 1], in1=two,
                                               op0=ALU.mult, op1=ALU.add).then_inc(x_new, 1)

            def norm2_stats(b, g, first):
                dve.wait_ge(x_new, g + 1)
                if not first:
                    dve.wait_ge(xn2_ready, g)
                carry(g)
                row_stats(lambda h: xs_row(b, h), stats2, stats2_done, mv2, mv2_done, g)

            def norm3_stats(b):
                dve.wait_ge(y_ready, b + 1)
                carry(b)
                row_stats(lambda h: xn2[:, h, :], stats3, stats3_done, mv3, mv3_done, b)

            def keep_logits(b):
                dve.wait_ge(logit_psum, b + 1)
                nc.vector.tensor_copy(logits[:, bass.ds(b * HALVES, HALVES), :],
                                      bank[0][:, 0:HALVES * 8].rearrange("p (h e) -> p h e", h=HALVES)).then_inc(logit_done, 1)

            def attention_step(layer, b, n):
                g = b + B * layer
                start = layer == 0 and n == 0
                settled = n is None or n >= 2
                more = n != B - 1
                max_sub(g, 0, start)
                if more:
                    if layer == 1:
                        add_first_layer(b + 1)
                    norm_stats(layer, b + 1, False)
                sums(g, 0)
                max_sub(g, 1, start)
                if more:
                    norm(layer, b + 1, False)
                max_sub(g, 2, start)
                sums(g, 1)
                if layer == 1 and settled:
                    keep_logits(b - 2)
                sums(g, 2)
                max_sub(g, 3, start)
                if n != 0:
                    add_attention(layer, b - 1, g - 1)
                    norm2_stats(b - 1, g - 1, layer == 0 and n == 1)
                sums(g, 3)
                if n != 0:
                    norm2(layer, b - 1, g - 1, layer == 0 and n == 1)
                    if layer == 1:
                        norm3_stats(b - 1)
                if more:
                    values(layer, b + 1, None if n is None else n + 1)
                if layer == 1 and n != 0:
                    norm3(b - 1)

            def clear_attention():
                for p in prob:
                    nc.vector.memset(p[:, HT * KV:], 0.0)
                nc.vector.memset(v_blk[:], 0.0).then_inc(v_zero, 1)

            def attention(layer):
                if layer == 1:
                    dve.wait_ge(y0_done, E0 + 1)
                    clear_attention()
                    dve.wait_ge(v_zero, 2)
                    add_first_layer(0)
                norm_stats(layer, 0, layer == 0)
                norm(layer, 0, layer == 0)
                values(layer, 0, 0)
                attention_step(layer, 0, 0)
                attention_step(layer, 1, 1)
                with dve.Fori(2, B - 1) as b:
                    attention_step(layer, b, None)
                attention_step(layer, B - 1, B - 1)
                g = B * layer + B - 1
                if layer == 1:
                    keep_logits(B - 2)
                add_attention(layer, B - 1, g)
                norm2_stats(B - 1, g, False)
                norm2(layer, B - 1, g, False)
                if layer == 1:
                    norm3_stats(B - 1)
                    norm3(B - 1)
                    keep_logits(B - 1)

            def hidden(n, buf, up, rows_n, at, f, width):
                dve.wait_ge(silu_done, n + 1)
                dve.wait_ge(hid_ready, n) if not isinstance(n, int) or n > 0 else None
                nc.vector.tensor_tensor(prod[0:rows_n, 0:width], silu[0:rows_n, buf, 0:width], up, ALU.mult).then_inc(gu_free, 1)
                dve.wait_ge(gu_free, n + 4)
                nc.vector.tensor_copy(hid_hi[0:rows_n, f, at:at + width], prod[0:rows_n, 0:width]).then_inc(hid_hi_done, 1)
                dve.wait_ge(hid_hi_done, n + 1)
                nc.vector.tensor_tensor(hid_lo[0:rows_n, f, at:at + width], prod[0:rows_n, 0:width],
                                        hid_hi[0:rows_n, f, at:at + width].bitcast(F32), ALU.subtract).then_inc(hid_ready, 1)

            def first_layer(e):
                for m in range(M0):
                    src = banks[2 + m % 3]
                    up = src[:, S:2 * S] if m < M0 - 1 else src[64:P, 0:S]
                    hidden(M0 * e + m, m % 2, up, P if m < M0 - 1 else 64, 0, m, S)
                    if 2 <= m <= 3:
                        j = m - 1
                        dve.wait_ge(hi2, 3 * e + j + 1)
                        nc.vector.tensor_tensor(w_lo[:, M0 + j, :], raw[:, M0 + j, :], w_hi[:, M0 + j, :].bitcast(F32),
                                                ALU.subtract).then_inc(lo2_first, 1)

            def shared_hidden(c, f):
                n = (GU_SHARED + FT * c if c < EARLY else GU_LATE + FT * (c - EARLY)) + f
                hidden(n, f % 2, banks[2 + 2 * (f % 2) + 1], P, 0, f, PIECE)

            def shared_add(c, j):
                dve.wait_ge(ys_psum, 4 * c + j + 1)
                two = xs[:, 4 * c + j, :]
                nc.vector.scalar_tensor_tensor(out=two, in0=bank_p[j % 2][:, 0:D], scalar=tanh_gate[:, 3:4], in1=two,
                                               op0=ALU.mult, op1=ALU.add).then_inc(ys_done, 1)

            def shared(c):
                for f in range(FT):
                    shared_hidden(c, f)
                for j in range(4):
                    shared_add(c, j)

            def slots_lo(e, hf):
                for kt in range(KT):
                    dve.wait_ge(xe_hi_done, 4 * e + KT * hf + kt + 1)
                    nc.vector.tensor_tensor(xe_lo[:, kt, hf * HC:(hf + 1) * HC], bank[kt][:, 0:HC],
                                            xe_hi[:, kt, hf * HC:(hf + 1) * HC].bitcast(F32), ALU.subtract).then_inc(xe_ready, 1)

            def expert(e, last_one):
                for hf in range(2):
                    for f in range(FT):
                        hidden(GU_ROUTED + 2 * FT * e + FT * hf + f, f % 2, banks[2 + 2 * (f % 2) + 1][:, 0:HC], P, hf * HC, f, HC)
                        if hf == 1 and f == FT // 2 and not last_one:
                            slots_lo(e + 1, 0)
                if not last_one:
                    slots_lo(e + 1, 1)
                for j in range(TT):
                    dve.wait_ge(yr_psum, TT * e + j + 1)
                    if j == 0 and not (isinstance(e, int) and e == 0):
                        dve.wait_ge(y_stored, 16 * e)
                    nc.vector.tensor_copy(y_out[:, j, :], bank_p[j % 2][0:TR, 0:D]).then_inc(yr_copied, 1)

            def routing_choices():
                steps = [0]

                def step(ins):
                    steps[0] += 1
                    ins.then_inc(added, 1)
                    dve.wait_ge(added, steps[0])

                for e in range(E1):
                    nc.vector.memset(order_w[:, e:e + 1], float(E1 - e))
                    last = nc.vector.memset(base_e[:, e:e + 1], float(CAP * e))
                step(last)
                dve.wait_ge(logit_done, B)
                lv = logits[:, :, 0:E1]
                wide = [P, T, E1]
                w_bc = order_w[:].unsqueeze(1).to_broadcast(wide)
                for c in range(2):
                    src = lv if c == 0 else cand[:]
                    step(nc.vector.tensor_reduce(top[:, c, :], src, AX_X, ALU.max))
                    step(nc.vector.tensor_tensor(eq[:], src, top[:, c, :].unsqueeze(2).to_broadcast(wide), ALU.is_equal))
                    step(nc.vector.tensor_tensor(eq[:], eq[:], w_bc, ALU.mult))
                    step(nc.vector.tensor_reduce(best[:], eq[:], AX_X, ALU.max))
                    step(nc.vector.tensor_tensor(pick[:, c], w_bc, best[:].unsqueeze(2).to_broadcast(wide), ALU.is_equal))
                    if c == 0:
                        step(nc.vector.scalar_tensor_tensor(out=cand[:], in0=pick[:, 0], scalar=-3.0e38, in1=lv, op0=ALU.mult, op1=ALU.add))
                nc.vector.tensor_tensor(e_dif[:], top[:, 1, :], top[:, 0, :], ALU.subtract).then_inc(e_done, 1)
                flat = pick[:].rearrange("p c t e -> p (c t) e")
                step(nc.vector.memset(cum[0][:, 0, :], 0.0))
                step(nc.vector.tensor_copy(cum[0][:, 1:, :], flat[:, 0:2 * T - 1, :]))
                d, at = 1, 0
                while d < 2 * T:
                    a, o = cum[at], cum[1 - at]
                    step(nc.vector.tensor_copy(o[:, 0:d, :], a[:, 0:d, :]))
                    ins = nc.vector.tensor_tensor(o[:, d:, :], a[:, d:, :], a[:, 0:2 * T - d, :], ALU.add)
                    d, at = 2 * d, 1 - at
                    if d >= 2 * T:
                        ins.then_inc(route, 1)
                    else:
                        step(ins)
                assert at == 1
                return steps

            def routing_slots(steps):
                def step(ins):
                    steps[0] += 1
                    ins.then_inc(added, 1)
                    dve.wait_ge(added, steps[0])

                flat = pick[:].rearrange("p c t e -> p (c t) e")
                dve.wait_ge(pos_psum, 1)
                step(nc.vector.tensor_tensor(cum[0][:], bank[0][:, 0:2 * T * E1].rearrange("p (g e) -> p g e", e=E1), flat, ALU.mult))
                step(nc.vector.tensor_reduce(pos[:], cum[0][:], AX_X, ALU.add))
                step(nc.vector.tensor_tensor(cum[0][:], flat, base_e[:].unsqueeze(1).to_broadcast([P, 2 * T, E1]), ALU.mult))
                step(nc.vector.tensor_reduce(first[:], cum[0][:], AX_X, ALU.add))
                step(nc.vector.tensor_scalar(keep[:], pos[:], float(CAP), None, ALU.is_lt))
                step(nc.vector.tensor_tensor(slot[:], pos[:], first[:], ALU.add))
                step(nc.vector.scalar_tensor_tensor(out=pos[:], in0=slot[:], scalar=-float(2 * SLOTS), in1=keep[:], op0=ALU.add, op1=ALU.mult))
                step(nc.vector.tensor_scalar(slot_put[:], pos[:], float(2 * SLOTS), None, ALU.add))
                step(nc.vector.tensor_tensor(slot_get[:], slot[:], keep[:], ALU.mult))
                dve.wait_ge(e_done, 2)
                step(nc.vector.tensor_scalar(den[:], e_dif[:], 1.0, None, ALU.add))
                step(nc.vector.reciprocal(gates12[:, 0, :], den[:]))
                step(nc.vector.tensor_tensor(gates12[:, 1, :], gates12[:, 0, :], e_dif[:], ALU.mult))
                nc.vector.scalar_tensor_tensor(out=weight[:], in0=gates12[:].rearrange("p c t -> p (c t)"), scalar=tanh_gate[:, 3:4],
                                               in1=keep[:], op0=ALU.mult, op1=ALU.mult).then_inc(slots_ready, 1)

            clear_attention()
            dve.wait_ge(v_zero, 1)
            dve.wait_ge(tanh_done, 1)
            for layer in range(2):
                last = nc.vector.tensor_scalar(row[:, layer, :], row[:, layer, :], tanh_gate[:, layer:layer + 1], None, ALU.mult)
            last.then_inc(bias_done, 1)
            attention(0)
            for t in (hid_hi, hid_lo):
                last = nc.vector.memset(t[64:P, M0 - 1, 0:S].bitcast(F32), 0.0)
            last.then_inc(tail_zero, 1)
            dve.wait_ge(tail_zero, 1)
            dve.wait_ge(zero_out, 16 * B)
            dve.sem_inc(gu_free, 3)
            dve.sem_inc(y0_done, 1)
            with dve.Fori(0, E0) as e:
                first_layer(e)
            attention(1)
            steps = routing_choices()
            for f in range(FT):
                shared_hidden(0, f)
                if f == 2:
                    routing_slots(steps)
            for j in range(4):
                shared_add(0, j)
            shared(1)
            slots_lo(0, 0)
            slots_lo(0, 1)
            expert(0, False)
            with dve.Fori(1, E1 - 1) as e:
                expert(e, False)
            expert(E1 - 1, True)

            def add_routed(t):
                for k in range(2):
                    if k == 1:
                        dve.wait_ge(added, steps[0] + t + 1)
                    ins = nc.vector.scalar_tensor_tensor(out=xs[:, t, :], in0=yg(k, t), scalar=weight[:, k * T + t:k * T + t + 1],
                                                         in1=xs[:, t, :], op0=ALU.mult, op1=ALU.add)
                    ins.then_inc(added if k == 0 else final, 1)

            shared(2)
            dve.wait_ge(slots_ready, 1)
            dve.wait_ge(ys_done, 4 * (EARLY + 1))
            for f in range(FT):
                shared_hidden(3, f)
                for t in range(f * 3 // 2, (f + 1) * 3 // 2):
                    if t % 4 == 0:
                        dve.wait_ge(gathered[t // 4], 16 * 8)
                    add_routed(t)
            dve.wait_ge(gathered[3], 16 * 8)
            for j in range(4):
                shared_add(3, j)
                dve.wait_ge(ys_done, 13 + j)
                add_routed(12 + j)

        @block.gpsimd
        def _(pool):
            def rstd_of(m, r, eps_sem, r_sem, g, m_sem):
                pool.wait_ge(m_sem, g + 1)
                nc.gpsimd.tensor_tensor(r[:], m[:, :, 1], eps_tile[:], ALU.add).then_inc(eps_sem, 1)
                pool.wait_ge(eps_sem, g + 1)
                nc.gpsimd.tensor_tensor(r[:], r[:], neg_half[:], ALU.pow).then_inc(r_sem, 1)

            def add_out_bias(layer, b):
                pool.wait_ge(xn_ready, b + B * layer + 1)
                settle(pool)
                two = xs[:, bass.ds(b * HALVES, HALVES), :]
                nc.gpsimd.tensor_tensor(two, two, row[:, layer, :].unsqueeze(1).to_broadcast([P, HALVES, D]), ALU.add).then_inc(xb_done, 1)

            def gain_and_bias(b, g):
                wide = [P, HALVES, D]
                pool.wait_ge(h_normed, b + 1)
                nc.gpsimd.tensor_tensor(xn2[:], xn2[:], row[:, 3, :].unsqueeze(1).to_broadcast(wide), ALU.mult).then_inc(h_step, 1)
                pool.wait_ge(h_step, b + 1)
                nc.gpsimd.tensor_tensor(xn2[:], xn2[:], row[:, 4, :].unsqueeze(1).to_broadcast(wide), ALU.add).then_inc(xn2_ready, 1)
                pool.wait_ge(xn2_ready, g + 1)
                settle(pool)
                nc.gpsimd.tensor_copy(yh[:, bass.ds(b, 1), :].rearrange("p a n -> p (a n)"),
                                      xn2[:].rearrange("p h d -> p (h d)")).then_inc(rows_kept, 1)

            def keys_blocked(b, g):
                if not isinstance(g, int) or g >= 2:
                    pool.wait_ge(s_psum, 4 * g - 4)
                    settle(pool)
                for dt in range(KT):
                    last = nc.gpsimd.tensor_tensor(
                        kb[:, b % 2, dt, :].rearrange("p (h n) -> p h n", n=KV),
                        k_t[:, dt, bass.ds(b * KV, KV)].unsqueeze(1).to_broadcast([P, HT, KV]),
                        head_mask[:].unsqueeze(2).to_broadcast([P, HT, KV]), ALU.mult)
                last.then_inc(kb_ready, 1)

            def by_head(p):
                return p[:, 0:HT * KV].rearrange("p (a h n) -> p a h n", a=2, n=KV)

            def normalise_probs(g, u):
                pool.wait_ge(recip_done, 4 * g + u + 1)
                nc.gpsimd.tensor_tensor(by_head(prob[u]), by_head(prob[u]), recip[:, u].unsqueeze(3).to_broadcast([P, 2, HT // 2, KV]),
                                        ALU.mult).then_inc(norm_done, 1)

            def act_low(b, g):
                pool.wait_ge(hi_ready, g + 1)
                settle(pool)
                nc.gpsimd.tensor_tensor(act_lo[:, :, bass.ds(b * S, S)], stage[:], act_hi[:, :, bass.ds(b * S, S)].bitcast(F32),
                                        ALU.subtract).then_inc(lo_ready, 1)

            def low(slot_f, at):
                return nc.gpsimd.tensor_tensor(w_lo[:, at, :], raw[:, slot_f, :], w_hi[:, at, :].bitcast(F32), ALU.subtract)

            def attention_step(layer, b, n):
                g = b + B * layer
                settled = n is None or n >= 2
                more = n != B - 1
                if more:
                    rstd_of(mv, rstd, eps_done, rstd_done, g + 1, mv_done)
                normalise_probs(g, 0)
                if more:
                    keys_blocked(b + 1, g + 1)
                    add_out_bias(layer, b + 1)
                normalise_probs(g, 1)
                if settled:
                    act_low(b - 2, g - 2)
                normalise_probs(g, 2)
                if layer == 1 and n in (0, 1):
                    low13(PIECES0 + M0 + n, M0 + n, M0 + n)
                if layer == 0 and settled:
                    p = bass.ds(b - 2, 1)
                    pool.wait_ge(hi13, b - 1)
                    settle(pool)
                    nc.gpsimd.tensor_tensor(w_lo[:, p, :].rearrange("p a n -> p (a n)"), raw[:, p, :].rearrange("p a n -> p (a n)"),
                                            w_hi[:, p, :].rearrange("p a n -> p (a n)").bitcast(F32), ALU.subtract).then_inc(lo13, 1)
                if n != 0:
                    rstd_of(mv2, rstd2, eps2_done, rstd2_done, g - 1, mv2_done)
                normalise_probs(g, 3)
                if layer == 1 and n != 0:
                    rstd_of(mv3, rstd3, eps3_done, rstd3_done, b - 1, mv3_done)
                    gain_and_bias(b - 1, g - 1)

            def attention(layer):
                rstd_of(mv, rstd, eps_done, rstd_done, B * layer, mv_done)
                add_out_bias(layer, 0)
                pool.wait_ge(kt_ready, layer + 1)
                keys_blocked(0, B * layer)
                attention_step(layer, 0, 0)
                attention_step(layer, 1, 1)
                with pool.Fori(2, B - 1) as b:
                    attention_step(layer, b, None)
                attention_step(layer, B - 1, B - 1)
                g = B * layer + B - 1
                act_low(B - 2, g - 1)
                rstd_of(mv2, rstd2, eps2_done, rstd2_done, g, mv2_done)
                if layer == 1:
                    rstd_of(mv3, rstd3, eps3_done, rstd3_done, B - 1, mv3_done)
                    gain_and_bias(B - 1, g)
                act_low(B - 1, g)

            def low13(n, slot_f, at):
                pool.wait_ge(hi13, n + 1)
                low(slot_f, at).then_inc(lo13, 1)

            def low2(n, slot_j, at):
                pool.wait_ge(hi2, n + 1)
                low(slot_j, at).then_inc(lo2, 1)

            def first_layer(e):
                pool.wait_ge(hi2, 3 * e + 1)
                low(M0, M0).then_inc(lo2, 1)
                for m in range(M0):
                    low13(M0 * (e + 1) + m, m, m)

            def expert(e):
                for f in range(4):
                    low2(3 * E0 + 4 * (e + 1) + f, f, FT + f)
                for f in range(FT):
                    low13(PIECES0 + FT * (e + 2) + f, f, f)

            for t in (ident, before, ones):
                nc.gpsimd.memset(t[:], 1.0)
            nc.gpsimd.memset(head_mask[:], float(HD) ** -0.5)
            nc.gpsimd.memset(eps_tile[:], EPS)
            nc.gpsimd.memset(neg_half[:], -0.5).then_inc(consts, 1)
            pool.wait_ge(consts, 1)
            nc.gpsimd.affine_select(out=ident[:], in_=ident[:], pattern=[[-1, P]], compare_op=ALU.is_equal, fill=0.0,
                                    base=0, channel_multiplier=1).then_inc(masked, 1)
            nc.gpsimd.affine_select(out=before[:], in_=before[:], pattern=[[1, P]], compare_op=ALU.is_gt, fill=0.0,
                                    base=0, channel_multiplier=-1).then_inc(masked, 1)
            nc.gpsimd.affine_select(out=head_mask[:], in_=head_mask[:], pattern=[[-HD, HT]], compare_op=ALU.is_ge, fill=0.0,
                                    base=0, channel_multiplier=1).then_inc(masked, 1)
            pool.wait_ge(masked, 3)
            nc.gpsimd.affine_select(out=head_mask[:], in_=head_mask[:], pattern=[[HD, HT]], compare_op=ALU.is_ge, fill=0.0,
                                    base=HD - 1, channel_multiplier=-1).then_inc(masked, 1)
            nc.gpsimd.memset(yh[:], 0.0).then_inc(zeros, 1)
            pool.wait_ge(masked, 4)
            pool.wait_ge(bias_done, 1)
            attention(0)
            with pool.Fori(0, E0) as e:
                first_layer(e)
            attention(1)
            for j in range(4):
                low2(3 * E0 + j, j, FT + j)
            pool.wait_ge(slots_ready, 1)
            pool.wait_ge(rows_kept, B)
            pool.wait_ge(zero_out, 16 * B)
            for k in range(2 * T):
                t = k % T
                nc.gpsimd.indirect_dma_start(
                    out=xe, out_offset=bass.IndirectOffsetOnAxis(ap=slot_put[:, k:k + 1], axis=0),
                    in_=yh[:, t // HALVES, t % HALVES * D:(t % HALVES + 1) * D], in_offset=None,
                    bounds_check=SLOTS - 1, oob_is_err=False).then_inc(scattered, 16)
            for f in range(FT):
                low13(PIECES0 + FT + f, f, f)
            with pool.Fori(0, E1) as e:
                expert(e)
            for j in range(4):
                low2(3 * E0 + 4 * (STREAM - 1) + j, j, FT + j)
            pool.wait_ge(y_stored, 16 * E1)
            for t in range(T):
                for k in range(2):
                    nc.gpsimd.indirect_dma_start(
                        out=yg(k, t), out_offset=None, in_=ye,
                        in_offset=bass.IndirectOffsetOnAxis(ap=slot_get[:, k * T + t:k * T + t + 1], axis=0),
                        bounds_check=SLOTS - 1, oob_is_err=False).then_inc(gathered[t // 4], 16)


def kernel(**inputs):
    import concourse.bacc as bacc
    from concourse.bass_utils import run_bass_kernel_spmd

    a = {k: np.asarray(v) for k, v in inputs.items()}
    f32 = np.float32

    def pad(t, rows):
        return np.concatenate([t, np.zeros((rows - t.shape[0],) + t.shape[1:], f32)]) if t.shape[0] < rows else t

    def attention_weights(*w):
        return np.stack([m.T for m in w], 1).reshape(KT, P, 4, D)

    def gate_up_pieces(w1, w3, n):
        g, u = (w[:, :n * P].reshape(KT, P, n, P) for w in (w1, w3))
        return [np.stack([g[:, :, f], u[:, :, f]], 2).transpose(1, 0, 2, 3).reshape(P, PIECE) for f in range(n)]

    def down_pieces(w2, n):
        w = pad(w2, n * 2 * P).reshape(n, 2, P, D)
        return [w[j].transpose(1, 0, 2).reshape(P, PIECE) for j in range(n)]

    first = []
    for w1, w3, w2 in zip(a["L0_ffn_w1"], a["L0_ffn_w3"], a["L0_ffn_w2"]):
        tail = np.concatenate([w1[:, 5 * P:], w3[:, 5 * P:]], 1).reshape(KT, P, P).transpose(1, 0, 2).reshape(P, KT * P)
        tail = np.concatenate([tail, np.zeros_like(tail)], 1)
        first.append(np.stack(gate_up_pieces(w1, w3, 5) + [tail] + down_pieces(w2, 3)))
    second = [np.stack(gate_up_pieces(w1, w3, FT) + down_pieces(w2, FT // 2))
              for w1, w3, w2 in [(a["L1_ffn_W1s"], a["L1_ffn_W3s"], a["L1_ffn_W2s"])]
              + list(zip(a["L1_ffn_W1"], a["L1_ffn_W3"], a["L1_ffn_W2"]))]
    zero = np.zeros(D, f32)
    wkv = a["L0_xattn_Wkv"]

    def on_rows(*v):
        return np.broadcast_to(np.stack(v), (P, len(v), v[0].shape[0]))

    def columns(v):
        return v.reshape(KT, P).T

    arrays = {
        "x_d": a["x"].reshape(T, P, D).transpose(1, 0, 2),
        "ctx_d": a["ctx_1024"].reshape(B * KV, D).T.reshape(KT, P, B, KV),
        "attn_w_d": np.stack([attention_weights(a["L0_xattn_Wq"], wkv[:D], wkv[D:], a["L0_xattn_Wout"]),
                              attention_weights(a["L1_xattn_W_q"], a["L1_xattn_W_k"], a["L1_xattn_W_v"], a["L1_xattn_W_o"])]),
        "rows_d": on_rows(a["L0_xattn_bout"], a["L1_xattn_b_o"], a["L1_xattn_b_v"], a["L1_ffn_ln_g"], a["L1_ffn_ln_b"]),
        "cols_d": np.stack([np.stack([columns(zero), columns(zero)], 1),
                            np.stack([columns(a["L1_xattn_b_q"]), columns(a["L1_xattn_b_k"])], 1)], 1),
        "gates_d": np.broadcast_to(np.concatenate([a["g_xattn"], a["g_ffn"]]), (P, 4)),
        "router_d": np.concatenate([a["L1_ffn_Wr"], np.zeros((D, 1), f32)], 1).reshape(KT, P, 8).transpose(1, 0, 2),
        "w_first_d": np.stack(first),
        "w_second_d": np.stack(second),
    }
    arrays = {k: np.ascontiguousarray(v) for k, v in arrays.items()}
    nc = bacc.Bacc("TRN2", target_bir_lowering=False, num_devices=1)
    ins = [nc.dram_tensor(k, v.shape, F32, kind="ExternalInput").ap() for k, v in arrays.items()]
    xe = nc.dram_tensor("slots_in", [SLOTS, D], F32, kind="Internal").ap()
    ye = nc.dram_tensor("slots_out", [SLOTS, D], F32, kind="Internal").ap()
    out = nc.dram_tensor("out_d", [P, T, D], F32, kind="ExternalOutput").ap()
    flamingo_program(nc, *ins, xe, ye, out)
    r = run_bass_kernel_spmd(nc, [arrays], core_ids=[0])
    return np.asarray(r.results[0]["out_d"]).transpose(1, 0, 2).reshape(B, S, D)
```

```python
from contextlib import ExitStack

import numpy as np

import concourse.bass as bass
from concourse import mybir

ALU = mybir.AluOpType
ACT = mybir.ActivationFunctionType
F32 = mybir.dt.float32
F32R = mybir.dt.float32r
I32 = mybir.dt.int32
AX_X = mybir.AxisListType.X

P = 128
B, S, D = 8, 256, 256
KT = D // P
HALVES = S // P
T = B * HALVES
KV, H, HD = 77, 16, 16
HT = H // KT
SC = KV * HT
PT = -(-SC // P)
KP = PT * P // HT
E0, F0 = 8, 704
C0 = S // E0
M0 = 6
E1, F1, CAP = 7, 1024, 732
FT = F1 // P
SLOTS = E1 * CAP
TT, TR = 6, CAP // 6
HC = CAP // 2
EPS = 1e-5
PIECE = 512
Q, K, V, O = range(4)


def flamingo_program(nc, x, ctx_t, attn_w, rows, cols, gates, router_w, w_first, w_second, xe, ye, v_d, out):
    with ExitStack() as scope:
        def sem(name):
            return scope.enter_context(nc.semaphore(name))

        def psum(name, shape):
            return scope.enter_context(nc.psum_tensor(name, shape, F32))

        place = [nc.sbuf_base + (-nc.sbuf_base) % 64]

        def sb(name, shape, dt=F32):
            size = int(np.prod(shape[1:])) * 4
            t = nc.alloc_sbuf_tensor_at(name, shape, dt, offset=place[0])
            place[0] += size + (-size) % 64
            return t

        xs = sb("residual", [P, T, D])
        act_hi = sb("act_hi", [P, KT, B * S], F32R)
        act_lo = sb("act_lo", [P, KT, B * S], F32R)
        raw = sb("raw", [P, 9, PIECE])
        w_hi = sb("w_hi", [P, 12, PIECE], F32R)
        w_lo = sb("w_lo", [P, 12, PIECE], F32R)
        yh = sb("yh", [P, B, HALVES * D])
        ident = sb("ident", [P, P])
        before = sb("before", [P, P])
        ones = sb("ones", [P, P])
        head_mask = sb("head_mask", [P, HT])
        neg_half = sb("neg_half", [P, HALVES])
        eps_tile = sb("eps", [P, HALVES])
        row = sb("row", [P, 4, D])
        bias_cols = sb("bias_cols", [P, 2, 3, KT])
        gate = sb("gate", [P, 4])
        tanh_gate = sb("tanh_gate", [P, 4])
        rw = sb("rw", [P, KT, 8])
        logits = sb("logits", [P, T, 8])
        warm = sb("warm", [P, 1])
        order_w = sb("order_w", [P, E1])
        base_e = sb("base_e", [P, E1])
        phase = place[0]

        prob = [sb(f"prob{u}", [P, PT * P]) for u in range(4)]
        v_blk = sb("v_blk", [P, KT * PT, P])
        ctx_all = sb("ctx_all", [P, KT, B * KV])
        first_ffn_end = phase + 4 * PIECE * 4 + 2 * M0 * S * 4
        assert place[0] <= first_ffn_end
        place[0] = first_ffn_end
        xn = sb("xn", [P, HALVES, D])
        xn_t = sb("xn_t", [P, KT, S])
        q_t = sb("q_t", [P, KT, S])
        v_rows = sb("v_rows", [P, 2, D])
        kb = sb("kb", [P, 2, KT, SC])
        prob_t = sb("prob_t", [P, KT * PT, S])
        k_t = sb("k_t", [P, KT, B * KV])
        end_attention = place[0]

        place[0] = phase
        silu = sb("silu", [P, 2, PIECE])
        prod = sb("prod", [P, 2, PIECE])
        first_hid = place[0]
        first_hid_hi = sb("first_hid_hi", [P, M0, S], F32R)
        first_hid_lo = sb("first_hid_lo", [P, M0, S], F32R)
        assert place[0] == first_ffn_end
        place[0] = first_hid
        hid_hi = sb("hid_hi", [P, FT, CAP], F32R)
        hid_lo = sb("hid_lo", [P, FT, CAP], F32R)
        place[0] = late = max(place[0], end_attention)
        xn2 = sb("xn2", [P, HALVES, D])
        stage = sb("stage", [P, KT, S])
        o_t = sb("o_t", [P, KT, S])
        ctx_b = sb("ctx_b", [P, KT, KV])
        waited = sb("waited", [P, 1])
        stats = sb("stats", [P, HALVES, 6])
        mv = sb("mv", [P, HALVES, 2])
        rstd = sb("rstd", [P, HALVES])
        mx = sb("mx", [P, 4, HT])
        total = sb("total", [P, 4, HT])
        recip = sb("recip", [P, 4, HT])
        stats2 = sb("stats2", [P, HALVES, 6])
        mv2 = sb("mv2", [P, HALVES, 2])
        rstd2 = sb("rstd2", [P, HALVES])
        stats3 = sb("stats3", [P, HALVES, 6])
        mv3 = sb("mv3", [P, HALVES, 2])
        rstd3 = sb("rstd3", [P, HALVES])
        wa = sb("wa", [P, KT, 4, D])
        end_late = place[0]

        place[0] = late
        xe_hi = sb("xe_hi", [P, KT, CAP], F32R)
        xe_lo = sb("xe_lo", [P, KT, CAP], F32R)
        eq = sb("eq", [P, T, E1])
        cand = sb("cand", [P, T, E1])
        pick = sb("pick", [P, 2, T, E1])
        cum = [sb(f"cum{i}", [P, 2 * T, E1]) for i in range(2)]
        top = sb("top", [P, 2, T])
        best = sb("best", [P, T])
        e_dif = sb("e_dif", [P, T])
        den = sb("den", [P, T])
        gates12 = sb("gates12", [P, 2, T])
        pos = sb("pos", [P, 2 * T])
        first = sb("first", [P, 2 * T])
        keep = sb("keep", [P, 2 * T])
        slot = sb("slot", [P, 2 * T])
        slot_put = sb("slot_put", [P, 2 * T], I32)
        slot_get = sb("slot_get", [P, 2 * T], I32)
        weight = sb("weight", [P, 2 * T])
        end_ffn = place[0]
        yh_rows = yh[:].rearrange("p b n -> p (b n)")
        xe_in = yh_rows[0:TR, 0:TT * D].rearrange("p (j n) -> p j n", j=TT)
        y_out = yh_rows[0:TR, TT * D:2 * TT * D].rearrange("p (j n) -> p j n", j=TT)
        assert max(end_late, end_ffn) <= nc.sbuf_usable_end, (end_late, end_ffn, nc.sbuf_usable_end)

        def yg(k, t):
            if k == 1:
                return yh_rows[:, t * D:(t + 1) * D]
            n = B * S // 2 // D
            half = (act_hi, act_lo)[t // (KT * n)]
            return half[:, t // n % KT, t % n * D:(t % n + 1) * D].bitcast(F32)

        bank = [psum(f"bank{i}", [P, 512]) for i in range(2)]
        score = [psum(f"score{i}", [P, 1024]) for i in range(2)]
        bank_p = [psum(f"bank_p{i}", [P, 512]) for i in range(2)]
        banks = [bank[0][:], bank[1][:], score[0][:, 0:512], score[0][:, 512:], score[1][:, 0:512], score[1][:, 512:],
                 bank_p[0][:], bank_p[1][:]]

        x_first, x_rest, small_in, rows_in, zero_out = sem("x_first"), sem("x_rest"), sem("small_in"), sem("rows_in"), sem("zero_out")
        wk_in, wa_in, ctx_in, ctx_all_in = sem("wk_in"), sem("wa_in"), sem("ctx_in"), sem("ctx_all_in")
        v_out, v_pad = sem("v_out"), sem("v_pad")
        v_in = [sem(f"v_in{i}") for i in range(KT)]
        raw_in = [sem(f"raw_in{i}") for i in range(9)]
        consts, masked, zeros, v_zero, tanh_done = sem("consts"), sem("masked"), sem("zeros"), sem("v_zero"), sem("tanh_done")
        bias_done = sem("bias_done")
        stats_done, mv_done, eps_done, rstd_done, xn_ready, xnt_psum, xnt_ready = (
            sem(n) for n in ("stats_done", "mv_done", "eps_done", "rstd_done", "xn_ready", "xnt_psum", "xnt_ready"))
        stats2_done, mv2_done, eps2_done, rstd2_done, xn2_ready, xn2t_psum, stage_ready, hi_ready, lo_ready = (
            sem(n) for n in ("stats2_done", "mv2_done", "eps2_done", "rstd2_done", "xn2_ready", "xn2t_psum",
                             "stage_ready", "hi_ready", "lo_ready"))
        y_ready, stats3_done, mv3_done, eps3_done, rstd3_done, h_step = (
            sem(n) for n in ("y_ready", "stats3_done", "mv3_done", "eps3_done", "rstd3_done", "h_step"))
        logit_psum, logit_done = sem("logit_psum"), sem("logit_done")
        k_psum, kt_ready, kb_ready, q_psum, qt_ready = (sem(n) for n in ("k_psum", "kt_ready", "kb_ready", "q_psum", "qt_ready"))
        s_psum, max_done, sub_done, exp_done, sum_done, recip_done, norm_done = (
            sem(n) for n in ("s_psum", "max_done", "sub_done", "exp_done", "sum_done", "recip_done", "norm_done"))
        pt_psum, pt_ready, v_psum, v_ready, pv_psum, ot_ready, o_psum, x_new = (
            sem(n) for n in ("pt_psum", "pt_ready", "v_psum", "v_ready", "pv_psum", "ot_ready", "o_psum", "x_new"))
        x_ffn, xb_done = sem("x_ffn"), sem("xb_done")
        hi13, lo13, hi2, lo2, lo2_first = sem("hi13"), sem("lo13"), sem("hi2"), sem("lo2"), sem("lo2_first")
        gu_psum, silu_done, gu_free, hid_hi_done, hid_ready, tail_zero = (
            sem(n) for n in ("gu_psum", "silu_done", "gu_free", "hid_hi_done", "hid_ready", "tail_zero"))
        y0_psum, y0_done, y0_first = sem("y0_psum"), sem("y0_done"), sem("y0_first")
        ys_psum, ys_done = sem("ys_psum"), sem("ys_done")
        xe_load, xet_psum, xe_hi_done, xe_ready = sem("xe_load"), sem("xet_psum"), sem("xe_hi_done"), sem("xe_ready")
        yr_psum, yr_copied, y_stored = sem("yr_psum"), sem("yr_copied"), sem("y_stored")
        choice, route, e_done, pos_psum = sem("choice"), sem("route"), sem("e_done"), sem("pos_psum")
        puts_ready, slots_ready = sem("puts_ready"), sem("slots_ready")
        scattered, rows_kept = sem("scattered"), sem("rows_kept")
        gathered = [sem(f"gathered{i}") for i in range(4)]
        added, final, stored = sem("added"), sem("final"), sem("stored")

        def staged(layer, g):
            return g + 1 - layer

        HID_FREE = 2

        def hid_count(n):
            return n + HID_FREE + 1

        PIECES0 = M0 * E0
        SHARED_CHUNKS = B * S // PIECE
        EARLY = SHARED_CHUNKS // 2
        GU_SHARED = M0 * E0
        GU_ROUTED = GU_SHARED + FT * EARLY
        GU_LATE = GU_ROUTED + 2 * FT * E1
        STREAM = E1 + 2

        assert SLOTS * D % (P * B) == 0 and SLOTS * D // P // B <= B * HALVES * D

        def mm3(o, a_hi, a_lo, b_hi, b_lo, start, stop):
            nc.tensor.matmul(o, a_hi, b_hi, start=start, stop=False)
            nc.tensor.matmul(o, a_hi, b_lo, start=False, stop=False)
            return nc.tensor.matmul(o, a_lo, b_hi, start=False, stop=stop)

        def piece13_slot_load(x1, f):
            return E0 + (2 * x1 if f < 4 else x1) + 1

        def piece2_slot_load(x1, j):
            return E0 + 2 * x1 + 2

        def settle(eng):
            eng.wait_ge(consts, 1)

        def by_row(p):
            return p[:, 0:SC].rearrange("p (n h) -> p n h", h=HT)

        block = scope.enter_context(nc.Block())

        @block.sync
        def _(sp):
            def matrix(layer, w):
                return sp.dma_start(wa[:, :, w, :], attn_w[layer, :, :, w, :].rearrange("k p n -> p k n"))

            def place_values(b, g):
                sp.wait_ge(v_ready, g + 1)
                v_g = v_d[bass.ds(g, 1), :, :].rearrange("a k n -> (a k) n")
                sp.dma_start(v_g[0:KV, :], v_rows[0:KV, bass.ds(b % 2, 1), :].rearrange("p a d -> p (a d)")).then_inc(v_out, 16)
                sp.wait_ge(v_out, 16 * g + 16)
                for dt in range(KT):
                    if not isinstance(g, int) or g > 0:
                        sp.wait_ge(pv_psum, KT * g - KT + 1 + dt)
                    for h in range(HT):
                        at = (dt * HT + h) * HD
                        sp.dma_start(v_blk[h:P:HT, dt * PT:(dt + 1) * PT, h * HD:(h + 1) * HD],
                                     v_g[:, at:at + HD].rearrange("(t k) d -> k t d", t=PT)).then_inc(v_in[dt], 16)

            def load_ctx(b):
                sp.dma_start(ctx_b[:], ctx_t[:, :, b, :].rearrange("k p n -> p k n")).then_inc(ctx_in, 16)

            zero_at = xe.rearrange("s d -> (s d)").rearrange("(p n) -> p n", p=P)
            zero_w = SLOTS * D // P // B

            def zero_slots(b):
                sp.dma_start(zero_at[:, bass.ds(b * zero_w, zero_w)], yh_rows[:, 0:zero_w]).then_inc(zero_out, 16)

            def first_pieces(layer, b):
                if layer == 0:
                    zero_slots(b)
                    if isinstance(b, int) and b == 0:
                        for m in range(M0 + 3):
                            sp.dma_start(raw[:, m, :], w_first[0, m]).then_inc(raw_in[m], 16)

            def attention_loads(layer):
                if layer == 1:
                    load_ctx(0)
                else:
                    sp.wait_ge(zeros, 1)
                if layer == 0:
                    sp.wait_ge(k_psum, 1)
                    matrix(1, K).then_inc(wk_in, 16)
                    sp.dma_start(v_d[:, KV:, :], yh_rows[0:2 * B, 0:(KP - KV) * D].rearrange("g (k n) -> g k n", k=KP - KV)).then_inc(v_pad, 16)
                    sp.wait_ge(v_pad, 16)
                sp.wait_ge(v_psum, B * layer + 1)
                load_ctx(1)
                sp.wait_ge(v_zero, layer + 1)
                place_values(0, B * layer)
                first_pieces(layer, 0)
                with sp.Fori(1, B - 1) as b:
                    sp.wait_ge(v_psum, b + B * layer + 1)
                    load_ctx(b + 1)
                    place_values(b, b + B * layer)
                    first_pieces(layer, b)
                place_values(B - 1, B * layer + B - 1)
                first_pieces(layer, B - 1)

            sp.dma_start(xs[:, 0:HALVES, :], x[:, 0:HALVES, :]).then_inc(x_first, 16)
            sp.dma_start(gate[:], gates).then_inc(small_in, 16)
            sp.dma_start(bias_cols[:], cols).then_inc(small_in, 16)
            matrix(0, K).then_inc(wk_in, 16)
            sp.dma_start(ctx_all[:], ctx_t.rearrange("k p b n -> p k (b n)")).then_inc(ctx_all_in, 16)
            for w in (Q, V, O):
                matrix(0, w).then_inc(wa_in, 16)
            load_ctx(0)
            sp.dma_start(row[:], rows).then_inc(rows_in, 16)
            sp.dma_start(rw[:], router_w).then_inc(rows_in, 16)
            sp.dma_start(xs[:, HALVES:, :], x[:, HALVES:, :]).then_inc(x_rest, 16)
            attention_loads(0)

            def gate_up_load(e, m):
                sp.wait_ge(lo13, M0 * (e - 1) + m + 1)
                sp.dma_start(raw[:, m, :], w_first[e, m]).then_inc(raw_in[m], 16)

            def down_load(e, j):
                if j == 0:
                    sp.wait_ge(lo2, e)
                else:
                    sp.wait_ge(lo2_first, 2 * (e - 1) + j)
                sp.dma_start(raw[:, M0 + j, :], w_first[e, M0 + j]).then_inc(raw_in[M0 + j], 16)

            for m in range(M0):
                gate_up_load(1, m)
            with sp.Fori(0, E0 - 2) as e:
                for m in range(M0):
                    if m < 3:
                        down_load(e + 1, m)
                    gate_up_load(e + 2, m)
            for j in range(3):
                down_load(E0 - 1, j)
            for m in range(M0):
                sp.wait_ge(lo13, M0 * (E0 - 1) + m + 1)
                sp.dma_start(raw[:, m, :], w_second[0, m]).then_inc(raw_in[m], 16)
            sp.wait_ge(x_new, B)
            for w in (Q, V, O):
                matrix(1, w).then_inc(wa_in, 16)
            sp.wait_ge(lo2, E0)
            sp.wait_ge(lo2_first, 2 * E0)
            for f in range(M0, FT):
                sp.dma_start(raw[:, f, :], w_second[0, f]).then_inc(raw_in[f], 16)
            attention_loads(1)

            def weights(x1):
                return x1 % (STREAM - 1) if isinstance(x1, int) else x1

            def pieces2(x1):
                for j in range(4):
                    sp.wait_ge(lo13, PIECES0 + FT * x1 + j + 1)
                    sp.dma_start(raw[:, j, :], w_second[weights(x1), FT + j]).then_inc(raw_in[j], 16)

            def pieces13(x1):
                for f in range(FT):
                    if f < 4:
                        sp.wait_ge(lo2, E0 + 4 * (x1 - 1) + f + 1)
                    else:
                        sp.wait_ge(lo13, PIECES0 + FT * (x1 - 1) + f + 1)
                    sp.dma_start(raw[:, f, :], w_second[weights(x1), f]).then_inc(raw_in[f], 16)

            def load_slots(e):
                rows_e = xe[bass.ds(e * CAP, CAP), :] if not isinstance(e, int) else xe[e * CAP:(e + 1) * CAP, :]
                sp.dma_start(xe_in, rows_e.rearrange("(j p) d -> p j d", p=TR)).then_inc(xe_load, 16)

            def store_outputs(e):
                sp.wait_ge(yr_copied, TT * e + TT)
                rows_e = ye[bass.ds(e * CAP, CAP), :] if not isinstance(e, int) else ye[e * CAP:(e + 1) * CAP, :]
                sp.dma_start(rows_e.rearrange("(j p) d -> p j d", p=TR), y_out).then_inc(y_stored, 16)

            pieces2(0)
            pieces13(1)
            sp.wait_ge(scattered, 16 * 2 * T)
            load_slots(0)
            pieces2(1)
            sp.wait_ge(xet_psum, 4)
            load_slots(1)

            def expert_loads(e, slots):
                pieces13(e + 2)
                pieces2(e + 2)
                if slots:
                    sp.wait_ge(xet_psum, 4 * e + 8)
                    load_slots(e + 2)
                store_outputs(e)

            with sp.Fori(0, E1 - 2) as e:
                expert_loads(e, True)
            expert_loads(E1 - 2, False)
            expert_loads(E1 - 1, False)
            for c in range(3):
                sp.wait_ge(final, 4 * c + 4)
                sp.dma_start(out[:, 4 * c:4 * c + 4, :], xs[:, 4 * c:4 * c + 4, :]).then_inc(stored, 16)
            sp.wait_ge(ys_done, T - 1)
            sp.dma_start(out[:, T - 4:T - 1, :], xs[:, T - 4:T - 1, :]).then_inc(stored, 16)
            sp.wait_ge(ys_done, T)
            sp.dma_start(out[:, T - 1:, :], xs[:, T - 1:, :]).then_inc(stored, 16)
            sp.wait_ge(stored, 5 * 16)

        @block.tensor
        def _(pe):
            def transpose4(o, src):
                for kt in range(KT):
                    for h in range(HALVES):
                        last = nc.tensor.transpose(o[:, kt * S + h * P:kt * S + (h + 1) * P],
                                                   src[:, h, kt * P:(kt + 1) * P], ident[:])
                return last

            def keys(layer):
                pe.wait_ge(wk_in, 16 * (layer + 1))
                pe.wait_ge(ctx_all_in, 16)
                for dt in range(KT):
                    for hf in range(2):
                        w = B * KV // 2
                        for kt in range(KT):
                            last = nc.tensor.matmul(score[dt][:, hf * 512:hf * 512 + w], wa[:, kt, K, dt * P:(dt + 1) * P],
                                                    ctx_all[:, kt, hf * w:(hf + 1) * w], start=kt == 0, stop=kt == KT - 1)
                last.then_inc(k_psum, 1)

            def norm_t(g):
                pe.wait_ge(xn_ready, g + 1)
                transpose4(bank[0], xn).then_inc(xnt_psum, 1)

            def norm2_t(g):
                pe.wait_ge(xn2_ready, g + 1)
                transpose4(bank[0], xn2).then_inc(xn2t_psum, 1)

            def route_logits(g, b):
                pe.wait_ge(stage_ready, staged(1, g))
                for h in range(HALVES):
                    for kt in range(KT):
                        last = nc.tensor.matmul(bank[0][:, h * 8:h * 8 + 8], stage[:, kt, h * P:(h + 1) * P], rw[:, kt, :],
                                                start=kt == 0, stop=kt == KT - 1)
                last.then_inc(logit_psum, 1)

            def scores(g, b, u, first):
                dt, qt = divmod(u, 2)
                if not (first and u < 2):
                    pe.wait_ge(sub_done, 4 * g + u - 1)
                for c in range(0, SC, 512):
                    w = min(512, SC - c)
                    last = nc.tensor.matmul(score[u % 2][:, c:c + w], q_t[:, dt, qt * P:(qt + 1) * P],
                                            kb[:, b % 2, dt, c:c + w], start=True, stop=True)
                last.then_inc(s_psum, 1)

            def prob_transposes(g, u):
                pe.wait_ge(norm_done, 4 * g + u + 1)
                if not (isinstance(g, int) and g == 0 and u == 0):
                    pe.wait_ge(pt_ready, 8 * g + 2 * u)
                for grp, tiles in enumerate(((0, 1, 2), (3, 4))):
                    for i, j in enumerate(tiles):
                        last = nc.tensor.transpose(bank_p[grp][:, i * P:(i + 1) * P], prob[u][:, j * P:(j + 1) * P], ident[:])
                    last.then_inc(pt_psum, 1)

            def weighted_values(g, dt):
                pe.wait_ge(pt_ready, 8 * g + 4 * dt + 4)
                pe.wait_ge(v_in[dt], 16 * HT * (g + 1))
                for j in range(PT):
                    last = nc.tensor.matmul(bank[1][:, dt * S:(dt + 1) * S], v_blk[:, dt * PT + j, :],
                                            prob_t[:, dt * PT + j, :], start=j == 0, stop=j == PT - 1)
                last.then_inc(pv_psum, 1)

            def project_out(g):
                pe.wait_ge(ot_ready, g + 1)
                for qt in range(HALVES):
                    for dt in range(KT):
                        last = nc.tensor.matmul(bank[1][:, qt * D:(qt + 1) * D], o_t[:, dt, qt * P:(qt + 1) * P],
                                                wa[:, dt, O, :], start=dt == 0, stop=dt == KT - 1)
                last.then_inc(o_psum, 1)

            def queries(g):
                pe.wait_ge(xnt_ready, g + 1)
                for dt in range(KT):
                    for kt in range(KT):
                        last = nc.tensor.matmul(bank[0][:, dt * S:(dt + 1) * S], wa[:, kt, Q, dt * P:(dt + 1) * P],
                                                xn_t[:, kt, :], start=kt == 0, stop=kt == KT - 1)
                last.then_inc(q_psum, 1)

            def values(g):
                pe.wait_ge(ctx_in, 16 * (g + 1))
                for kt in range(KT):
                    last = nc.tensor.matmul(bank[1][0:KV, 0:D], ctx_b[:, kt, :], wa[:, kt, V, :], start=kt == 0, stop=kt == KT - 1)
                last.then_inc(v_psum, 1)

            def attention_step(layer, b, n):
                g = b + B * layer
                start = layer == 0 and n == 0
                settled = n is None or n >= 2
                pe.wait_ge(qt_ready, KT * g + 1)
                pe.wait_ge(kb_ready, g + 1)
                scores(g, b, 0, start)
                pe.wait_ge(qt_ready, KT * g + KT)
                pe.wait_ge(v_ready, g + 1)
                if n != 0:
                    weighted_values(g - 1, 0)
                    prob_transposes(g - 1, 2)
                scores(g, b, 1, start)
                if n != 0:
                    prob_transposes(g - 1, 3)
                else:
                    values(g + 1)
                if settled:
                    norm2_t(g - 2)
                scores(g, b, 2, start)
                if n != 0:
                    weighted_values(g - 1, 1)
                prob_transposes(g, 0)
                if layer == 1 and settled:
                    route_logits(g - 2, b - 2)
                scores(g, b, 3, start)
                if n != 0:
                    project_out(g - 1)
                if n != B - 1:
                    if settled:
                        pe.wait_ge(stage_ready, staged(layer, g - 2))
                        if layer == 1:
                            pe.wait_ge(logit_done, b - 1)
                    norm_t(g + 1)
                prob_transposes(g, 1)
                if n != B - 1:
                    queries(g + 1)
                    if n != 0:
                        pe.wait_ge(x_new, g)
                        values(g + 1)

            def attention(layer):
                if layer == 0:
                    keys(0)
                if layer == 1:
                    pe.wait_ge(wa_in, 16 * 3 * (layer + 1))
                    pe.wait_ge(x_new, B)
                    values(B * layer)
                norm_t(B * layer)
                if layer == 0:
                    pe.wait_ge(wa_in, 16 * 3 * (layer + 1))
                queries(B * layer)
                if layer == 0:
                    values(B * layer)
                attention_step(layer, 0, 0)
                attention_step(layer, 1, 1)
                with pe.Fori(2, B - 1) as b:
                    attention_step(layer, b, None)
                attention_step(layer, B - 1, B - 1)
                g = B * layer + B - 1
                prob_transposes(g, 2)
                pe.wait_ge(x_new, g)
                weighted_values(g, 0)
                if layer == 1:
                    shared_weights(0)
                    pe.wait_ge(lo_ready, B + PIECE // S)
                    pe.wait_ge(hi_ready, B + PIECE // S)
                    shared_gate_up(0, 0)
                pe.wait_ge(stage_ready, staged(layer, g - 2))
                if layer == 1:
                    pe.wait_ge(logit_done, B - 2)
                norm2_t(g - 1)
                prob_transposes(g, 3)
                if layer == 1:
                    route_logits(g - 1, B - 2)
                weighted_values(g, 1)
                project_out(g)
                if layer == 0:
                    keys(1)
                else:
                    for f in range(1, 3):
                        shared_gate_up(0, f)
                pe.wait_ge(stage_ready, staged(layer, g - 1))
                if layer == 1:
                    pe.wait_ge(logit_done, B - 1)
                norm2_t(g)
                if layer == 1:
                    shared_gate_up(0, 3)
                    route_logits(g, B - 1)

            def first_layer(e):
                for m in range(M0):
                    pe.wait_ge(hi13, M0 * e + m + 1)
                    pe.wait_ge(lo13, M0 * e + m + 1)
                    pe.wait_ge(gu_free, M0 * e + m + 1)
                    for gu in range(1 if m == 0 else 2):
                        for kt in range(KT):
                            c = kt * (P if m == 0 else 2 * P) + gu * P
                            rhs = [a[:, kt, :].rearrange("p (b s) -> p b s", s=S)[:, :, bass.ds(e * C0, C0)] for a in (act_hi, act_lo)]
                            last = mm3(banks[2 + m % 3][:, gu * S:(gu + 1) * S], w_hi[:, m, c:c + P], w_lo[:, m, c:c + P],
                                       rhs[0], rhs[1], kt == 0, kt == KT - 1)
                    last.then_inc(gu_psum, 1)
                pe.wait_ge(y0_done, 2 * e + 2)
                for k in range(M0):
                    j, c = k // 2, k % 2 * D
                    pe.wait_ge(hid_ready, hid_count(M0 * e + k))
                    if k % 2 == 0:
                        pe.wait_ge(hi2, 3 * e + j + 1)
                        if j == 0:
                            pe.wait_ge(lo2, e + 1)
                        else:
                            pe.wait_ge(lo2_first, 2 * e + j)
                    for h in range(HALVES):
                        last = mm3(bank_p[h][:, 0:D], first_hid_hi[:, k, h * P:(h + 1) * P], first_hid_lo[:, k, h * P:(h + 1) * P],
                                   w_hi[:, M0 + j, c:c + D], w_lo[:, M0 + j, c:c + D], k == 0, k == M0 - 1)
                last.then_inc(y0_psum, 1)

            def gate_up(n, f, width, rhs_hi, rhs_lo):
                for gu in range(2):
                    for kt in range(KT):
                        c = kt * 2 * P + gu * P
                        last = mm3(banks[2 + 2 * (f % 2) + gu][:, 0:width], w_hi[:, f, c:c + P], w_lo[:, f, c:c + P],
                                   rhs_hi[kt], rhs_lo[kt], kt == 0, kt == KT - 1)
                last.then_inc(gu_psum, 1)

            def down(o, at, width, n=None):
                for f in range(FT):
                    j, c = FT + f // 2, f % 2 * D
                    if n is not None:
                        pe.wait_ge(hid_ready, hid_count(n + f))
                    last = mm3(o, hid_hi[:, f, at:at + width], hid_lo[:, f, at:at + width], w_hi[:, j, c:c + D], w_lo[:, j, c:c + D],
                               f == 0, f == FT - 1)
                return last

            def shared_base(c):
                return GU_SHARED + FT * c if c < EARLY else GU_LATE + FT * (c - EARLY)

            def shared_gate_up(c, f):
                n = shared_base(c) + f
                pe.wait_ge(gu_free, n + 2)
                gate_up(n, f, PIECE, *([a[:, kt, c * PIECE:(c + 1) * PIECE] for kt in range(KT)] for a in (act_hi, act_lo)))

            def shared_down(c, j):
                if c == EARLY and j == 0:
                    pe.wait_ge(yr_copied, TT * E1)
                if 4 * c + j >= 2:
                    pe.wait_ge(ys_done, 4 * c + j - 1)
                down(bank_p[j % 2][:, 0:D], j * P, P, shared_base(c) if j == 0 else None).then_inc(ys_psum, 1)

            def shared_weights(entry):
                pe.wait_ge(hi13, PIECES0 + FT * (entry + 1))
                pe.wait_ge(lo13, PIECES0 + FT * (entry + 1))

            def shared_down_weights(entry):
                pe.wait_ge(hi2, 3 * E0 + 4 * (entry + 1))
                pe.wait_ge(lo2, E0 + 4 * (entry + 1))

            def shared(c):
                for f in range(FT):
                    shared_gate_up(c, f)
                shared_down_weights(0 if c < EARLY else STREAM - 1)
                for j in range(4):
                    shared_down(c, j)

            def slots_t(e, hf):
                pe.wait_ge(xe_load, 16 * (e + 1))
                for kt in range(KT):
                    n = 4 * e + KT * hf + kt
                    if not isinstance(e, int) or n >= KT:
                        pe.wait_ge(xe_ready, n - KT + 1)
                    for j in range(3):
                        last = nc.tensor.transpose(bank[kt][:, j * TR:(j + 1) * TR],
                                                   xe_in[:, 3 * hf + j, kt * P:(kt + 1) * P], ident[0:TR, 0:TR])
                    last.then_inc(xet_psum, 1)

            def expert(e, last_one):
                for hf in range(2):
                    pe.wait_ge(xe_ready, 4 * e + KT * hf + KT)
                    for f in range(FT):
                        n = GU_ROUTED + 2 * FT * e + FT * hf + f
                        if hf == 0:
                            pe.wait_ge(hi13, PIECES0 + FT * (e + 1) + f + 1)
                            pe.wait_ge(lo13, PIECES0 + FT * (e + 1) + f + 1)
                        pe.wait_ge(gu_free, n + 2)
                        gate_up(n, f, HC, *([a[:, kt, hf * HC:(hf + 1) * HC] for kt in range(KT)] for a in (xe_hi, xe_lo)))
                        if hf == 1 and f == FT // 2 and not last_one:
                            slots_t(e + 1, 0)
                if not last_one:
                    slots_t(e + 1, 1)
                pe.wait_ge(hi2, 3 * E0 + 4 * (e + 1) + 4)
                pe.wait_ge(lo2, E0 + 4 * (e + 1) + 4)
                for j in range(TT):
                    pe.wait_ge(hid_ready, hid_count(GU_ROUTED + 2 * FT * e + FT * (j // 3) + FT - 1))
                    if not (isinstance(e, int) and e == 0 and j < 2):
                        pe.wait_ge(yr_copied, TT * e + j - 1)
                    down(bank_p[j % 2][0:TR, 0:D], j * TR, TR).then_inc(yr_psum, 1)

            pe.wait_ge(masked, 2)
            attention(0)
            pe.wait_ge(lo_ready, B)
            pe.wait_ge(hi_ready, B)
            pe.wait_ge(kt_ready, 2)
            with pe.Fori(0, E0) as e:
                first_layer(e)
            attention(1)
            for f in range(4, FT):
                shared_gate_up(0, f)
            pe.wait_ge(route, 1)
            pick_v = pick[:].rearrange("p c t e -> p (c t e)")
            nc.tensor.matmul(bank[0][:, 0:2 * T * E1], before[:], pick_v, start=True, stop=False)
            nc.tensor.matmul(bank[0][:, 0:2 * T * E1], ones[:], cum[1][:].rearrange("p g e -> p (g e)"),
                             start=False, stop=True).then_inc(pos_psum, 1)
            shared_down_weights(0)
            for j in range(4):
                shared_down(0, j)
            pe.wait_ge(lo_ready, 2 * B)
            pe.wait_ge(hi_ready, 2 * B)
            shared(1)
            slots_t(0, 0)
            slots_t(0, 1)
            pe.wait_ge(ys_done, 4 * EARLY)
            expert(0, False)
            with pe.Fori(1, E1 - 1) as e:
                expert(e, False)
            expert(E1 - 1, True)
            shared_weights(STREAM - 1)
            shared(2)
            shared(3)

        @block.scalar
        def _(act):
            def split13(slot_f, n_load, at, width=PIECE):
                act.wait_ge(raw_in[slot_f], 16 * n_load)
                nc.scalar.activation(w_hi[:, at, 0:width], raw[:, slot_f, 0:width], ACT.Copy).then_inc(hi13, 1)

            def split2(slot_j, n_load, at):
                act.wait_ge(raw_in[slot_j], 16 * n_load)
                nc.scalar.activation(w_hi[:, at, :], raw[:, slot_j, :], ACT.Copy).then_inc(hi2, 1)

            def keys():
                act.wait_ge(k_psum, 1)
                w = B * KV // 2
                for dt in range(KT):
                    last = nc.scalar.activation(k_t[:, dt, :].rearrange("p (h n) -> p h n", h=2),
                                                score[dt][:].rearrange("p (h n) -> p h n", h=2)[:, :, 0:w], ACT.Identity,
                                                bias=bias_cols[:, 0, 1, dt:dt + 1])
                last.then_inc(kt_ready, 1)

            def norm_t(g):
                act.wait_ge(xnt_psum, g + 1)
                nc.scalar.activation(xn_t[:].rearrange("p k s -> p (k s)"), bank[0][:], ACT.Copy).then_inc(xnt_ready, 1)

            def norm2_t(g, first):
                act.wait_ge(xn2t_psum, g + 1)
                if not first:
                    act.wait_ge(lo_ready, g)
                    act.wait_ge(hi_ready, g)
                nc.scalar.activation(stage[:].rearrange("p k s -> p (k s)"), bank[0][:], ACT.Copy).then_inc(stage_ready, 1)

            def high(layer, g, b):
                act.wait_ge(stage_ready, staged(layer, g))
                nc.scalar.activation(act_hi[:, :, bass.ds(b * S, S)], stage[:], ACT.Copy).then_inc(hi_ready, 1)

            def queries(layer, g):
                act.wait_ge(q_psum, g + 1)
                for dt in range(KT):
                    nc.scalar.activation(q_t[:, dt, :], bank[0][:, dt * S:(dt + 1) * S], ACT.Identity,
                                         bias=bias_cols[:, layer, 0, dt:dt + 1]).then_inc(qt_ready, 1)

            def exps(g, u):
                act.wait_ge(sub_done, 4 * g + u + 1)
                pv = prob[u][:, 0:SC]
                nc.scalar.activation(pv, pv, ACT.Exp).then_inc(exp_done, 1)

            def probs_t(g, u):
                dt, qt = divmod(u, 2)
                for grp, (j, n) in enumerate(((0, 3), (3, 2))):
                    act.wait_ge(pt_psum, 8 * g + 2 * u + grp + 1)
                    at = dt * PT + j
                    nc.scalar.activation(prob_t[:, at:at + n, qt * P:(qt + 1) * P],
                                         bank_p[grp][:, 0:n * P].rearrange("p (j n) -> p j n", j=n), ACT.Copy).then_inc(pt_ready, 1)

            def out_t(layer, g):
                act.wait_ge(pv_psum, KT * g + KT)
                for dt in range(KT):
                    last = nc.scalar.activation(o_t[:, dt, :], bank[1][:, dt * S:(dt + 1) * S], ACT.Identity,
                                                bias=bias_cols[:, layer, 2, dt:dt + 1])
                last.then_inc(ot_ready, 1)

            def values(layer, b, n):
                g = b + B * layer
                act.wait_ge(v_psum, g + 1)
                if n is None or n >= 2 or layer == 1:
                    act.wait_ge(v_out, 16 * (g - 1))
                nc.scalar.activation(v_rows[0:KV, bass.ds(b % 2, 1), :].rearrange("p a d -> p (a d)"), bank[1][0:KV, 0:D],
                                     ACT.Copy).then_inc(v_ready, 1)

            def attention_step(layer, b, n):
                g = b + B * layer
                settled = n is None or n >= 2
                exps(g, 0)
                if n != 0:
                    probs_t(g - 1, 2)
                    probs_t(g - 1, 3)
                if layer == 1 and settled:
                    keep_rows(b - 2, g - 2)
                if settled:
                    norm2_t(g - 2, layer == 0 and n == 2)
                exps(g, 1)
                if settled:
                    high(layer, g - 2, b - 2)
                if n != 0:
                    out_t(layer, g - 1)
                else:
                    values(layer, b + 1, n + 1)
                exps(g, 2)
                probs_t(g, 0)
                if layer == 1 and n in (0, 1):
                    split13(M0 + n, piece13_slot_load(0, M0 + n), M0 + n)
                if layer == 0 and settled:
                    p = bass.ds(b - 2, 1)
                    nc.scalar.activation(w_hi[:, p, :], raw[:, p, :], ACT.Copy).then_inc(hi13, 1)
                if n != B - 1:
                    norm_t(g + 1)
                if n == B - 1:
                    probs_t(g, 1)
                    exps(g, 3)
                    warm_up(ACT.Silu)
                else:
                    exps(g, 3)
                    probs_t(g, 1)
                if n != B - 1:
                    queries(layer, g + 1)
                    if n != 0:
                        values(layer, b + 1, None if n is None else n + 1)
                elif layer == 1:
                    for j in range(4):
                        split2(j, piece2_slot_load(0, j), FT + j)

            def keep_rows(b, g):
                act.wait_ge(xn2_ready, g + 1)
                nc.scalar.activation(yh[:, bass.ds(b, 1), :].rearrange("p a n -> p (a n)"),
                                     xn2[:].rearrange("p h d -> p (h d)"), ACT.Copy).then_inc(rows_kept, 1)

            def attention(layer):
                warm_up(ACT.Exp)
                if layer == 0:
                    keys()
                if layer == 1:
                    values(layer, 0, 0)
                norm_t(B * layer)
                queries(layer, B * layer)
                if layer == 0:
                    values(layer, 0, 0)
                if layer == 1:
                    act.wait_ge(y0_psum, E0)
                attention_step(layer, 0, 0)
                attention_step(layer, 1, 1)
                if layer == 0:
                    for m in range(M0):
                        act.wait_ge(raw_in[m], 16)
                    attention_step(layer, 2, 2)
                with act.Fori(3 if layer == 0 else 2, B - 1) as b:
                    attention_step(layer, b, None)
                attention_step(layer, B - 1, B - 1)
                g = B * layer + B - 1
                probs_t(g, 2)
                if layer == 1:
                    keep_rows(B - 2, g - 1)
                norm2_t(g - 1, False)
                probs_t(g, 3)
                high(layer, g - 1, B - 2)
                out_t(layer, g)
                if layer == 0:
                    act.wait_ge(xn2t_psum, B)
                    nc.scalar.activation(act_hi[:, :, (B - 1) * S:], bank[0][:].rearrange("p (k s) -> p k s", k=KT), ACT.Copy).then_inc(hi_ready, 1)
                else:
                    for f in range(3):
                        shared_silu(0, f)
                    keep_rows(B - 1, g)
                    norm2_t(g, False)
                    high(layer, g, B - 1)

            def silu_of(n, buf, src, rows_n, width):
                act.wait_ge(gu_psum, n + 1)
                act.wait_ge(gu_free, n + 2)
                nc.scalar.activation(silu[0:rows_n, buf, 0:width], src, ACT.Silu).then_inc(silu_done, 1)

            def first_layer(e, i, part):
                for m in range(M0):
                    src = banks[2 + m % 3]
                    silu_of(M0 * e + m, m % 2, src[0:64, 0:S] if m == 0 else src[:, 0:S], 64 if m == 0 else P, S)
                    if m < 3:
                        split2(M0 + m, e + 1, M0 + m)
                    split13(m, e + 2, m)
                act.wait_ge(y0_psum, e + 1)
                for j in range(B // HALVES):
                    last = nc.scalar.activation(
                        yh[i * C0:(i + 1) * C0, j, bass.ds(part * D, D)], bank_p[0][j * C0:(j + 1) * C0, 0:D],
                        ACT.Identity, scale=tanh_gate[j * C0:(j + 1) * C0, 2:3])
                    if j == 0:
                        last.then_inc(y0_first, 1)
                last.then_inc(y0_done, 1)

            def shared_silu(c, f):
                base = GU_SHARED + FT * c if c < EARLY else GU_LATE + FT * (c - EARLY)
                silu_of(base + f, f % 2, banks[2 + 2 * (f % 2)], P, PIECE)

            def shared(c):
                for f in range(FT):
                    shared_silu(c, f)
                    if c == EARLY - 1:
                        split13(f, piece13_slot_load(1, f), f)
                    if c == EARLY and f < 4:
                        split2(f, piece2_slot_load(STREAM - 1, f), FT + f)

            def expert(e, last_one):
                for hf in range(2):
                    for f in range(FT):
                        silu_of(GU_ROUTED + 2 * FT * e + FT * hf + f, f % 2, banks[2 + 2 * (f % 2)][:, 0:HC], P, HC)
                        if hf == 0 and f < 4:
                            split2(f, piece2_slot_load(e + 1, f), FT + f)
                        if hf == 1:
                            split13(f, piece13_slot_load(e + 2, f), f)
                        if hf == 1 and f == FT // 2 and not last_one:
                            slots_hi(e + 1, 0)
                if not last_one:
                    slots_hi(e + 1, 1)

            def slots_hi(e, hf):
                for kt in range(KT):
                    act.wait_ge(xet_psum, 4 * e + KT * hf + kt + 1)
                    nc.scalar.activation(xe_hi[:, kt, hf * HC:(hf + 1) * HC], bank[kt][:, 0:HC], ACT.Copy).then_inc(xe_hi_done, 1)

            def warm_up(function):
                nc.scalar.activation(warm[:], gate[:, 0:1], function)

            act.wait_ge(small_in, 32)
            nc.scalar.activation(tanh_gate[:], gate[:], ACT.Tanh).then_inc(tanh_done, 1)
            attention(0)
            act.wait_ge(zero_out, 16 * B)
            per = E0 // HALVES
            with act.Fori(0, HALVES) as part:
                for i in range(per):
                    first_layer(per * part + i, i, part)
            attention(1)
            for f in range(3, FT):
                shared_silu(0, f)
            act.wait_ge(e_done, 1)
            nc.scalar.activation(e_dif[:], e_dif[:], ACT.Exp).then_inc(e_done, 1)
            shared(1)
            slots_hi(0, 0)
            slots_hi(0, 1)
            with act.Fori(0, E1 - 1) as e:
                expert(e, False)
            expert(E1 - 1, True)
            shared(2)
            shared(3)

        @block.vector
        def _(dve):
            def carry(n):
                if not isinstance(n, int):
                    nc.vector.memset(waited[:], 0.0)

            def row_stats(src, st, st_sem, m, m_sem, g):
                for h in range(HALVES):
                    last = nc.vector.bn_stats(st[:, h, :], src(h))
                last.then_inc(st_sem, 1)
                dve.wait_ge(st_sem, g + 1)
                carry(g)
                for h in range(HALVES):
                    last = nc.vector.bn_aggr(m[:, h, :], st[:, h, :])
                last.then_inc(m_sem, 1)

            def xs_row(b, h):
                return xs[:, bass.ds(b * HALVES + h, 1), :].rearrange("p a d -> p (a d)")

            def norm_stats(layer, b, first):
                g = b + B * layer
                if layer == 0 and isinstance(b, int) and b < 2:
                    dve.wait_ge(x_rest if b else x_first, 16)
                if layer == 1:
                    dve.wait_ge(x_ffn, b + 1)
                if not first:
                    dve.wait_ge(xn_ready, g)
                carry(g)
                row_stats(lambda h: xs_row(b, h), stats, stats_done, mv, mv_done, g)

            def normalise(src, dst, m, r, r_sem, done, g):
                dve.wait_ge(r_sem, g + 1)
                for h in range(HALVES):
                    last = nc.vector.tensor_scalar(dst[:, h, :], src(h), m[:, h, 0:1], r[:, h:h + 1], ALU.subtract, ALU.mult)
                last.then_inc(done, 1)

            def norm(layer, b, first):
                g = b + B * layer
                if not first:
                    dve.wait_ge(xnt_psum, g)
                normalise(lambda h: xs_row(b, h), xn, mv, rstd, rstd_done, xn_ready, g)

            def norm2(layer, b, g, first):
                if not first:
                    dve.wait_ge(xn2t_psum, g)
                if layer == 1 and not (isinstance(b, int) and b == 0):
                    dve.wait_ge(rows_kept, b)
                normalise(lambda h: xs_row(b, h), xn2, mv2, rstd2, rstd2_done, xn2_ready if layer == 0 else y_ready, g)

            def norm3(b, g):
                dve.wait_ge(mv3_done, b + 1)
                for h in range(HALVES):
                    last = nc.vector.scalar_tensor_tensor(out=xn2[:, h, :], in0=xn2[:, h, :], scalar=mv3[:, h, 0:1], in1=row[:, 2, :],
                                                          op0=ALU.subtract, op1=ALU.mult)
                last.then_inc(h_step, 1)
                dve.wait_ge(rstd3_done, b + 1)
                dve.wait_ge(h_step, b + 1)
                for h in range(HALVES):
                    last = nc.vector.scalar_tensor_tensor(out=xn2[:, h, :], in0=xn2[:, h, :], scalar=rstd3[:, h:h + 1], in1=row[:, 3, :],
                                                          op0=ALU.mult, op1=ALU.add)
                last.then_inc(xn2_ready, 1)

            def of_heads(p):
                return p[:, 0:SC].rearrange("p (n h) -> p h n", h=HT)

            def max_sub(g, u, start):
                dve.wait_ge(s_psum, 4 * g + u + 1)
                nc.vector.tensor_reduce(mx[:, u], of_heads(score[u % 2]), AX_X, ALU.max).then_inc(max_done, 1)
                dve.wait_ge(max_done, 4 * g + u + 1)
                if not start:
                    dve.wait_ge(pt_psum, 8 * g - 8 + 2 * u + 2)
                nc.vector.tensor_tensor(by_row(prob[u]), by_row(score[u % 2]), mx[:, u].unsqueeze(1).to_broadcast([P, KV, HT]),
                                        ALU.subtract).then_inc(sub_done, 1)

            def sums(g, u):
                dve.wait_ge(exp_done, 4 * g + u + 1)
                nc.vector.tensor_reduce(total[:, u], of_heads(prob[u]), AX_X, ALU.add).then_inc(sum_done, 1)
                dve.wait_ge(sum_done, 4 * g + u + 1)
                nc.vector.reciprocal(recip[:, u], total[:, u]).then_inc(recip_done, 1)

            def add_attention(layer, b, g):
                dve.wait_ge(o_psum, g + 1)
                dve.wait_ge(xb_done, g + 1)
                two = xs[:, bass.ds(b * HALVES, HALVES), :].rearrange("p a d -> p (a d)")
                nc.vector.scalar_tensor_tensor(out=two, in0=bank[1][:], scalar=tanh_gate[:, layer:layer + 1], in1=two,
                                               op0=ALU.mult, op1=ALU.add).then_inc(x_new, 1)

            def norm2_stats(b, g, first):
                dve.wait_ge(x_new, g + 1)
                if not first:
                    dve.wait_ge(xn2_ready, g)
                carry(g)
                row_stats(lambda h: xs_row(b, h), stats2, stats2_done, mv2, mv2_done, g)

            def norm3_stats(b):
                dve.wait_ge(y_ready, b + 1)
                carry(b)
                row_stats(lambda h: xn2[:, h, :], stats3, stats3_done, mv3, mv3_done, b)

            def keep_logits(b):
                dve.wait_ge(logit_psum, b + 1)
                nc.vector.tensor_copy(logits[:, bass.ds(b * HALVES, HALVES), :],
                                      bank[0][:, 0:HALVES * 8].rearrange("p (h e) -> p h e", h=HALVES)).then_inc(logit_done, 1)

            def attention_step(layer, b, n):
                g = b + B * layer
                start = layer == 0 and n == 0
                settled = n is None or n >= 2
                more = n != B - 1
                max_sub(g, 0, start)
                if layer == 1 and settled:
                    norm3(b - 2, g - 2)
                if layer == 0 and more:
                    norm_stats(layer, b + 1, False)
                sums(g, 0)
                max_sub(g, 1, start)
                if layer == 1 and more and n != 0:
                    norm_stats(layer, b + 1, False)
                if layer == 0 and more:
                    norm(layer, b + 1, False)
                max_sub(g, 2, start)
                sums(g, 1)
                if layer == 1 and more and n != 0:
                    norm(layer, b + 1, False)
                if layer == 1 and settled:
                    keep_logits(b - 2)
                sums(g, 2)
                max_sub(g, 3, start)
                if n != 0:
                    add_attention(layer, b - 1, g - 1)
                    norm2_stats(b - 1, g - 1, layer == 0 and n == 1)
                sums(g, 3)
                if n != 0:
                    norm2(layer, b - 1, g - 1, layer == 0 and n == 1)
                    if layer == 1:
                        norm3_stats(b - 1)
                if layer == 1 and n == B - 1:
                    norm3(b - 1, g - 1)

            first_batch = xs[:, 0:HALVES, :].rearrange("p a d -> p (a d)")

            def clear_attention():
                for p in prob:
                    nc.vector.memset(p[:, SC:], 0.0)
                nc.vector.memset(v_blk[:], 0.0).then_inc(v_zero, 1)

            def attention(layer):
                if layer == 1:
                    dve.wait_ge(y0_first, E0)
                    nc.vector.tensor_tensor(first_batch, first_batch, yh[:, 0, :], ALU.add).then_inc(x_ffn, 1)
                norm_stats(layer, 0, layer == 0)
                norm(layer, 0, layer == 0)
                if layer == 0:
                    dve.wait_ge(tanh_done, 1)
                    dve.wait_ge(rows_in, 32)
                    for i in range(2):
                        last = nc.vector.tensor_scalar(row[:, i, :], row[:, i, :], tanh_gate[:, i:i + 1], None, ALU.mult)
                    last.then_inc(bias_done, 1)
                if layer == 1:
                    norm_stats(1, 1, False)
                    dve.wait_ge(y0_done, 2 * E0 + 2)
                    clear_attention()
                    dve.wait_ge(v_zero, 2)
                    norm(1, 1, False)
                attention_step(layer, 0, 0)
                attention_step(layer, 1, 1)
                with dve.Fori(2, B - 1) as b:
                    attention_step(layer, b, None)
                attention_step(layer, B - 1, B - 1)
                g = B * layer + B - 1
                if layer == 1:
                    keep_logits(B - 2)
                add_attention(layer, B - 1, g)
                norm2_stats(B - 1, g, False)
                if layer == 1:
                    shared_hidden(0, 0)
                norm2(layer, B - 1, g, False)
                if layer == 0:
                    dve.wait_ge(k_psum, 2)
                    dve.wait_ge(kb_ready, B)
                    w = B * KV // 2
                    for dt in range(KT):
                        last = nc.vector.tensor_scalar(k_t[:, dt, :].rearrange("p (h n) -> p h n", h=2),
                                                       score[dt][:].rearrange("p (h n) -> p h n", h=2)[:, :, 0:w],
                                                       bias_cols[:, 1, 1, dt:dt + 1], None, ALU.add)
                    last.then_inc(kt_ready, 1)
                    dve.wait_ge(hi_ready, B)
                    nc.vector.tensor_tensor(act_lo[:, :, (B - 1) * S:], bank[0][:].rearrange("p (k s) -> p k s", k=KT),
                                            act_hi[:, :, (B - 1) * S:].bitcast(F32), ALU.subtract).then_inc(lo_ready, 1)
                else:
                    norm3_stats(B - 1)
                    norm3(B - 1, g)
                    for f in range(1, 4):
                        shared_hidden(0, f)
                    keep_logits(B - 1)

            def product(n, buf, up, rows_n, width):
                dve.wait_ge(silu_done, n + 1)
                dve.wait_ge(hid_ready, hid_count(n - 2))
                nc.vector.tensor_tensor(prod[0:rows_n, buf, 0:width], silu[0:rows_n, buf, 0:width], up, ALU.mult).then_inc(gu_free, 1)

            def hidden_high(n, buf, rows_n, hi):
                dve.wait_ge(gu_free, n + 4)
                nc.vector.tensor_copy(hi, prod[0:rows_n, buf, 0:hi.shape[-1]]).then_inc(hid_hi_done, 1)

            def hidden_low(n, buf, rows_n, hi, lo):
                dve.wait_ge(hid_hi_done, n + 1)
                nc.vector.tensor_tensor(lo, prod[0:rows_n, buf, 0:hi.shape[-1]], hi.bitcast(F32), ALU.subtract).then_inc(hid_ready, 1)

            def hidden(n, buf, up, rows_n, at, f, width):
                product(n, buf, up, rows_n, width)
                hidden_high(n, buf, rows_n, hid_hi[0:rows_n, f, at:at + width])
                hidden_low(n, buf, rows_n, hid_hi[0:rows_n, f, at:at + width], hid_lo[0:rows_n, f, at:at + width])

            def first_layer(e, i, part):
                def tile(m):
                    rows_n = 64 if m == 0 else P
                    return M0 * e + m, m % 2, rows_n, first_hid_hi[0:rows_n, m, :]

                for m in range(M0):
                    n, buf, rows_n, hi = tile(m)
                    src = banks[2 + m % 3]
                    product(n, buf, src[64:P, 0:S] if m == 0 else src[:, S:2 * S], rows_n, S)
                    if m > 0:
                        hidden_low(*tile(m - 1), first_hid_lo[0:64 if m == 1 else P, m - 1, :])
                    hidden_high(n, buf, rows_n, hi)
                    if 2 <= m <= 3:
                        j = m - 1
                        dve.wait_ge(hi2, 3 * e + j + 1)
                        nc.vector.tensor_tensor(w_lo[:, M0 + j, :], raw[:, M0 + j, :], w_hi[:, M0 + j, :].bitcast(F32),
                                                ALU.subtract).then_inc(lo2_first, 1)
                hidden_low(*tile(M0 - 1), first_hid_lo[:, M0 - 1, :])
                dve.wait_ge(y0_psum, e + 1)
                for j in range(B // HALVES):
                    last = nc.vector.tensor_scalar(
                        yh[i * C0:(i + 1) * C0, B // HALVES + j, bass.ds(part * D, D)], bank_p[1][j * C0:(j + 1) * C0, 0:D],
                        tanh_gate[j * C0:(j + 1) * C0, 2:3], None, ALU.mult)
                last.then_inc(y0_done, 1)

            def shared_hidden(c, f):
                n = (GU_SHARED + FT * c if c < EARLY else GU_LATE + FT * (c - EARLY)) + f
                up = banks[2 + 2 * (f % 2) + 1]
                if c > 0:
                    hidden(n, f % 2, up, P, 0, f, PIECE)
                else:
                    product(n, f % 2, up, P, PIECE)
                    hidden_high(n, f % 2, P, hid_hi[:, f, 0:PIECE])

            def shared_add(c, j):
                dve.wait_ge(ys_psum, 4 * c + j + 1)
                two = xs[:, 4 * c + j, :]
                nc.vector.scalar_tensor_tensor(out=two, in0=bank_p[j % 2][:, 0:D], scalar=tanh_gate[:, 3:4], in1=two,
                                               op0=ALU.mult, op1=ALU.add).then_inc(ys_done, 1)

            def shared(c):
                for f in range(FT):
                    shared_hidden(c, f)
                for j in range(4):
                    shared_add(c, j)

            def slots_lo(e, hf):
                for kt in range(KT):
                    dve.wait_ge(xe_hi_done, 4 * e + KT * hf + kt + 1)
                    nc.vector.tensor_tensor(xe_lo[:, kt, hf * HC:(hf + 1) * HC], bank[kt][:, 0:HC],
                                            xe_hi[:, kt, hf * HC:(hf + 1) * HC].bitcast(F32), ALU.subtract).then_inc(xe_ready, 1)

            def expert(e, last_one):
                for hf in range(2):
                    for f in range(FT):
                        hidden(GU_ROUTED + 2 * FT * e + FT * hf + f, f % 2, banks[2 + 2 * (f % 2) + 1][:, 0:HC], P, hf * HC, f, HC)
                        if hf == 1 and f == FT // 2 and not last_one:
                            slots_lo(e + 1, 0)
                if not last_one:
                    slots_lo(e + 1, 1)
                for j in range(TT):
                    dve.wait_ge(yr_psum, TT * e + j + 1)
                    if j == 0 and not (isinstance(e, int) and e == 0):
                        dve.wait_ge(y_stored, 16 * e)
                    nc.vector.tensor_copy(y_out[:, j, :], bank_p[j % 2][0:TR, 0:D]).then_inc(yr_copied, 1)

            def routing_choices():
                steps = [0]

                def step(ins):
                    steps[0] += 1
                    ins.then_inc(choice, 1)
                    dve.wait_ge(choice, steps[0])

                dve.wait_ge(logit_done, B)
                lv = logits[:, :, 0:E1]
                wide = [P, T, E1]
                w_bc = order_w[:].unsqueeze(1).to_broadcast(wide)
                for c in range(2):
                    src = lv if c == 0 else cand[:]
                    step(nc.vector.tensor_reduce(top[:, c, :], src, AX_X, ALU.max))
                    step(nc.vector.tensor_tensor(eq[:], src, top[:, c, :].unsqueeze(2).to_broadcast(wide), ALU.is_equal))
                    step(nc.vector.tensor_tensor(eq[:], eq[:], w_bc, ALU.mult))
                    step(nc.vector.tensor_reduce(best[:], eq[:], AX_X, ALU.max))
                    step(nc.vector.tensor_tensor(pick[:, c], w_bc, best[:].unsqueeze(2).to_broadcast(wide), ALU.is_equal))
                    if c == 0:
                        step(nc.vector.scalar_tensor_tensor(out=cand[:], in0=pick[:, 0], scalar=-3.0e38, in1=lv, op0=ALU.mult, op1=ALU.add))
                nc.vector.tensor_tensor(e_dif[:], top[:, 1, :], top[:, 0, :], ALU.subtract).then_inc(e_done, 1)
                return steps

            def routing_counts(steps):
                def step(ins):
                    steps[0] += 1
                    ins.then_inc(choice, 1)
                    dve.wait_ge(choice, steps[0])

                flat = pick[:].rearrange("p c t e -> p (c t) e")
                step(nc.vector.memset(cum[0][:, 0, :], 0.0))
                step(nc.vector.tensor_copy(cum[0][:, 1:, :], flat[:, 0:2 * T - 1, :]))
                d, at = 1, 0
                while d < 2 * T:
                    if d == 4:
                        shared_hidden(0, 5)
                    a, o = cum[at], cum[1 - at]
                    step(nc.vector.tensor_copy(o[:, 0:d, :], a[:, 0:d, :]))
                    ins = nc.vector.tensor_tensor(o[:, d:, :], a[:, d:, :], a[:, 0:2 * T - d, :], ALU.add)
                    d, at = 2 * d, 1 - at
                    if d >= 2 * T:
                        ins.then_inc(route, 1)
                    else:
                        step(ins)
                assert at == 1

            def routing_slots(steps):
                def step(ins):
                    steps[0] += 1
                    ins.then_inc(added, 1)
                    dve.wait_ge(added, steps[0])

                flat = pick[:].rearrange("p c t e -> p (c t) e")
                step(nc.vector.tensor_tensor(cum[0][:], flat, base_e[:].unsqueeze(1).to_broadcast([P, 2 * T, E1]), ALU.mult))
                step(nc.vector.tensor_reduce(first[:], cum[0][:], AX_X, ALU.add))
                dve.wait_ge(pos_psum, 1)
                step(nc.vector.tensor_tensor(cum[0][:], bank[0][:, 0:2 * T * E1].rearrange("p (g e) -> p g e", e=E1), flat, ALU.mult))
                step(nc.vector.tensor_reduce(pos[:], cum[0][:], AX_X, ALU.add))
                step(nc.vector.tensor_scalar(keep[:], pos[:], float(CAP), None, ALU.is_lt))
                step(nc.vector.tensor_tensor(slot[:], pos[:], first[:], ALU.add))
                step(nc.vector.scalar_tensor_tensor(out=pos[:], in0=slot[:], scalar=-float(2 * SLOTS), in1=keep[:], op0=ALU.add, op1=ALU.mult))
                nc.vector.tensor_scalar(slot_put[:], pos[:], float(2 * SLOTS), None, ALU.add).then_inc(puts_ready, 1)
                step(nc.vector.tensor_tensor(slot_get[:], slot[:], keep[:], ALU.mult))
                dve.wait_ge(e_done, 2)
                step(nc.vector.tensor_scalar(den[:], e_dif[:], 1.0, None, ALU.add))
                step(nc.vector.reciprocal(gates12[:, 0, :], den[:]))
                step(nc.vector.tensor_tensor(gates12[:, 1, :], gates12[:, 0, :], e_dif[:], ALU.mult))
                nc.vector.scalar_tensor_tensor(out=weight[:], in0=gates12[:].rearrange("p c t -> p (c t)"), scalar=tanh_gate[:, 3:4],
                                               in1=keep[:], op0=ALU.mult, op1=ALU.mult).then_inc(slots_ready, 1)

            clear_attention()
            dve.wait_ge(v_zero, 1)
            attention(0)
            dve.wait_ge(k_psum, 2)
            for t in (first_hid_hi, first_hid_lo):
                last = nc.vector.memset(t[64:P, 0, :].bitcast(F32), 0.0)
            last.then_inc(tail_zero, 1)
            dve.wait_ge(tail_zero, 1)
            dve.wait_ge(zero_out, 16 * B)
            dve.sem_inc(gu_free, 3)
            dve.sem_inc(hid_ready, HID_FREE)
            dve.sem_inc(y0_done, 2)
            per = E0 // HALVES
            with dve.Fori(0, HALVES) as part:
                for i in range(per):
                    first_layer(per * part + i, i, part)
            attention(1)
            steps = routing_choices()
            shared_hidden(0, 4)
            routing_counts(steps)
            for f in range(6, FT):
                shared_hidden(0, f)
            steps = [0]
            routing_slots(steps)
            for j in range(4):
                shared_add(0, j)
            shared(1)
            slots_lo(0, 0)
            slots_lo(0, 1)
            expert(0, False)
            with dve.Fori(1, E1 - 1) as e:
                expert(e, False)
            expert(E1 - 1, True)

            def add_routed(t):
                for k in range(2):
                    if k == 1:
                        dve.wait_ge(added, steps[0] + t + 1)
                    ins = nc.vector.scalar_tensor_tensor(out=xs[:, t, :], in0=yg(k, t), scalar=weight[:, k * T + t:k * T + t + 1],
                                                         in1=xs[:, t, :], op0=ALU.mult, op1=ALU.add)
                    ins.then_inc(added if k == 0 else final, 1)

            dve.wait_ge(slots_ready, 1)
            for f in range(FT):
                shared_hidden(EARLY, f)
            shared_add(EARLY, 0)
            dve.wait_ge(ys_done, 4)
            for j in range(1, 4):
                shared_add(EARLY, j)
                if j == 1:
                    dve.wait_ge(gathered[0], 16 * 8)
                for t in ((0,), (1,), (2, 3))[j - 1]:
                    add_routed(t)
            dve.wait_ge(ys_done, 4 * (EARLY + 1))
            for f in range(FT):
                shared_hidden(EARLY + 1, f)
                t = 4 + f
                if t < 10:
                    if t % 4 == 0:
                        dve.wait_ge(gathered[t // 4], 16 * 8)
                    add_routed(t)
            for j, tiles in enumerate(((10, 11, 12), (13,), (14,), (15,))):
                for t in tiles:
                    if t % 4 == 0:
                        dve.wait_ge(gathered[t // 4], 16 * 8)
                    add_routed(t)
                dve.wait_ge(final, 13 + j)
                shared_add(EARLY + 1, j)

        @block.gpsimd
        def _(pool):
            def rstd_of(m, r, eps_sem, r_sem, g, m_sem):
                pool.wait_ge(m_sem, g + 1)
                nc.gpsimd.tensor_tensor(r[:], m[:, :, 1], eps_tile[:], ALU.add).then_inc(eps_sem, 1)
                pool.wait_ge(eps_sem, g + 1)
                nc.gpsimd.tensor_tensor(r[:], r[:], neg_half[:], ALU.pow).then_inc(r_sem, 1)

            def add_out_bias(layer, b):
                if layer == 1:
                    settle(pool)
                pool.wait_ge(xn_ready, b + B * layer + 1)
                if layer == 0:
                    settle(pool)
                two = xs[:, bass.ds(b * HALVES, HALVES), :]
                nc.gpsimd.tensor_tensor(two, two, row[:, layer, :].unsqueeze(1).to_broadcast([P, HALVES, D]), ALU.add).then_inc(xb_done, 1)

            def add_first_layer(b):
                two = xs[:, bass.ds(b * HALVES, HALVES), :].rearrange("p a d -> p (a d)")
                nc.gpsimd.tensor_tensor(two, two, yh[:, bass.ds(b, 1), :].rearrange("p a n -> p (a n)"), ALU.add).then_inc(x_ffn, 1)

            def keys_blocked(b, g):
                if not isinstance(g, int) or g >= 2:
                    pool.wait_ge(s_psum, 4 * g - 4)
                    settle(pool)
                for dt in range(KT):
                    last = nc.gpsimd.tensor_tensor(
                        kb[:, b % 2, dt, :].rearrange("p (n h) -> p n h", h=HT),
                        k_t[:, dt, bass.ds(b * KV, KV)].unsqueeze(2).to_broadcast([P, KV, HT]),
                        head_mask[:].unsqueeze(1).to_broadcast([P, KV, HT]), ALU.mult)
                last.then_inc(kb_ready, 1)

            def normalise_probs(g, u):
                pool.wait_ge(recip_done, 4 * g + u + 1)
                nc.gpsimd.tensor_tensor(by_row(prob[u]), by_row(prob[u]), recip[:, u].unsqueeze(1).to_broadcast([P, KV, HT]),
                                        ALU.mult).then_inc(norm_done, 1)

            def act_low(b, g):
                pool.wait_ge(hi_ready, g + 1)
                settle(pool)
                nc.gpsimd.tensor_tensor(act_lo[:, :, bass.ds(b * S, S)], stage[:], act_hi[:, :, bass.ds(b * S, S)].bitcast(F32),
                                        ALU.subtract).then_inc(lo_ready, 1)

            def low(slot_f, at):
                return nc.gpsimd.tensor_tensor(w_lo[:, at, :], raw[:, slot_f, :], w_hi[:, at, :].bitcast(F32), ALU.subtract)

            def attention_step(layer, b, n):
                g = b + B * layer
                settled = n is None or n >= 2
                more = n != B - 1
                if layer == 1 and n == 0:
                    rstd_of(mv, rstd, eps_done, rstd_done, g + 1, mv_done)
                elif layer == 1 and more:
                    add_first_layer(b + 1)
                if layer == 0 and more:
                    rstd_of(mv, rstd, eps_done, rstd_done, g + 1, mv_done)
                normalise_probs(g, 0)
                if more:
                    keys_blocked(b + 1, g + 1)
                if layer == 1 and more and n != 0:
                    rstd_of(mv, rstd, eps_done, rstd_done, g + 1, mv_done)
                if layer == 0 and more:
                    add_out_bias(layer, b + 1)
                normalise_probs(g, 1)
                if layer == 1 and more:
                    add_out_bias(layer, b + 1)
                if settled:
                    act_low(b - 2, g - 2)
                normalise_probs(g, 2)
                if layer == 1 and n in (0, 1):
                    low13(PIECES0 + M0 + n, M0 + n, M0 + n)
                if layer == 0 and settled:
                    p = bass.ds(b - 2, 1)
                    pool.wait_ge(hi13, b - 1)
                    settle(pool)
                    nc.gpsimd.tensor_tensor(w_lo[:, p, :].rearrange("p a n -> p (a n)"), raw[:, p, :].rearrange("p a n -> p (a n)"),
                                            w_hi[:, p, :].rearrange("p a n -> p (a n)").bitcast(F32), ALU.subtract).then_inc(lo13, 1)
                if n != 0:
                    rstd_of(mv2, rstd2, eps2_done, rstd2_done, g - 1, mv2_done)
                normalise_probs(g, 3)
                if layer == 1 and n != 0:
                    rstd_of(mv3, rstd3, eps3_done, rstd3_done, b - 1, mv3_done)

            def attention(layer):
                if layer == 1:
                    pool.wait_ge(y0_done, 2 * E0 + 2)
                    pool.wait_ge(x_ffn, 1)
                    add_first_layer(1)
                rstd_of(mv, rstd, eps_done, rstd_done, B * layer, mv_done)
                pool.wait_ge(bias_done, 1)
                add_out_bias(layer, 0)
                if layer == 0:
                    pool.wait_ge(kt_ready, 1)
                    keys_blocked(0, 0)
                attention_step(layer, 0, 0)
                attention_step(layer, 1, 1)
                with pool.Fori(2, B - 1) as b:
                    attention_step(layer, b, None)
                attention_step(layer, B - 1, B - 1)
                g = B * layer + B - 1
                act_low(B - 2, g - 1)
                if layer == 1:
                    for j in range(2):
                        low2(3 * E0 + j, j, FT + j)
                rstd_of(mv2, rstd2, eps2_done, rstd2_done, g, mv2_done)
                if layer == 1:
                    rstd_of(mv3, rstd3, eps3_done, rstd3_done, B - 1, mv3_done)
                    shared_low(0)
                    for j in range(2, 4):
                        low2(3 * E0 + j, j, FT + j)
                    shared_low(1)
                    shared_low(2)
                    act_low(B - 1, g)
                    for f in range(3, FT):
                        shared_low(f)
                else:
                    pool.wait_ge(kt_ready, 2)
                    keys_blocked(0, B)

            def shared_low(f):
                n = GU_SHARED + f
                pool.wait_ge(hid_hi_done, n + 1)
                nc.gpsimd.tensor_tensor(hid_lo[:, f, 0:PIECE], prod[:, f % 2, :], hid_hi[:, f, 0:PIECE].bitcast(F32),
                                        ALU.subtract).then_inc(hid_ready, 1)

            def low13(n, slot_f, at):
                pool.wait_ge(hi13, n + 1)
                low(slot_f, at).then_inc(lo13, 1)

            def low2(n, slot_j, at):
                pool.wait_ge(hi2, n + 1)
                low(slot_j, at).then_inc(lo2, 1)

            def first_layer(e):
                pool.wait_ge(hi2, 3 * e + 1)
                low(M0, M0).then_inc(lo2, 1)
                for m in range(M0):
                    low13(M0 * (e + 1) + m, m, m)

            def expert(e):
                for f in range(4):
                    low2(3 * E0 + 4 * (e + 1) + f, f, FT + f)
                for f in range(FT):
                    low13(PIECES0 + FT * (e + 2) + f, f, f)

            for t in (ident, before, ones):
                nc.gpsimd.memset(t[:], 1.0)
            nc.gpsimd.memset(head_mask[:], float(HD) ** -0.5)
            nc.gpsimd.memset(eps_tile[:], EPS)
            for e in range(E1):
                nc.gpsimd.memset(order_w[:, e:e + 1], float(E1 - e))
                nc.gpsimd.memset(base_e[:, e:e + 1], float(CAP * e))
            nc.gpsimd.memset(neg_half[:], -0.5).then_inc(consts, 1)
            pool.wait_ge(consts, 1)
            nc.gpsimd.affine_select(out=ident[:], in_=ident[:], pattern=[[-1, P]], compare_op=ALU.is_equal, fill=0.0,
                                    base=0, channel_multiplier=1).then_inc(masked, 1)
            nc.gpsimd.affine_select(out=before[:], in_=before[:], pattern=[[1, P]], compare_op=ALU.is_gt, fill=0.0,
                                    base=0, channel_multiplier=-1).then_inc(masked, 1)
            nc.gpsimd.affine_select(out=head_mask[:], in_=head_mask[:], pattern=[[-HD, HT]], compare_op=ALU.is_ge, fill=0.0,
                                    base=0, channel_multiplier=1).then_inc(masked, 1)
            pool.wait_ge(masked, 3)
            nc.gpsimd.affine_select(out=head_mask[:], in_=head_mask[:], pattern=[[HD, HT]], compare_op=ALU.is_ge, fill=0.0,
                                    base=HD - 1, channel_multiplier=-1).then_inc(masked, 1)
            nc.gpsimd.memset(yh[:], 0.0).then_inc(zeros, 1)
            pool.wait_ge(masked, 4)
            attention(0)
            with pool.Fori(0, E0) as e:
                first_layer(e)
            attention(1)
            pool.wait_ge(puts_ready, 1)
            pool.wait_ge(rows_kept, B)
            pool.wait_ge(zero_out, 16 * B)
            for k in range(2 * T):
                t = k % T
                nc.gpsimd.indirect_dma_start(
                    out=xe, out_offset=bass.IndirectOffsetOnAxis(ap=slot_put[:, k:k + 1], axis=0),
                    in_=yh[:, t // HALVES, t % HALVES * D:(t % HALVES + 1) * D], in_offset=None,
                    bounds_check=SLOTS - 1, oob_is_err=False).then_inc(scattered, 16)
            for f in range(FT):
                low13(PIECES0 + FT + f, f, f)
            with pool.Fori(0, E1) as e:
                expert(e)
            for j in range(4):
                low2(3 * E0 + 4 * (STREAM - 1) + j, j, FT + j)
            pool.wait_ge(slots_ready, 1)
            pool.wait_ge(y_stored, 16 * E1)
            for t in range(T):
                for k in range(2):
                    nc.gpsimd.indirect_dma_start(
                        out=yg(k, t), out_offset=None, in_=ye,
                        in_offset=bass.IndirectOffsetOnAxis(ap=slot_get[:, k * T + t:k * T + t + 1], axis=0),
                        bounds_check=SLOTS - 1, oob_is_err=False).then_inc(gathered[t // 4], 16)


def kernel(**inputs):
    import concourse.bacc as bacc
    from concourse.bass_utils import run_bass_kernel_spmd

    a = {k: np.asarray(v) for k, v in inputs.items()}
    f32 = np.float32

    def pad(t, rows):
        return np.concatenate([t, np.zeros((rows - t.shape[0],) + t.shape[1:], f32)]) if t.shape[0] < rows else t

    def attention_weights(*w):
        return np.stack([m.T for m in w], 1).reshape(KT, P, 4, D)

    def gate_up_pieces(w1, w3, n):
        g, u = (w[:, :n * P].reshape(KT, P, n, P) for w in (w1, w3))
        return [np.stack([g[:, :, f], u[:, :, f]], 2).transpose(1, 0, 2, 3).reshape(P, PIECE) for f in range(n)]

    def down_pieces(w2, n):
        w = pad(w2, n * 2 * P).reshape(n, 2, P, D)
        return [w[j].transpose(1, 0, 2).reshape(P, PIECE) for j in range(n)]

    first = []
    for w1, w3, w2 in zip(a["L0_ffn_w1"], a["L0_ffn_w3"], a["L0_ffn_w2"]):
        tail = np.concatenate([w1[:, 5 * P:], w3[:, 5 * P:]], 1).reshape(KT, P, P).transpose(1, 0, 2).reshape(P, KT * P)
        tail = np.concatenate([tail, np.zeros_like(tail)], 1)
        w2 = np.concatenate([pad(w2[5 * P:], P), w2[:5 * P]])
        first.append(np.stack([tail] + gate_up_pieces(w1, w3, 5) + down_pieces(w2, 3)))
    second = [np.stack(gate_up_pieces(w1, w3, FT) + down_pieces(w2, FT // 2))
              for w1, w3, w2 in [(a["L1_ffn_W1s"], a["L1_ffn_W3s"], a["L1_ffn_W2s"])]
              + list(zip(a["L1_ffn_W1"], a["L1_ffn_W3"], a["L1_ffn_W2"]))]
    zero = np.zeros(D, f32)
    wkv = a["L0_xattn_Wkv"]

    def on_rows(*v):
        return np.broadcast_to(np.stack(v), (P, len(v), v[0].shape[0]))

    def columns(v):
        return v.reshape(KT, P).T

    arrays = {
        "x_d": a["x"].reshape(T, P, D).transpose(1, 0, 2),
        "ctx_d": a["ctx_1024"].reshape(B * KV, D).T.reshape(KT, P, B, KV),
        "attn_w_d": np.stack([attention_weights(a["L0_xattn_Wq"], wkv[:D], wkv[D:], a["L0_xattn_Wout"]),
                              attention_weights(a["L1_xattn_W_q"], a["L1_xattn_W_k"], a["L1_xattn_W_v"], a["L1_xattn_W_o"])]),
        "rows_d": on_rows(a["L0_xattn_bout"], a["L1_xattn_b_o"], a["L1_ffn_ln_g"], a["L1_ffn_ln_b"]),
        "cols_d": np.stack([np.stack([columns(zero)] * 3, 1),
                            np.stack([columns(a["L1_xattn_b_q"]), columns(a["L1_xattn_b_k"]), columns(a["L1_xattn_b_v"])], 1)], 1),
        "gates_d": np.broadcast_to(np.concatenate([a["g_xattn"], a["g_ffn"]]), (P, 4)),
        "router_d": np.concatenate([a["L1_ffn_Wr"], np.zeros((D, 1), f32)], 1).reshape(KT, P, 8).transpose(1, 0, 2),
        "w_first_d": np.stack(first),
        "w_second_d": np.stack(second),
    }
    arrays = {k: np.ascontiguousarray(v) for k, v in arrays.items()}
    nc = bacc.Bacc("TRN2", target_bir_lowering=False, num_devices=1)
    ins = [nc.dram_tensor(k, v.shape, F32, kind="ExternalInput").ap() for k, v in arrays.items()]
    xe = nc.dram_tensor("slots_in", [SLOTS, D], F32, kind="Internal").ap()
    ye = nc.dram_tensor("slots_out", [SLOTS, D], F32, kind="Internal").ap()
    out = nc.dram_tensor("out_d", [P, T, D], F32, kind="ExternalOutput").ap()
    v_d = nc.dram_tensor("values", [2 * B, KP, D], F32, kind="Internal").ap()
    flamingo_program(nc, *ins, xe, ye, v_d, out)
    r = run_bass_kernel_spmd(nc, [arrays], core_ids=[0])
    return np.asarray(r.results[0]["out_d"]).transpose(1, 0, 2).reshape(B, S, D)
```
